# Optimizing a Trainium2 kernel written in Bass

```python
import numpy as np
import jax
import jax.numpy as jnp

def _softmax(x, axis=-1):
    return jax.nn.softmax(x, axis=axis)

def _gelu(x):
    return jax.nn.gelu(x, approximate=True)

def _silu(x):
    return jax.nn.silu(x)

def _sigmoid(x):
    return jax.nn.sigmoid(x)

def _layernorm(x, axis=-1, eps=1e-05):
    m = jnp.mean(x, axis=axis, keepdims=True)
    v = jnp.var(x, axis=axis, keepdims=True)
    return (x - m) / jnp.sqrt(v + eps)

def _scatter_add(tgt, idx, src, axis=0):
    return tgt.at[idx].add(src)

def _segment_sum(src, seg, n):
    return jax.ops.segment_sum(src, seg, n)
kernel_name = 'mk_xattn_ffn_d1_seqx_r4_475a6a'

def setup_inputs(seed: int=0):
    np.random.seed(seed)
    _w = jnp.asarray

    def _rec_inputs():
        import jax
        import jax.numpy as jnp
        _rk = jax.random.key(seed)
        x = -0.000125 + 0.9999 * jax.random.normal(jax.random.fold_in(_rk, 1), (2, 512, 512), jnp.float32)
        _lenS = 512 - jax.random.randint(jax.random.fold_in(_rk, 7), (2,), 0, max(1, 512 // 4) + 1, jnp.int32)
        _lenS2 = 1024 - jax.random.randint(jax.random.fold_in(_rk, 8), (2,), 0, max(1, 1024 // 4) + 1, jnp.int32)
        _ctx_2048P = jax.random.normal(jax.random.fold_in(_rk, 11), (2, 16, 512), jnp.float32)
        _ctx_2048c = jax.random.dirichlet(jax.random.fold_in(_rk, 511), 0.3 * jnp.ones((16,), jnp.float32), (2, 1024))
        _ctx_2048t = jnp.einsum('bsk,bkd->bsd', _ctx_2048c, _ctx_2048P)
        _ctx_2048t = _ctx_2048t * jax.lax.rsqrt(jnp.mean(jnp.square(_ctx_2048t)) + 1e-12) * 0.953939
        ctx_2048 = 1.72703e-05 + 1.00003 * (_ctx_2048t + 0.3 * jax.random.normal(jax.random.fold_in(_rk, 611), (2, 1024, 512), jnp.float32))
        return (x, ctx_2048)
    x, ctx_2048 = _rec_inputs()

    def _L0_xattn_setup():
        import jax, jax.numpy as jnp
        import numpy as np
        DIM = 512
        NH = 16
        HD = DIM // NH
        EPS = 1e-06
        IMG_LEN = 257

        def rms_norm(x, w, eps=EPS):
            xf = x.astype(jnp.float32)
            y = xf * jax.lax.rsqrt(jnp.mean(xf * xf, axis=-1, keepdims=True) + eps)
            return y.astype(x.dtype) * w

        def linear(x, w, b):
            return jnp.einsum('blc,oc->blo', x, w) + b

        def attention(q, k, v):
            scale = 1.0 / jnp.sqrt(jnp.asarray(HD, q.dtype))
            scores = jnp.einsum('bqhd,bkhd->bhqk', q, k) * scale
            probs = jax.nn.softmax(scores, axis=-1)
            return jnp.einsum('bhqk,bkhd->bqhd', probs, v)
        key = jax.random.key(seed)
        ks = jax.random.split(key, 12)
        B, L = (2, 2048)
        s = 0.02
        inp = {'x': jax.random.normal(ks[0], (B, L, DIM), jnp.float32), 'context': jax.random.normal(ks[1], (B, 769, DIM), jnp.float32), 'q_w': jax.random.normal(ks[2], (DIM, DIM), jnp.float32) * s, 'q_b': jnp.zeros((DIM,), jnp.float32), 'k_w': jax.random.normal(ks[3], (DIM, DIM), jnp.float32) * s, 'k_b': jnp.zeros((DIM,), jnp.float32), 'v_w': jax.random.normal(ks[4], (DIM, DIM), jnp.float32) * s, 'v_b': jnp.zeros((DIM,), jnp.float32), 'k_img_w': jax.random.normal(ks[5], (DIM, DIM), jnp.float32) * s, 'k_img_b': jnp.zeros((DIM,), jnp.float32), 'v_img_w': jax.random.normal(ks[6], (DIM, DIM), jnp.float32) * s, 'v_img_b': jnp.zeros((DIM,), jnp.float32), 'o_w': jax.random.normal(ks[7], (DIM, DIM), jnp.float32) * s, 'o_b': jnp.zeros((DIM,), jnp.float32), 'norm_q_w': jnp.ones((DIM,), jnp.float32), 'norm_k_w': jnp.ones((DIM,), jnp.float32), 'norm_k_img_w': jnp.ones((DIM,), jnp.float32)}
        return inp
    _L0_xattn_all = _L0_xattn_setup()
    _L0_xattn_in = {k: v for k, v in _L0_xattn_all.items() if k in ('q_w', 'q_b', 'k_w', 'k_b', 'v_w', 'v_b', 'k_img_w', 'k_img_b', 'v_img_w', 'v_img_b', 'o_w', 'o_b', 'norm_q_w', 'norm_k_w', 'norm_k_img_w')}
    del _L0_xattn_all

    def _L0_ffn_setup():
        import jax, jax.numpy as jnp
        import numpy as np
        EPS = 1e-06
        K_STEPS = 4
        USE_GATING = True

        def layer_norm(x, gamma, beta):
            mu = jnp.mean(x, axis=-1, keepdims=True)
            var = jnp.mean(jnp.square(x - mu), axis=-1, keepdims=True)
            return (x - mu) * jax.lax.rsqrt(var + EPS) * gamma + beta
        key = jax.random.key(seed)
        B, L, D, H = (4, 1024, 512, 2048)
        ks = jax.random.split(key, 16)
        s = 0.02
        return {'x': jax.random.normal(ks[0], (B, L, D), dtype=jnp.float32), 'in_gamma': jnp.ones((D,), jnp.float32), 'in_beta': jnp.zeros((D,), jnp.float32), 'agg_w': jax.random.normal(ks[1], (D, D), jnp.float32) * s, 'agg_b': jnp.zeros((D,), jnp.float32), 'pn_gamma': jnp.ones((D,), jnp.float32), 'pn_beta': jnp.zeros((D,), jnp.float32), 'd1_w': jax.random.normal(ks[2], (D, H), jnp.float32) * s, 'd1_b': jnp.zeros((H,), jnp.float32), 'd2_w': jax.random.normal(ks[3], (H, D), jnp.float32) * s, 'd2_b': jnp.zeros((D,), jnp.float32), 'bc_w': jax.random.normal(ks[4], (D, D), jnp.float32) * s, 'bc_b': jnp.zeros((D,), jnp.float32), 'gate_w': jax.random.normal(ks[5], (D, D), jnp.float32) * s, 'gate_b': jnp.zeros((D,), jnp.float32), 'out_gamma': jnp.ones((D,), jnp.float32), 'out_beta': jnp.zeros((D,), jnp.float32)}
    _L0_ffn_all = _L0_ffn_setup()
    _L0_ffn_in = {k: v for k, v in _L0_ffn_all.items() if k in ('in_gamma', 'in_beta', 'agg_w', 'agg_b', 'pn_gamma', 'pn_beta', 'd1_w', 'd1_b', 'd2_w', 'd2_b', 'bc_w', 'bc_b', 'gate_w', 'gate_b', 'out_gamma', 'out_beta')}
    del _L0_ffn_all
    return {'x': x, 'ctx_2048': ctx_2048, 'L0_xattn_q_w': _L0_xattn_in['q_w'], 'L0_xattn_q_b': _L0_xattn_in['q_b'], 'L0_xattn_k_w': _L0_xattn_in['k_w'], 'L0_xattn_k_b': _L0_xattn_in['k_b'], 'L0_xattn_v_w': _L0_xattn_in['v_w'], 'L0_xattn_v_b': _L0_xattn_in['v_b'], 'L0_xattn_k_img_w': _L0_xattn_in['k_img_w'], 'L0_xattn_k_img_b': _L0_xattn_in['k_img_b'], 'L0_xattn_v_img_w': _L0_xattn_in['v_img_w'], 'L0_xattn_v_img_b': _L0_xattn_in['v_img_b'], 'L0_xattn_o_w': _L0_xattn_in['o_w'], 'L0_xattn_o_b': _L0_xattn_in['o_b'], 'L0_xattn_norm_q_w': _L0_xattn_in['norm_q_w'], 'L0_xattn_norm_k_w': _L0_xattn_in['norm_k_w'], 'L0_xattn_norm_k_img_w': _L0_xattn_in['norm_k_img_w'], 'L0_ffn_in_gamma': _L0_ffn_in['in_gamma'], 'L0_ffn_in_beta': _L0_ffn_in['in_beta'], 'L0_ffn_agg_w': _L0_ffn_in['agg_w'], 'L0_ffn_agg_b': _L0_ffn_in['agg_b'], 'L0_ffn_pn_gamma': _L0_ffn_in['pn_gamma'], 'L0_ffn_pn_beta': _L0_ffn_in['pn_beta'], 'L0_ffn_d1_w': _L0_ffn_in['d1_w'], 'L0_ffn_d1_b': _L0_ffn_in['d1_b'], 'L0_ffn_d2_w': _L0_ffn_in['d2_w'], 'L0_ffn_d2_b': _L0_ffn_in['d2_b'], 'L0_ffn_bc_w': _L0_ffn_in['bc_w'], 'L0_ffn_bc_b': _L0_ffn_in['bc_b'], 'L0_ffn_gate_w': _L0_ffn_in['gate_w'], 'L0_ffn_gate_b': _L0_ffn_in['gate_b'], 'L0_ffn_out_gamma': _L0_ffn_in['out_gamma'], 'L0_ffn_out_beta': _L0_ffn_in['out_beta']}

def reference(x, ctx_2048, L0_xattn_q_w, L0_xattn_q_b, L0_xattn_k_w, L0_xattn_k_b, L0_xattn_v_w, L0_xattn_v_b, L0_xattn_k_img_w, L0_xattn_k_img_b, L0_xattn_v_img_w, L0_xattn_v_img_b, L0_xattn_o_w, L0_xattn_o_b, L0_xattn_norm_q_w, L0_xattn_norm_k_w, L0_xattn_norm_k_img_w, L0_ffn_in_gamma, L0_ffn_in_beta, L0_ffn_agg_w, L0_ffn_agg_b, L0_ffn_pn_gamma, L0_ffn_pn_beta, L0_ffn_d1_w, L0_ffn_d1_b, L0_ffn_d2_w, L0_ffn_d2_b, L0_ffn_bc_w, L0_ffn_bc_b, L0_ffn_gate_w, L0_ffn_gate_b, L0_ffn_out_gamma, L0_ffn_out_beta):
    import jax
    import jax.numpy as jnp

    def _L0_xattn_ref(x, context, q_w, q_b, k_w, k_b, v_w, v_b, k_img_w, k_img_b, v_img_w, v_img_b, o_w, o_b, norm_q_w, norm_k_w, norm_k_img_w):
        import jax, jax.numpy as jnp
        import numpy as np
        DIM = 512
        NH = 16
        HD = DIM // NH
        EPS = 1e-06
        IMG_LEN = 257

        def rms_norm(x, w, eps=EPS):
            xf = x.astype(jnp.float32)
            y = xf * jax.lax.rsqrt(jnp.mean(xf * xf, axis=-1, keepdims=True) + eps)
            return y.astype(x.dtype) * w

        def linear(x, w, b):
            return jnp.einsum('blc,oc->blo', x, w) + b

        def attention(q, k, v):
            scale = 1.0 / jnp.sqrt(jnp.asarray(HD, q.dtype))
            scores = jnp.einsum('bqhd,bkhd->bhqk', q, k) * scale
            probs = jax.nn.softmax(scores, axis=-1)
            return jnp.einsum('bhqk,bkhd->bqhd', probs, v)
        B, L, _ = x.shape
        ctx_img = context[:, :IMG_LEN]
        ctx_txt = context[:, IMG_LEN:]
        q = rms_norm(linear(x, q_w, q_b), norm_q_w).reshape(B, L, NH, HD)
        k = rms_norm(linear(ctx_txt, k_w, k_b), norm_k_w).reshape(B, -1, NH, HD)
        v = linear(ctx_txt, v_w, v_b).reshape(B, -1, NH, HD)
        k_img = rms_norm(linear(ctx_img, k_img_w, k_img_b), norm_k_img_w).reshape(B, -1, NH, HD)
        v_img = linear(ctx_img, v_img_w, v_img_b).reshape(B, -1, NH, HD)
        img_x = attention(q, k_img, v_img)
        txt_x = attention(q, k, v)
        out = (txt_x + img_x).reshape(B, L, DIM)
        return linear(out, o_w, o_b)

    def _L0_ffn_ref(x, in_gamma, in_beta, agg_w, agg_b, pn_gamma, pn_beta, d1_w, d1_b, d2_w, d2_b, bc_w, bc_b, gate_w, gate_b, out_gamma, out_beta):
        import jax, jax.numpy as jnp
        import numpy as np
        EPS = 1e-06
        K_STEPS = 4
        USE_GATING = True

        def layer_norm(x, gamma, beta):
            mu = jnp.mean(x, axis=-1, keepdims=True)
            var = jnp.mean(jnp.square(x - mu), axis=-1, keepdims=True)
            return (x - mu) * jax.lax.rsqrt(var + EPS) * gamma + beta
        x_norm = layer_norm(x, in_gamma, in_beta)
        thought = x_norm[:, -1, :] @ agg_w + agg_b
        for _ in range(K_STEPS):
            t = layer_norm(thought, pn_gamma, pn_beta)
            t = jax.nn.gelu(t @ d1_w + d1_b, approximate=False)
            thought = thought + (t @ d2_w + d2_b)
        broadcast = (thought @ bc_w + bc_b)[:, None, :]
        if USE_GATING:
            gate = jax.nn.sigmoid(x @ gate_w + gate_b)
            out = x + gate * broadcast
        else:
            out = x + broadcast
        return layer_norm(out, out_gamma, out_beta)
    x = x + _L0_xattn_ref(_layernorm(x, axis=-1), ctx_2048, L0_xattn_q_w, L0_xattn_q_b, L0_xattn_k_w, L0_xattn_k_b, L0_xattn_v_w, L0_xattn_v_b, L0_xattn_k_img_w, L0_xattn_k_img_b, L0_xattn_v_img_w, L0_xattn_v_img_b, L0_xattn_o_w, L0_xattn_o_b, L0_xattn_norm_q_w, L0_xattn_norm_k_w, L0_xattn_norm_k_img_w)
    x = x + _L0_ffn_ref(_layernorm(x, axis=-1), L0_ffn_in_gamma, L0_ffn_in_beta, L0_ffn_agg_w, L0_ffn_agg_b, L0_ffn_pn_gamma, L0_ffn_pn_beta, L0_ffn_d1_w, L0_ffn_d1_b, L0_ffn_d2_w, L0_ffn_d2_b, L0_ffn_bc_w, L0_ffn_bc_b, L0_ffn_gate_w, L0_ffn_gate_b, L0_ffn_out_gamma, L0_ffn_out_beta)
    return x

_drawn_inputs = setup_inputs


def setup_inputs(seed=0):
    import zlib

    import numpy as np

    out = dict(_drawn_inputs(seed))
    spreads = {'L0_xattn_q_b': (0.0, 0.637),
     'L0_xattn_k_b': (0.0, 0.8),
     'L0_xattn_v_b': (0.0, 0.1),
     'L0_xattn_k_img_b': (0.0, 0.8),
     'L0_xattn_v_img_b': (0.0, 0.1),
     'L0_xattn_o_b': (0.0, 0.1),
     'L0_xattn_norm_q_w': (1.0, 0.6),
     'L0_xattn_norm_k_w': (1.0, 0.6),
     'L0_xattn_norm_k_img_w': (1.0, 0.6),
     'L0_ffn_in_gamma': (1.0, 0.6),
     'L0_ffn_in_beta': (0.0, 0.736),
     'L0_ffn_agg_b': (0.0, 0.355),
     'L0_ffn_pn_gamma': (1.0, 0.6),
     'L0_ffn_pn_beta': (0.0, 0.653),
     'L0_ffn_d1_b': (0.0, 0.324),
     'L0_ffn_d2_b': (0.0, 0.1),
     'L0_ffn_bc_b': (0.0, 0.336),
     'L0_ffn_gate_b': (0.0, 0.8),
     'L0_ffn_out_gamma': (1.0, 0.2),
     'L0_ffn_out_beta': (0.0, 0.1)}
    factors = {}
    for name, (base, spread) in spreads.items():
        noise = np.random.default_rng([zlib.crc32(name.encode()), seed]).standard_normal(out[name].shape)
        drawn = base * np.exp(spread * noise) if base else spread * noise
        out[name] = jnp.asarray(drawn.astype(out[name].dtype))
    for name, factor in factors.items():
        out[name] = (out[name] * factor).astype(out[name].dtype)
    return out
```

```python
from contextlib import ExitStack

import numpy as np

import concourse.bass as bass
from concourse import mybir

F32 = mybir.dt.float32
F32R = mybir.dt.float32r
ALU = mybir.AluOpType
ACT = mybir.ActivationFunctionType
AX = mybir.AxisListType

P = 128
D = 512
KC = D // P
NB = 2
TOK = 512
KEYS = 1024
IMG = 257
IMG_CHUNK = IMG // P
NH = 16
HD = D // NH
HPG = P // HD
NG = NH // HPG
QH = TOK // 2
NU = 2 * NB * NG
CH = KEYS // P
PAIRS = 6
NP = 2
XS = 6
LEAD = 4
HID = 2048
K_STEPS = 4
EPS_LN = 1e-5
EPS = 1e-6
SCALE = 1.0 / float(np.sqrt(np.float32(HD)))

COLS = ['L0_xattn_q_b', 'L0_xattn_k_b', 'L0_xattn_k_img_b', 'L0_xattn_norm_q_w', 'L0_xattn_norm_k_w',
        'L0_xattn_norm_k_img_w', 'L0_xattn_v_b', 'L0_xattn_v_img_b', 'L0_ffn_in_gamma', 'L0_ffn_in_beta',
        'L0_ffn_pn_gamma', 'L0_ffn_pn_beta']
QB, KB, KIB, NQ, NK, NKI, VB, VIB, ING, INB, PNG, PNB = range(len(COLS))
ROWS = ['L0_xattn_o_b', 'L0_ffn_gate_b', 'L0_ffn_out_gamma', 'L0_ffn_out_beta']
R_O, R_GATE, R_OG, R_OB = range(4)


def make_plan():
    plan = []
    add = lambda *e: plan.append(e)

    def proj(tile):
        kind = TILES[tile]
        for oc in range(KC):
            for piece in range(2 if kind[0] == 'k' and kind[2] == 0 else 1):
                add('proj', tile, oc, piece)

    def v(b, chunks):
        for c in chunks:
            add('v', b, c)
            if c == IMG_CHUNK:
                add('vimg', b)
            add('vstore', b, c)

    add('split', 0)
    add('xstat', 1)
    add('xnorm', 1)
    for n in range(4):
        add('xT', 1, n)
    add('split', 1)
    add('xstat', 0)
    add('xnorm', 0)
    proj(0)
    for n in range(4):
        add('xT', 0, n)
    add('split', 2)
    add('sumsq', 0)
    add('split', 3)
    proj(1)
    add('norm', 0)
    add('split', 4)
    proj(2)
    add('sumsq', 1)
    add('norm', 1)
    add('split', 5)
    add('split', 6)
    proj(3)
    add('sumsq', 2)
    add('norm', 2)
    v(0, range(0, 1))
    add('sumsq', 3)
    v(0, range(1, 4))
    add('norm', 3)
    add('split', 7)
    v(0, range(4, 8))
    add('split', 8)
    proj(4)
    add('load', 0)
    proj(5)
    add('sumsq', 4)
    add('norm', 4)
    v(1, range(0, 1))
    add('sumsq', 5)
    v(1, range(1, 4))
    add('norm', 5)
    v(1, range(4, 8))
    add('phase2')
    add('load_v', 0)
    add('load', 1)
    add('load_v', 1)
    add('load', 2)
    ahead = 8 + LEAD
    extra = {}

    def at(step, *e):
        extra.setdefault(step, []).append(e)

    for k in range(4):
        base = 8 * 4 * (k + 1)
        at(base + 1, 'o', k, 0)
        at(base + 2, 'o', k, 1)
    s = 8 * 8 + 4
    at(s, 'ch_row')
    at(s + 2, 'ch_stat', 0)
    at(s + 3, 'ch_ln', 0)
    at(s + 3, 'ch_stat', 1)
    at(s + 4, 'ch_ln', 1)
    at(s + 4, 'ch_turn', 0)
    at(s + 5, 'ch_agg')
    at(s + 5, 'ch_stat', 2)
    s += 6
    for k in range(K_STEPS):
        at(s, 'ch_ln', 2 + k)
        at(s, 'ch_turn', 1 + k)
        at(s + 1, 'ch_d1', k)
        at(s + 3, 'ch_hT', k)
        at(s + 4, 'ch_d2', k)
        at(s + 5, 'ch_sum', k)
        if k < K_STEPS - 1:
            at(s + 5, 'ch_stat', 3 + k)
        s += 6
    at(s, 'ch_turn', 1 + K_STEPS)
    at(s + 1, 'ch_bc')
    at(s + 2, 'ch_spread', 0)
    at(s + 2, 'ch_spread', 1)
    s += 3
    for f in range(6):
        at(s, 'f_stat', f)
        at(s + 1, 'f_turn', f)
        at(s + 2, 'f_gate', f)
        at(s + 4, 'f_stat2', f)
        at(s + 5, 'f_out', f)
        if f == 1:
            at(s + 6, 'res2')
        s += 3
    for t in range(ahead):
        add('S1', t)
    last = max(max(extra), 8 * NU)
    for r in range(last + 1):
        if r < 8 * NU:
            add('S2', r)
            if r % 8 == 0 and r > 0 and r // 8 + 2 < NU:
                add('load', r // 8 + 2)
            if r % 8 == 1 and r // 8 + 1 < NU and r > 8:
                add('load_v', r // 8 + 1)
        if r + ahead < 8 * NU:
            add('S1', r + ahead)
        if 1 <= r <= 8 * NU:
            add('PV', r - 1)
            if r % 8 == 0:
                add('attn', r // 8 - 1)
        t = r + ahead
        if t % 8 == 0 and t <= 8 * NU:
            add('logs', t // 8 - 1)
        if t % 8 == 1 and t // 8 <= NU:
            add('shift', t // 8 - 1)
        if r < 12:
            add('late', r)
        for e in extra.get(r, []):
            if e != ('o', 3, 0) and e != ('o', 3, 1):
                plan.append(e)
    for n in range(2):
        add('o', 3, n)
        add('f_stat', 6 + n)
    for n in range(2):
        add('f_turn', 6 + n)
        add('f_gate', 6 + n)
    for n in range(2):
        add('f_stat2', 6 + n)
        add('f_out', 6 + n)
    first = [i for i, e in enumerate(plan) if e == ('S1', 8)][0]
    plan.insert(first + 1, ('logs', 0))
    first = [i for i, e in enumerate(plan) if e == ('S1', 9)][0]
    plan.insert(first + 1, ('shift', 0))
    return plan


TILES = [('q', 1), ('q', 0), ('k', 0, 0), ('k', 0, 1), ('k', 1, 0), ('k', 1, 1)]
SPLITS = ['wq', 'wki', 'wk', 'c00', 'c01', 'wvi', 'wv', 'c10', 'c11']
JOBS = {'xT': 'dve', 'proj': 'act', 'sumsq': 'act', 'v': 'act', 'vimg': 'act', 'shift': 'dve', 'o': 'dve',
        'ch_turn': 'dve', 'ch_agg': 'dve', 'ch_d1': 'dve', 'ch_hT': 'dve', 'ch_d2': 'dve', 'ch_sum': 'dve',
        'ch_bc': 'dve', 'ch_spread': 'dve', 'f_turn': 'act', 'f_gate': 'dve'}
SHARED_BANK = 7


def build(nc, T, out):
    plan = make_plan()
    jobs = [e for e in plan if e[0] in JOBS]
    job_at = {e: n for n, e in enumerate(jobs)}
    n_first = next(n for n, e in enumerate(jobs) if e[0] == 'shift')
    bank_of = [n % 8 if n < n_first else SHARED_BANK for n in range(len(jobs))]

    def emptied(n):
        eng = JOBS[jobs[n][0]]
        return eng, sum(JOBS[e[0]] == eng for e in jobs[:n + 1])

    def before_in_bank(bank, n):
        return max((m for m in range(n) if bank_of[m] == bank), default=None)

    def pieces(tile):
        kind = TILES[tile]
        if kind[0] == 'q':
            return [('wq', 0, 512, 0, 512, QB, None)]
        if kind[2] == 1:
            return [('wk', 0, 512, 0, 512, KB, NK)]
        return [('wki', 0, IMG + 1, 0, IMG, KIB, NKI), ('wk', IMG - 1, 512, IMG, 512, KB, NK)]

    def unit(u):
        k = u // NG
        return 1 - k // NB, k % NB, u % NG

    def pair_slot(u, j):
        n = 2 * u + j // 2
        return n % PAIRS, j % 2, n // PAIRS

    ctx = ExitStack()
    with ctx:
        base = (nc.sbuf_base + 63) // 64 * 64
        KB_ = 1024

        def sb(name, shape, dt, off):
            return nc.alloc_sbuf_tensor_at(name, shape, dt, offset=base + int(off))

        kst = sb("kst", [P, PAIRS, 2, KEYS], F32R, 0)
        qst = sb("qst", [P, PAIRS, 2, QH], F32R, 48 * KB_)
        o = 60 * KB_
        colp = sb("colp", [P, len(COLS), KC], F32, o); o += 256
        rows = sb("rows", [P, 4, D], F32, o); o += 8 * KB_
        chrow = sb("chrow", [P, D], F32, o); o += 2 * KB_
        d1b = sb("d1b", [P, D], F32, o)
        bcb0 = sb("bcb0", [P, D], F32, o); o += 2 * KB_
        ident = sb("ident", [P, P], F32, o); o += 512
        inv_d = sb("inv_d", [P, 1], F32, o); o += 32
        epsln = sb("epsln", [P, 1], F32, o); o += 32
        epsf = sb("epsf", [P, 1], F32, o); o += 32
        sel = sb("sel", [P, 32], F32, o); o += 128
        qw = sb("qw", [P, KC], F32, o); o += 64
        vbias = sb("vbias", [P, KC], F32, o); o += 64
        negm = sb("negm", [P, 2, 16], F32, o); o += 128
        esum = sb("esum", [P, 2, 16], F32, o); o += 128
        lnl = sb("lnl", [P, 2, 16], F32, o); o += 128
        negc = sb("negc", [P, 2, 16], F32, o); o += 128
        bst = sb("bst", [P, 8, 6], F32, o); o += 192
        mv = sb("mv", [P, 8, 2], F32, o); o += 64
        rs = sb("rs", [P, 8], F32, o); o += 64
        cst = sb("cst", [P, 6], F32, o); o += 32
        cmv = sb("cmv", [P, 2], F32, o); o += 32
        crs = sb("crs", [P, 1], F32, o); o += 32
        fst = sb("fst", [P, 2, 2, 6], F32, o); o += 96
        fmv = sb("fmv", [P, 2, 2, 2], F32, o); o += 32
        frs = sb("frs", [P, 2, 2], F32, o); o += 32
        crow = sb("crow", [8, 2, QH], F32R, o); o += 2 * KB_
        assert o % 32 == 0
        arena = o
        o += 96 * KB_
        rest = o
        xin = sb("xin", [P, 8, D], F32, 0)
        raw = sb("raw", [P, 2, KC, D], F32, 16 * KB_)
        token_parts = [sb(f"tok{i}", [P, 2, KC, 512], F32R, arena + 16 * KB_ * i) for i in range(2)]
        w_at = {'wki': 2, 'wk': 3, 'wvi': 4, 'wv': 5, 'wq': 4}
        w_parts = {n: sb("p_" + n, [P, 2, KC, D], F32R, arena + 16 * KB_ * i) for n, i in w_at.items()}
        raw4 = sb("raw4", [P, 2, KC, 512], F32, 32 * KB_)
        sq4 = sb("sq4", [P, KC, 512], F32, rest)
        ind_in = sb("ind_in", [4, KEYS], F32, rest)
        ssum = sb("ssum", [P, 512], F32, rest + 8 * KB_)
        rt = sb("rt", [P, 2, 512], F32, rest + 10 * KB_)
        hl = sb("hl", [P, 2, 2, 512], F32R, rest + 14 * KB_)
        vbuf = sb("vbuf", [P, 2, D], F32, rest + 22 * KB_)
        ind = sb("ind", [4, KEYS], F32R, rest + 26 * KB_)
        d1 = sb("d1", [P, KC, HID], F32, arena)
        vring = sb("vring", [P, 2, CH, P], F32, arena + 32 * KB_)
        wo = sb("wo", [P, KC, D], F32, arena + 40 * KB_)
        wg = sb("wg", [P, KC, D], F32, arena + 48 * KB_)
        aggbc = sb("aggbc", [P, KC, D], F32, arena + 56 * KB_)
        d2 = sb("d2", [P, HID // P, D], F32, arena + 64 * KB_)
        prob = sb("prob", [P, NP, HPG * QH], F32, rest)
        o = rest + 8 * KB_
        chx = sb("chx", [32, D], F32, o)
        th = sb("th", [32, D], F32, o + 2 * KB_)
        hb = sb("hb", [P, D], F32, o + 4 * KB_)
        hT = sb("hT", [P, KC, P], F32, o + 6 * KB_)
        tT = sb("tT", [P, KC, 32], F32, o + 8 * KB_)
        x2n = sb("x2n", [P, D], F32, o)
        xTt = sb("xTt", [P, KC, P], F32, o + 2 * KB_)
        zt = sb("zt", [P, 2, D], F32, o + 4 * KB_)
        attT = sb("attT", [P, NG, QH], F32, rest + 17 * KB_)
        bcb1 = sb("bcb1", [P, D], F32, rest + 21 * KB_)
        x2s = sb("x2s", [P, XS, D], F32, rest + 23 * KB_)

        psum = ctx.enter_context(nc.psum_tensor("psum", [P, 8, 512], F32))
        score1 = psum[:, 0:4, :].rearrange("p (a b) n -> p a (b n)", a=2)
        score2 = psum[:, 4:6, :].rearrange("p b n -> p (b n)")
        PV_BANK = 6

        kscr = nc.dram_tensor("kscr", (2, NB, D, KEYS), F32).ap()
        qscr = nc.dram_tensor("qscr", (2, 2, D, NB * QH), F32).ap()
        vscr = nc.dram_tensor("vscr", (NB, CH, P, D), F32).ap()

        def sem(name):
            return ctx.enter_context(nc.semaphore(name))

        const_loaded = sem("const_loaded")
        ind_placed = sem("ind_placed")
        ind_ready = sem("ind_ready")
        x_loaded = [sem(f"x_loaded{i}") for i in range(2)]
        raw_loaded = [sem(f"raw_loaded{i}") for i in range(2)]
        hi_done = sem("hi_done")
        lo_done = sem("lo_done")
        x_mean = sem("x_mean")
        x_rstd = sem("x_rstd")
        xn_done = sem("xn_done")
        job_done = sem("job_done")
        emptied_by = {'act': sem("emptied_by_act"), 'dve': sem("emptied_by_dve")}
        sumsq_added = sem("sumsq_added")
        rms_done = sem("rms_done")
        norm_done = sem("norm_done")
        hl_stored = [sem(f"hl_stored{i}") for i in range(2)]
        v_stored = [sem(f"v_stored{i}") for i in range(2)]
        pair_loaded = [sem(f"pair_loaded{i}") for i in range(PAIRS)]
        v_loaded = [sem(f"v_loaded{i}") for i in range(2)]
        s1_done = sem("s1_done")
        max_done = sem("max_done")
        exp1_done = sem("exp1_done")
        ln_done = sem("ln_done")
        negc_done = sem("negc_done")
        shift_loaded = [sem(f"shift_loaded{i}") for i in range(2)]
        s2_done = sem("s2_done")
        exp2_done = sem("exp2_done")
        pv_done = sem("pv_done")
        attn_done = sem("attn_done")
        act_order = sem("act_order")
        dve_order = sem("dve_order")
        pool_order = sem("pool_order")
        qw_ready = sem("qw_ready")
        ones_ready = sem("ones_ready")
        res_loaded = sem("res_loaded")
        res_ready = sem("res_ready")
        late_loaded = {n: sem("loaded_" + n) for n in ('wo', 'wg', 'agg', 'd1', 'd2', 'bc')}
        chx_zero = sem("chx_zero")
        row_loaded = sem("row_loaded")
        ch_stats = sem("ch_stats")
        ch_rstd = sem("ch_rstd")
        ch_norm = sem("ch_norm")
        gelu_in = sem("gelu_in")
        gelu_done = sem("gelu_done")
        tb_ready = sem("tb_ready")
        f_stats = sem("f_stats")
        f_rstd = sem("f_rstd")
        x2n_done = sem("x2n_done")
        z_ready = sem("z_ready")
        z_exp = sem("z_exp")
        z_clamped = sem("z_clamped")
        gate_done = sem("gate_done")
        mix_done = sem("mix_done")
        x2b_ready = sem("x2b_ready")
        out_ready = sem("out_ready")
        slot_stored = sem("slot_stored")
        out_stored = sem("out_stored")

        pieces_before = [sum(len(pieces(t)) for t in range(n)) * KC for n in range(7)]

        f_stat_count = {e: n + 1 for n, e in enumerate(e for e in plan if e[0] in ('f_stat', 'f_stat2'))}

        def stores_of(tiles):
            return 16 * (4 * tiles // 2)

        n_const = 4 + 3 + 4 + 2
        i_split = {n: i for i, n in enumerate(SPLITS)}
        tok_of = {('k', 0, 0): 'c00', ('k', 0, 1): 'c01', ('k', 1, 0): 'c10', ('k', 1, 1): 'c11'}

        def last_job(test):
            return max(n for n, e in enumerate(jobs) if test(e))

        split_after = {
            'c00': last_job(lambda e: e[0] == 'proj' and e[1] == 0),
            'c01': last_job(lambda e: e[0] == 'proj' and e[1] == 1),
            'wvi': last_job(lambda e: e[0] == 'proj' and e[1] == 1),
            'c10': last_job(lambda e: e[0] in ('v', 'vimg') and e[1] == 0 and (e[0] == 'vimg' or e[2] < 4)),
            'c11': last_job(lambda e: e[0] == 'v' and e[1] == 0),
        }
        last_k = last_job(lambda e: e[0] == 'proj')
        last_v = last_job(lambda e: e[0] == 'v')

        block = ctx.enter_context(nc.Block())

        @block.sync
        def _(sp):
            x_t = T['x'].rearrange("b (q p) d -> p b q d", p=P)

            def load_raw(i):
                name = SPLITS[i]
                if name[0] == 'w':
                    src = T[name].rearrange("(k p) n -> p k n", p=P)
                else:
                    c0 = int(name[1]) * KEYS + int(name[2]) * 512
                    src = T['ctxT'].rearrange("(k p) n -> p k n", p=P)[:, :, c0:c0 + 512]
                sp.dma_start(raw[:, i % 2], src).then_inc(raw_loaded[i % 2], 16)

            for h in (1,):
                for b in range(NB):
                    sp.dma_start(xin[:, 4 * h + 2 * b:4 * h + 2 * b + 2, :], x_t[:, b, 2 * h:2 * h + 2, :]).then_inc(x_loaded[h], 16)
            load_raw(0)
            load_raw(1)
            for b in range(NB):
                sp.dma_start(xin[:, 2 * b:2 * b + 2, :], x_t[:, b, 0:2, :]).then_inc(x_loaded[0], 16)

            def split(i):
                if i + 2 < len(SPLITS):
                    sp.wait_ge(lo_done, i + 1)
                    load_raw(i + 2)

            def norm(tile):
                kind = TILES[tile]
                for oc in range(KC):
                    n = KC * tile + oc
                    if kind[0] == 'q':
                        dst = qscr[:, kind[1], oc * P:(oc + 1) * P, :]
                    else:
                        dst = kscr[:, kind[1], oc * P:(oc + 1) * P, 512 * kind[2]:512 * kind[2] + 512]
                    sp.wait_ge(norm_done, n + 1)
                    sp.dma_start(dst.rearrange("s p n -> p s n"), hl[:, n % 2].bitcast(F32)).then_inc(hl_stored[n % 2], 16)

            def vstore(b, c):
                i = CH * b + c
                n = job_at[('vimg', b)] if c == IMG_CHUNK else job_at[('v', b, c)]
                sp.wait_ge(emptied_by['act'], emptied(n)[1])
                sp.dma_start(vscr[b, c], vbuf[:, i % 2, :]).then_inc(v_stored[i % 2], 16)

            def load(u):
                h, b, g = unit(u)
                if u == 0:
                    for s in range(2):
                        sp.wait_ge(hl_stored[s], stores_of(4))
                    sp.wait_ge(ind_ready, 1)
                    sp.wait_ge(xn_done, 8)
                    sp.wait_ge(job_done, job_at[('xT', 0, 3)] + 1)
                    sp.wait_ge(lo_done, len(SPLITS))
                if u == 2:
                    for s in range(2):
                        sp.wait_ge(hl_stored[s], stores_of(6))
                for pp in range(2):
                    n = 2 * u + pp
                    slot = n % PAIRS
                    if n >= PAIRS:
                        sp.wait_ge(s2_done, 8 * ((n - PAIRS) // 2 + 1))
                    else:
                        for jj in range(2):
                            sp.dma_start(kst[96:100, slot, jj, :].bitcast(F32), ind[:, :].bitcast(F32)).then_inc(ind_placed, 16)
                    r0 = P * g + 64 * pp
                    for part, row in ((0, 0), (0, 32), (1, 64)):
                        src = kscr[part, b, r0:r0 + 64, :].rearrange("(j d) n -> d j n", d=HD)
                        sp.dma_start(kst[row:row + 32, slot].bitcast(F32), src).then_inc(pair_loaded[slot], 16)
                    for part, row in ((0, 0), (1, 32), (0, 64)):
                        src = qscr[part, h, r0:r0 + 64, b * QH:(b + 1) * QH].rearrange("(j d) n -> d j n", d=HD)
                        sp.dma_start(qst[row:row + 32, slot].bitcast(F32), src).then_inc(pair_loaded[slot], 16)

            def load_v(u):
                h, b, g = unit(u)
                if u == 0:
                    for s in range(2):
                        sp.wait_ge(v_stored[s], 16 * CH)
                    sp.wait_ge(job_done, last_k + 1)
                if u >= 2:
                    sp.wait_ge(pv_done, 8 * (u - 1))
                sp.dma_start(vring[:, u % 2], vscr[b, :, :, P * g:P * (g + 1)].rearrange("c p n -> p c n")).then_inc(v_loaded[u % 2], 16)

            def shift(u):
                sp.wait_ge(emptied_by['dve'], emptied(job_at[('shift', u)])[1])
                for part in range(2):
                    for s in range(2):
                        for pp in range(2):
                            slot = pair_slot(u, 2 * pp)[0]
                            row = 96 + 2 * part + s
                            src = crow[4 * s + 2 * pp:4 * s + 2 * pp + 2, part, :]
                            sp.dma_start(qst[row:row + 1, slot].bitcast(F32), src.bitcast(F32)).then_inc(shift_loaded[u % 2], 16)

            def ch_row():
                sp.wait_ge(emptied_by['dve'], emptied(job_at[('o', 1, 1)])[1])
                sp.wait_ge(chx_zero, 1)
                for b in range(NB):
                    sp.dma_start(chx[b:b + 1, :], x2s[P - 1:P, 2 * b + 1, :]).then_inc(row_loaded, 16)

            def f_out(f):
                h, b, _ = unit(NG * (f // 2))
                sp.wait_ge(out_ready, f + 1)
                sp.dma_start(out.rearrange("b (q p) d -> b q p d", p=P)[b, 2 * h + f % 2], x2s[:, f % XS, :])\
                  .then_inc(slot_stored if f < 8 - XS else out_stored, 16)

            steps = {'split': split, 'norm': norm, 'vstore': vstore, 'load': load, 'load_v': load_v, 'shift': shift,
                     'ch_row': ch_row, 'f_out': f_out}
            for e in plan:
                if e[0] in steps:
                    steps[e[0]](*e[1:])
            sp.wait_ge(slot_stored, 16 * (8 - XS))
            sp.wait_ge(out_stored, 16 * XS)

        @block.tensor
        def _(pe):
            def open_bank(n):
                m = before_in_bank(bank_of[n], n)
                if m is not None:
                    eng, count = emptied(m)
                    pe.wait_ge(emptied_by[eng], count)
                return psum[:, bank_of[n], :]

            def xT(h, n):
                job = job_at[('xT', h, n)]
                ps = open_bank(job)
                if job == 0:
                    pe.wait_ge(const_loaded, 16 * n_const)
                pe.wait_ge(xn_done, 4 * (1 - h) + n + 1)
                for kc in range(KC):
                    mm = pe.transpose(ps[:, kc * P:(kc + 1) * P], xin[:, 4 * h + n, kc * P:(kc + 1) * P], ident[:, :])
                mm.then_inc(job_done, 1)

            def three_passes(ps, left, right):
                for kc in range(KC):
                    for a, b in ((0, 0), (0, 1), (1, 0)):
                        mm = pe.matmul(ps, left(a, kc), right(b, kc), start=(kc == 0 and a + b == 0), stop=(kc == KC - 1 and a == 1))
                return mm

            def proj(tile, oc, piece):
                kind = TILES[tile]
                w, c0, c1 = pieces(tile)[piece][:3]
                job = job_at[('proj', tile, oc, piece)]
                ps = open_bank(job)
                if oc == 0 and piece == 0:
                    if kind[0] == 'q':
                        pe.wait_ge(emptied_by['dve'], emptied(job_at[('xT', kind[1], 3)])[1])
                        pe.wait_ge(lo_done, i_split['wq'] + 1)
                    else:
                        pe.wait_ge(lo_done, max(i_split[tok_of[kind]], i_split['wk']) + 1)
                x = token_parts[1 - kind[1] if kind[0] == 'q' else kind[2]]
                wt = w_parts[w]
                three_passes(ps[:, 0:c1 - c0], lambda a, kc: wt[:, a, kc, oc * P:(oc + 1) * P],
                             lambda a, kc: x[:, a, kc, c0:c1]).then_inc(job_done, 1)

            def sumsq(tile):
                ps = open_bank(job_at[('sumsq', tile)])
                if tile == 0:
                    pe.wait_ge(ones_ready, 1)
                pe.wait_ge(sumsq_added, tile + 1)
                pe.matmul(ps, inv_d[:, :].to_broadcast([P, P]), ssum[:, :], start=True, stop=True).then_inc(job_done, 1)

            def v_job(job, b, c, w):
                ps = open_bank(job)
                pe.wait_ge(lo_done, i_split[w] + 1)
                pe.wait_ge(lo_done, i_split[f"c{b}{c // 4}"] + 1)
                x = token_parts[c // 4]
                wt = w_parts[w]
                t0 = (c % 4) * P
                three_passes(ps, lambda a, kc: x[:, a, kc, t0:t0 + P], lambda a, kc: wt[:, a, kc, :]).then_inc(job_done, 1)

            def v(b, c):
                v_job(job_at[('v', b, c)], b, c, 'wvi' if c < IMG_CHUNK else 'wv')

            def vimg(b):
                v_job(job_at[('vimg', b)], b, IMG_CHUNK, 'wvi')

            def bank_before_attention(bank):
                eng, count = emptied(before_in_bank(bank, n_first))
                pe.wait_ge(emptied_by[eng], count)

            def S1(t):
                u, s = t // 8, t % 8
                j, qt = s // 2, s % 2
                slot, jj, rnd = pair_slot(u, j)
                if s % 4 == 0:
                    pe.wait_ge(pair_loaded[slot], 96 * (rnd + 1))
                if t < 2:
                    bank_before_attention(2 * t)
                    bank_before_attention(2 * t + 1)
                else:
                    pe.wait_ge(exp1_done, t - 1)
                for half in range(2):
                    mm = pe.matmul(score1[:, t % 2, half * 512:(half + 1) * 512], qst[0:96, slot, jj, qt * P:(qt + 1) * P],
                                   kst[0:96, slot, jj, half * 512:(half + 1) * 512], start=True, stop=True)
                mm.then_inc(s1_done, 1)

            def S2(r):
                u, c = r // 8, r % 8
                if r == 0:
                    pe.wait_ge(ind_placed, 16 * 2 * PAIRS)
                    bank_before_attention(4)
                    bank_before_attention(5)
                else:
                    pe.wait_ge(exp2_done, r)
                if c == 0:
                    pe.wait_ge(shift_loaded[u % 2], 16 * 8 * (u // 2 + 1))
                for j in range(HPG):
                    slot, jj, _ = pair_slot(u, j)
                    mm = pe.matmul(score2[:, j * QH:(j + 1) * QH], kst[0:100, slot, jj, c * P:(c + 1) * P],
                                   qst[0:100, slot, jj, :], start=True, stop=True)
                mm.then_inc(s2_done, 1)

            def PV(r):
                u, c = r // 8, r % 8
                if c == 0:
                    pe.wait_ge(v_loaded[u % 2], 16 * (u // 2 + 1))
                    if u == 0:
                        bank_before_attention(PV_BANK)
                    else:
                        pe.wait_ge(attn_done, u)
                pe.wait_ge(exp2_done, r + 1)
                for j in range(HPG):
                    mm = pe.matmul(psum[32 * j:32 * j + 32, PV_BANK, 0:QH], vring[:, u % 2, c, 32 * j:32 * j + 32],
                                   prob[:, r % NP, j * QH:(j + 1) * QH], start=(c == 0), stop=(c == 7))
                mm.then_inc(pv_done, 1)

            def shift(u):
                ps = open_bank(job_at[('shift', u)])
                pe.wait_ge(negc_done, u + 1)
                for qt in range(2):
                    mm = pe.transpose(ps[0:8, qt * P:(qt + 1) * P], negc[:, u % 2, qt * 8:qt * 8 + 8], ident[:, :])
                mm.then_inc(job_done, 1)

            def o(k, n):
                ps = open_bank(job_at[('o', k, n)])
                pe.wait_ge(attn_done, NG * (k + 1))
                if k == 0:
                    pe.wait_ge(late_loaded['wo'], 16)
                for g in range(NG):
                    mm = pe.matmul(ps, attT[:, g, n * P:(n + 1) * P], wo[:, g, :], start=(g == 0), stop=(g == NG - 1))
                mm.then_inc(job_done, 1)

            def ch_turn(i):
                ps = open_bank(job_at[('ch_turn', i)])
                src = chx
                if i == 1 + K_STEPS:
                    pe.wait_ge(emptied_by['dve'], emptied(job_at[('ch_sum', K_STEPS - 1)])[1])
                    src = th
                else:
                    pe.wait_ge(ch_norm, i + 2)
                for kc in range(KC):
                    mm = pe.transpose(ps[:, kc * 32:(kc + 1) * 32], src[:, kc * P:(kc + 1) * P], ident[0:32, 0:32])
                mm.then_inc(job_done, 1)

            def thin(ps, w):
                for kc in range(KC):
                    mm = pe.matmul(ps[0:32, :], tT[:, kc, :], w[:, kc, :], start=(kc == 0), stop=(kc == KC - 1))
                mm.then_inc(job_done, 1)

            def ch_agg():
                ps = open_bank(job_at[('ch_agg',)])
                pe.wait_ge(late_loaded['agg'], 16)
                thin(ps, aggbc)

            def ch_d1(k):
                ps = open_bank(job_at[('ch_d1', k)])
                if k == 0:
                    pe.wait_ge(late_loaded['d1'], 64)
                for kc in range(KC):
                    for j in range(4):
                        mm = pe.matmul(ps[32 * j:32 * j + 32, :], tT[:, kc, :], d1[:, kc, 512 * j:512 * (j + 1)],
                                       start=(kc == 0), stop=(kc == KC - 1))
                mm.then_inc(job_done, 1)

            def ch_hT(k):
                ps = open_bank(job_at[('ch_hT', k)])
                pe.wait_ge(gelu_done, k + 1)
                for m in range(4):
                    mm = pe.transpose(ps[:, m * P:(m + 1) * P], hb[:, m * P:(m + 1) * P], ident[:, :])
                mm.then_inc(job_done, 1)

            def ch_d2(k):
                ps = open_bank(job_at[('ch_d2', k)])
                if k == 0:
                    pe.wait_ge(late_loaded['d2'], 64)
                for j in range(4):
                    for m in range(4):
                        mm = pe.matmul(ps[32 * m:32 * m + 32, :], hT[:, m, 32 * j:32 * j + 32], d2[:, 4 * j + m, :],
                                       start=(j == 0), stop=(j == 3))
                mm.then_inc(job_done, 1)

            def ch_sum(k):
                ps = open_bank(job_at[('ch_sum', k)])
                pe.matmul(ps[0:32, :], sel[:, :], hb[:, :], start=True, stop=True).then_inc(job_done, 1)

            def ch_bc():
                ps = open_bank(job_at[('ch_bc',)])
                pe.wait_ge(late_loaded['bc'], 16)
                thin(ps, aggbc)

            def ch_spread(b):
                ps = open_bank(job_at[('ch_spread', b)])
                pe.wait_ge(emptied_by['dve'], emptied(job_at[('ch_bc',)])[1])
                pe.matmul(ps, ident[0:32, b:b + 1].to_broadcast([32, P]), chx[:, :], start=True, stop=True).then_inc(job_done, 1)

            def f_turn(f):
                ps = open_bank(job_at[('f_turn', f)])
                pe.wait_ge(x2n_done, f + 1)
                for kc in range(KC):
                    mm = pe.transpose(ps[:, kc * P:(kc + 1) * P], x2n[:, kc * P:(kc + 1) * P], ident[:, :])
                mm.then_inc(job_done, 1)

            def f_gate(f):
                ps = open_bank(job_at[('f_gate', f)])
                if f == 0:
                    pe.wait_ge(late_loaded['wg'], 16)
                for kc in range(KC):
                    mm = pe.matmul(ps, xTt[:, kc, :], wg[:, kc, :], start=(kc == 0), stop=(kc == KC - 1))
                mm.then_inc(job_done, 1)

            steps = {'xT': xT, 'proj': proj, 'sumsq': sumsq, 'v': v, 'vimg': vimg, 'S1': S1, 'S2': S2, 'PV': PV,
                     'shift': shift, 'o': o, 'ch_turn': ch_turn, 'ch_agg': ch_agg, 'ch_d1': ch_d1, 'ch_hT': ch_hT,
                     'ch_d2': ch_d2, 'ch_sum': ch_sum, 'ch_bc': ch_bc, 'ch_spread': ch_spread, 'f_turn': f_turn,
                     'f_gate': f_gate}
            for e in plan:
                if e[0] in steps:
                    steps[e[0]](*e[1:])

        @block.scalar
        def _(act):
            for dst, src in ((colp[:], T['cols']), (ident[:, :], T['ident']), (sel[:, :], T['sel'])):
                act.dma_start(dst, src).then_inc(const_loaded, 16)
            act.dma_start(ind_in[:, :], T['ind']).then_inc(const_loaded, 16)
            for i, n in enumerate(('d2_b', 'agg_b', 'bc_b')):
                act.dma_start(chrow[32 * i:32 * i + 32, :], T[n].partition_broadcast(32)).then_inc(const_loaded, 16)
            for j in range(4):
                act.dma_start(d1b[32 * j:32 * j + 32, :], T['d1_b'][512 * j:512 * (j + 1)].partition_broadcast(32)).then_inc(const_loaded, 16)
            act.dma_start(rows[:, 0:2, :], T['rows'][0:2].partition_broadcast(P)).then_inc(const_loaded, 16)
            act.dma_start(rows[:, 2:4, :], T['rows'][2:4].partition_broadcast(P)).then_inc(const_loaded, 16)
            links = [0]

            def link(ins):
                links[0] += 1
                ins.then_inc(act_order, 1)
                act.wait_ge(act_order, links[0])

            def rstd(dst, var, eps):
                link(act.activation(dst, var, ACT.Ln, bias=eps))
                return act.activation(dst, dst, ACT.Exp, scale=-0.5)

            def split(i):
                name = SPLITS[i]
                act.wait_ge(raw_loaded[i % 2], 16 * (i // 2 + 1))
                if name in split_after:
                    act.wait_ge(job_done, split_after[name] + 1)
                dst = w_parts[name] if name[0] == 'w' else token_parts[int(name[2])]
                act.activation(dst[:, 0], raw[:, i % 2], ACT.Copy).then_inc(hi_done, 1)

            def xstat(h):
                act.wait_ge(x_mean, 2 - h)
                rstd(rs[:, 4 * h:4 * h + 4], mv[:, 4 * h:4 * h + 4, 1], epsln[:, 0:1]).then_inc(x_rstd, 1)

            def proj(tile, oc, piece):
                _, c0, _, k0, k1, bias, _ = pieces(tile)[piece]
                job = job_at[('proj', tile, oc, piece)]
                if oc == 0 and piece == 0:
                    if tile >= 1:
                        act.wait_ge(sumsq_added, tile)
                    if tile == 0:
                        act.wait_ge(ind_ready, 1)
                if tile >= 2 and piece == 0:
                    act.wait_ge(norm_done, KC * (tile - 2) + oc + 1)
                act.wait_ge(job_done, job + 1)
                src = psum[:, bank_of[job], k0 - c0:k1 - c0]
                b = colp[:, bias, oc:oc + 1]
                act.activation(raw4[:, tile % 2, oc, k0:k1], src, ACT.Identity, bias=b)
                act.activation(sq4[:, oc, k0:k1], src, ACT.Square, bias=b).then_inc(emptied_by['act'], 1)

            def sumsq(tile):
                job = job_at[('sumsq', tile)]
                if tile >= 2:
                    act.wait_ge(norm_done, KC * (tile - 1))
                act.wait_ge(job_done, job + 1)
                r = rt[:, tile % 2, :]
                n = emptied(job)[1]
                act.activation(r, psum[:, bank_of[job], :], ACT.Ln, bias=epsf[:, 0:1]).then_inc(emptied_by['act'], 1)
                act.wait_ge(emptied_by['act'], n)
                act.activation(r, r, ACT.Exp, scale=-0.5).then_inc(rms_done, 1)

            def v(b, c):
                i = CH * b + c
                job = job_at[('v', b, c)]
                if i >= 2:
                    act.wait_ge(v_stored[i % 2], 16 * (i // 2))
                act.wait_ge(job_done, job + 1)
                act.copy(vbuf[:, i % 2, :], psum[:, bank_of[job], :]).then_inc(emptied_by['act'], 1)

            def vimg(b):
                job = job_at[('vimg', b)]
                act.wait_ge(emptied_by['act'], emptied(job_at[('v', b, IMG_CHUNK)])[1])
                act.wait_ge(job_done, job + 1)
                act.copy(vbuf[0:1, (CH * b + IMG_CHUNK) % 2, :], psum[0:1, bank_of[job], :]).then_inc(emptied_by['act'], 1)

            def exp1(t):
                u, s = t // 8, t % 8
                j, qt = s // 2, s % 2
                act.wait_ge(max_done, t + 1)
                for st, (k0, k1) in enumerate(((0, IMG), (IMG, KEYS))):
                    col = qt * 8 + st * 4 + j
                    s1 = score1[:, t % 2, k0:k1]
                    ins = act.activation(s1, s1, ACT.Exp, bias=negm[:, u % 2, col:col + 1], accum_out=esum[:, u % 2, col:col + 1])
                ins.then_inc(exp1_done, 1)

            def S1(t):
                if t >= 1:
                    exp1(t - 1)
                if t == 8 * NU - 1:
                    exp1(t)

            def S2(r):
                act.wait_ge(s2_done, r + 1)
                if r >= NP:
                    act.wait_ge(pv_done, r - NP + 1)
                act.activation(prob[:, r % NP, :], score2, ACT.Exp).then_inc(exp2_done, 1)

            def logs(u):
                act.wait_ge(exp1_done, 8 * (u + 1))
                act.activation(lnl[:, u % 2, :], esum[:, u % 2, :], ACT.Ln).then_inc(ln_done, 1)

            def ch_stat(i):
                act.wait_ge(ch_stats, i + 1)
                rstd(crs[0:32, :], cmv[0:32, 1:2], (epsln if i == 0 else epsf)[0:32, 0:1]).then_inc(ch_rstd, 1)

            def ch_d1(k):
                act.wait_ge(gelu_in, k + 1)
                act.activation(hb[:, :], hb[:, :], ACT.Gelu).then_inc(gelu_done, 1)
                act.preload_act_table_set("natural_log_exp_and_others")

            def f_stat(f):
                act.wait_ge(f_stats, f_stat_count[('f_stat', f)])
                rstd(frs[:, f % 2, 0:1], fmv[:, f % 2, 0, 1:2], epsln[:, 0:1]).then_inc(f_rstd, 1)

            def f_turn(f):
                job = job_at[('f_turn', f)]
                act.wait_ge(job_done, job + 1)
                act.copy(xTt[:].rearrange("p k n -> p (k n)"), psum[:, bank_of[job], :]).then_inc(emptied_by['act'], 1)

            def f_gate(f):
                z = zt[:, f % 2, :]
                act.wait_ge(z_ready, f + 1)
                act.activation(z, z, ACT.Exp, scale=-1.0).then_inc(z_exp, 1)
                act.wait_ge(z_clamped, f + 1)
                link(act.activation(z, z, ACT.Ln, bias=1.0))
                act.activation(z, z, ACT.Exp, scale=-1.0).then_inc(gate_done, 1)

            def f_stat2(f):
                act.wait_ge(f_stats, f_stat_count[('f_stat2', f)])
                rstd(frs[:, f % 2, 1:2], fmv[:, f % 2, 1, 1:2], epsf[:, 0:1]).then_inc(f_rstd, 1)

            act.preload_act_table_set("natural_log_exp_and_others")
            act.wait_ge(ones_ready, 1)
            act.wait_ge(const_loaded, 16 * n_const)
            steps = {'split': split, 'xstat': xstat, 'proj': proj, 'sumsq': sumsq, 'v': v, 'vimg': vimg, 'S1': S1,
                     'S2': S2, 'logs': logs, 'ch_stat': ch_stat, 'ch_d1': ch_d1, 'f_stat': f_stat, 'f_turn': f_turn,
                     'f_gate': f_gate, 'f_stat2': f_stat2}
            for e in plan:
                if e[0] in steps:
                    steps[e[0]](*e[1:])

        @block.vector
        def _(dve):
            links = [0]

            def link(ins):
                links[0] += 1
                ins.then_inc(dve_order, 1)
                dve.wait_ge(dve_order, links[0])

            dve.memset(epsln[:, :], EPS_LN)
            dve.memset(epsf[:, :], EPS)
            dve.memset(inv_d[:, :], 1.0 / D).then_inc(ones_ready, 1)
            dve.wait_ge(const_loaded, 16 * n_const)
            dve.tensor_copy(ind[:, :], ind_in[:, :]).then_inc(ind_ready, 1)
            dve.tensor_scalar(qw[:, :], colp[:, NQ, :], SCALE, None, ALU.mult)
            dve.tensor_tensor(vbias[:, :], colp[:, VB, :], colp[:, VIB, :], ALU.add).then_inc(qw_ready, 1)

            def stats(src, st, mean_var):
                link(dve.bn_stats(st, src))
                return dve.bn_aggr(mean_var, st)

            def split(i):
                name = SPLITS[i]
                dst = w_parts[name] if name[0] == 'w' else token_parts[int(name[2])]
                dve.wait_ge(hi_done, i + 1)
                dve.tensor_tensor(dst[:, 1], raw[:, i % 2], dst[:, 0], ALU.subtract).then_inc(lo_done, 1)

            def xstat(h):
                dve.wait_ge(x_loaded[h], 32)
                for n in range(4):
                    dve.bn_stats(bst[:, 4 * h + n, :], xin[:, 4 * h + n, :]).then_inc(dve_order, 1)
                links[0] += 4
                dve.wait_ge(dve_order, links[0])
                for n in range(4):
                    ins = dve.bn_aggr(mv[:, 4 * h + n, :], bst[:, 4 * h + n, :])
                ins.then_inc(x_mean, 1)

            def xnorm(h):
                dve.wait_ge(x_mean, 2 - h)
                dve.wait_ge(x_rstd, 2 - h)
                for n in range(4):
                    i = 4 * h + n
                    dve.tensor_scalar(xin[:, i, :], xin[:, i, :], mv[:, i, 0:1], rs[:, i:i + 1], ALU.subtract, ALU.mult)\
                       .then_inc(xn_done, 1)

            def xT(h, n):
                job = job_at[('xT', h, n)]
                dve.wait_ge(job_done, job + 1)
                src = psum[:, bank_of[job], :].rearrange("p (k n) -> p k n", k=KC)
                dst = token_parts[1 - h]
                cols = slice(n * P, (n + 1) * P)
                link(dve.tensor_copy(dst[:, 0, :, cols], src))
                dve.tensor_tensor(dst[:, 1, :, cols], src, dst[:, 0, :, cols], ALU.subtract).then_inc(emptied_by['dve'], 1)

            def norm(tile):
                kind = TILES[tile]
                dve.wait_ge(rms_done, tile + 1)
                for oc in range(KC):
                    n = KC * tile + oc
                    x = raw4[:, tile % 2, oc, :]
                    for _, _, _, k0, k1, _, w in pieces(tile):
                        wcol = qw[:, oc:oc + 1] if w is None else colp[:, w, oc:oc + 1]
                        ins = dve.scalar_tensor_tensor(x[:, k0:k1], x[:, k0:k1], wcol, rt[:, tile % 2, k0:k1], ALU.mult, ALU.mult)
                    link(ins)
                    if n >= 2:
                        dve.wait_ge(hl_stored[n % 2], 16 * (n // 2))
                    link(dve.tensor_copy(hl[:, n % 2, 0, :], x))
                    dve.tensor_tensor(hl[:, n % 2, 1, :], x, hl[:, n % 2, 0, :], ALU.subtract).then_inc(norm_done, 1)

            def S1(t):
                u, s = t // 8, t % 8
                j, qt = s // 2, s % 2
                dve.wait_ge(s1_done, t + 1)
                for st, (k0, k1) in enumerate(((0, IMG), (IMG, KEYS))):
                    col = qt * 8 + st * 4 + j
                    ins = dve.tensor_reduce(negm[:, u % 2, col:col + 1], score1[:, t % 2, k0:k1], AX.X, ALU.max, negate=True)
                ins.then_inc(max_done, 1)

            def attn(u):
                g = u % NG
                dve.wait_ge(pv_done, 8 * (u + 1))
                if u >= NG and g == 0:
                    dve.wait_ge(job_done, job_at[('o', u // NG - 1, 1)] + 1)
                dve.tensor_scalar(attT[:, g, :], psum[:, PV_BANK, 0:QH], vbias[:, g:g + 1], None, ALU.add).then_inc(attn_done, 1)

            def shift(u):
                job = job_at[('shift', u)]
                dve.wait_ge(ln_done, u + 1)
                dve.wait_ge(max_done, 8 * (u + 1))
                dve.tensor_tensor(negc[:, u % 2, :], negm[:, u % 2, :], lnl[:, u % 2, :], ALU.subtract).then_inc(negc_done, 1)
                if u >= 1:
                    dve.wait_ge(shift_loaded[(u - 1) % 2], 16 * 8 * ((u + 1) // 2))
                dve.wait_ge(job_done, job + 1)
                src = psum[0:8, bank_of[job], 0:QH]
                link(dve.tensor_copy(crow[:, 0, :], src))
                dve.tensor_tensor(crow[:, 1, :], src, crow[:, 0, :], ALU.subtract).then_inc(emptied_by['dve'], 1)

            def o(k, n):
                job = job_at[('o', k, n)]
                f = 2 * k + n
                dve.wait_ge(res_ready, f + 1)
                dve.wait_ge(job_done, job + 1)
                dve.tensor_tensor(x2s[:, f % XS, :], psum[:, bank_of[job], :], x2s[:, f % XS, :], ALU.add).then_inc(emptied_by['dve'], 1)

            def ch_stat(i):
                src = chx if i < 2 else th
                if i == 0:
                    dve.wait_ge(row_loaded, 32)
                elif i == 1:
                    dve.wait_ge(ch_norm, 1)
                else:
                    job = job_at[('ch_agg',)] if i == 2 else job_at[('ch_sum', i - 3)]
                    dve.wait_ge(emptied_by['dve'], emptied(job)[1])
                stats(src[:, :], cst[0:32, :], cmv[0:32, :]).then_inc(ch_stats, 1)

            def ch_ln(i):
                src = chx if i < 2 else th
                dve.wait_ge(ch_stats, i + 1)
                dve.wait_ge(ch_rstd, i + 1)
                dve.tensor_scalar(chx[:, :], src[:, :], cmv[0:32, 0:1], crs[0:32, 0:1], ALU.subtract, ALU.mult).then_inc(ch_norm, 1)

            def ch_turn(i):
                job = job_at[('ch_turn', i)]
                dve.wait_ge(job_done, job + 1)
                for kc in range(KC):
                    src = psum[:, bank_of[job], kc * 32:(kc + 1) * 32]
                    if i == 1 + K_STEPS:
                        ins = dve.tensor_copy(tT[:, kc, :], src)
                    else:
                        ga, be = (ING, INB) if i == 0 else (PNG, PNB)
                        ins = dve.tensor_scalar(tT[:, kc, :], src, colp[:, ga, kc:kc + 1], colp[:, be, kc:kc + 1], ALU.mult, ALU.add)
                ins.then_inc(emptied_by['dve'], 1)

            def ch_agg():
                job = job_at[('ch_agg',)]
                dve.wait_ge(job_done, job + 1)
                dve.tensor_tensor(th[:, :], psum[0:32, bank_of[job], :], chrow[32:64, :], ALU.add).then_inc(emptied_by['dve'], 1)

            def ch_d1(k):
                job = job_at[('ch_d1', k)]
                dve.wait_ge(job_done, job + 1)
                dve.tensor_tensor(hb[:, :], psum[:, bank_of[job], :], d1b[:, :], ALU.add).then_inc(gelu_in, 1)
                dve.wait_ge(gelu_in, k + 1)
                dve.engine_nop().then_inc(emptied_by['dve'], 1)

            def ch_hT(k):
                job = job_at[('ch_hT', k)]
                dve.wait_ge(job_done, job + 1)
                dve.tensor_copy(hT[:].rearrange("p k n -> p (k n)"), psum[:, bank_of[job], :]).then_inc(emptied_by['dve'], 1)

            def ch_d2(k):
                job = job_at[('ch_d2', k)]
                dve.wait_ge(job_done, job + 1)
                dve.tensor_copy(hb[:, :], psum[:, bank_of[job], :]).then_inc(emptied_by['dve'], 1)

            def ch_sum(k):
                job = job_at[('ch_sum', k)]
                dve.wait_ge(tb_ready, k + 1)
                dve.wait_ge(job_done, job + 1)
                dve.tensor_tensor(th[:, :], psum[0:32, bank_of[job], :], th[:, :], ALU.add).then_inc(emptied_by['dve'], 1)

            def ch_bc():
                job = job_at[('ch_bc',)]
                dve.wait_ge(job_done, job + 1)
                dve.tensor_tensor(chx[:, :], psum[0:32, bank_of[job], :], chrow[64:96, :], ALU.add).then_inc(emptied_by['dve'], 1)

            def ch_spread(b):
                job = job_at[('ch_spread', b)]
                dve.wait_ge(job_done, job + 1)
                dve.tensor_copy((bcb0, bcb1)[b][:, :], psum[:, bank_of[job], :]).then_inc(emptied_by['dve'], 1)

            def f_stat(f):
                dve.wait_ge(emptied_by['dve'], emptied(job_at[('o', f // 2, f % 2)])[1])
                stats(x2s[:, f % XS, :], fst[:, f % 2, 0, :], fmv[:, f % 2, 0, :]).then_inc(f_stats, 1)

            def f_turn(f):
                if f >= 1:
                    dve.wait_ge(mix_done, f)
                dve.wait_ge(f_stats, f_stat_count[('f_stat', f)])
                dve.wait_ge(f_rstd, f_stat_count[('f_stat', f)])
                dve.tensor_scalar(x2n[:, :], x2s[:, f % XS, :], fmv[:, f % 2, 0, 0:1], frs[:, f % 2, 0:1], ALU.subtract, ALU.mult)\
                   .then_inc(x2n_done, 1)

            def f_gate(f):
                job = job_at[('f_gate', f)]
                if f >= 2:
                    dve.wait_ge(out_ready, f - 1)
                dve.wait_ge(job_done, job + 1)
                dve.tensor_tensor(zt[:, f % 2, :], psum[:, bank_of[job], :], rows[:, R_GATE, :], ALU.add).then_inc(z_ready, 1)
                dve.wait_ge(z_ready, f + 1)
                dve.engine_nop().then_inc(emptied_by['dve'], 1)

            def f_stat2(f):
                dve.wait_ge(mix_done, f + 1)
                stats(zt[:, f % 2, :], fst[:, f % 2, 1, :], fmv[:, f % 2, 1, :]).then_inc(f_stats, 1)

            def f_out(f):
                z = zt[:, f % 2, :]
                dve.wait_ge(f_stats, f_stat_count[('f_stat2', f)])
                dve.wait_ge(f_rstd, f_stat_count[('f_stat2', f)])
                dve.wait_ge(x2b_ready, f + 1)
                link(dve.tensor_scalar(z, z, fmv[:, f % 2, 1, 0:1], frs[:, f % 2, 1:2], ALU.subtract, ALU.mult))
                link(dve.tensor_tensor(z, z, rows[:, R_OG, :], ALU.mult))
                dve.tensor_tensor(x2s[:, f % XS, :], z, x2s[:, f % XS, :], ALU.add).then_inc(out_ready, 1)

            steps = {'split': split, 'xstat': xstat, 'xnorm': xnorm, 'xT': xT, 'norm': norm, 'S1': S1, 'attn': attn,
                     'shift': shift, 'o': o, 'ch_stat': ch_stat, 'ch_ln': ch_ln, 'ch_turn': ch_turn, 'ch_agg': ch_agg,
                     'ch_d1': ch_d1, 'ch_hT': ch_hT, 'ch_d2': ch_d2, 'ch_sum': ch_sum, 'ch_bc': ch_bc,
                     'ch_spread': ch_spread, 'f_stat': f_stat, 'f_turn': f_turn, 'f_gate': f_gate,
                     'f_stat2': f_stat2, 'f_out': f_out}
            for e in plan:
                if e[0] in steps:
                    steps[e[0]](*e[1:])

        @block.gpsimd
        def _(pool):
            links = [0]

            def link(ins):
                links[0] += 1
                ins.then_inc(pool_order, 1)
                pool.wait_ge(pool_order, links[0])

            def sumsq(tile):
                pool.wait_ge(emptied_by['act'], emptied(job_at[('proj', tile, KC - 1, len(pieces(tile)) - 1)])[1])
                if tile >= 1:
                    pool.wait_ge(job_done, job_at[('sumsq', tile - 1)] + 1)
                link(pool.tensor_tensor(ssum[:, :], sq4[:, 0, :], sq4[:, 1, :], ALU.add))
                link(pool.tensor_tensor(ssum[:, :], ssum[:, :], sq4[:, 2, :], ALU.add))
                pool.tensor_tensor(ssum[:, :], ssum[:, :], sq4[:, 3, :], ALU.add).then_inc(sumsq_added, 1)

            def load_res(f):
                h, b, _ = unit(NG * (f // 2))
                pool.dma_start(x2s[:, f % XS, :], T['x'][b, (2 * h + f % 2) * P:(2 * h + f % 2 + 1) * P, :]).then_inc(res_loaded, 16)

            def add_o_bias(f):
                pool.tensor_tensor(x2s[:, f % XS, :], x2s[:, f % XS, :], rows[:, R_O, :], ALU.add).then_inc(res_ready, 1)

            def res2():
                pool.wait_ge(slot_stored, 16 * (8 - XS))
                for f in range(XS, 8):
                    load_res(f)
                pool.wait_ge(res_loaded, 16 * 8)
                for f in range(XS, 8):
                    add_o_bias(f)

            def phase2():
                pool.wait_ge(job_done, last_v + 1)
                for s in range(2):
                    pool.wait_ge(hl_stored[s], stores_of(6))
                    pool.wait_ge(v_stored[s], 16 * CH)
                pool.wait_ge(ind_placed, 16 * 2 * PAIRS)
                for f in range(XS):
                    load_res(f)
                pool.dma_start(wo[:], T['wo'].rearrange("(k p) n -> p k n", p=P)).then_inc(late_loaded['wo'], 16)

            def late(i):
                if i == 0:
                    pool.wait_ge(res_loaded, 16 * XS)
                    for f in range(XS):
                        add_o_bias(f)
                elif i == 1:
                    pool.dma_start(aggbc[:], T['agg'].rearrange("(k p) n -> p k n", p=P)).then_inc(late_loaded['agg'], 16)
                elif i == 2:
                    pool.dma_start(wg[:], T['wg'].rearrange("(k p) n -> p k n", p=P)).then_inc(late_loaded['wg'], 16)
                elif i < 7:
                    kc = i - 3
                    pool.dma_start(d1[:, kc, :], T['d1'][kc * P:(kc + 1) * P, :]).then_inc(late_loaded['d1'], 16)
                elif i < 11:
                    c = 4 * (i - 7)
                    pool.dma_start(d2[:, c:c + 4, :], T['d2'][c * P:(c + 4) * P, :].rearrange("(k p) n -> p k n", p=P))\
                        .then_inc(late_loaded['d2'], 16)
                else:
                    pool.wait_ge(max_done, 24)
                    pool.memset(chx[:, :], 0.0).then_inc(chx_zero, 1)

            def ch_d1(k):
                pool.wait_ge(ch_norm, 3 + k)
                pool.tensor_tensor(th[:, :], th[:, :], chrow[0:32, :], ALU.add).then_inc(tb_ready, 1)

            def ch_d2(k):
                if k == 0:
                    pool.dma_start(aggbc[:], T['bc'].rearrange("(k p) n -> p k n", p=P)).then_inc(late_loaded['bc'], 16)

            def f_turn(f):
                pool.wait_ge(x2n_done, f + 1)
                pool.tensor_tensor(x2s[:, f % XS, :], x2s[:, f % XS, :], rows[:, R_OB, :], ALU.add).then_inc(x2b_ready, 1)

            def f_gate(f):
                h, b, _ = unit(NG * (f // 2))
                z = zt[:, f % 2, :]
                pool.wait_ge(z_exp, f + 1)
                pool.tensor_scalar(z, z, 1e18, 0.0, ALU.min, ALU.max).then_inc(z_clamped, 1)
                pool.wait_ge(gate_done, f + 1)
                if f < 2:
                    pool.wait_ge(emptied_by['dve'], emptied(job_at[('ch_spread', 1)])[1])
                link(pool.tensor_tensor(z, z, (bcb0, bcb1)[b][:, :], ALU.mult))
                pool.tensor_tensor(z, z, x2n[:, :], ALU.add).then_inc(mix_done, 1)

            steps = {'sumsq': sumsq, 'phase2': phase2, 'late': late, 'res2': res2, 'ch_d1': ch_d1, 'ch_d2': ch_d2, 'f_turn': f_turn,
                     'f_gate': f_gate}
            for e in plan:
                if e[0] in steps:
                    steps[e[0]](*e[1:])


def kernel(**inputs):
    import concourse.bacc as bacc
    from concourse.bass_utils import run_bass_kernel_spmd

    get = lambda n: np.asarray(inputs[n])
    eye = np.eye(P, dtype=np.float32)
    ind = np.zeros((4, KEYS), np.float32)
    ind[0::2, :IMG] = 1
    ind[1::2, IMG:] = 1
    host = {
        'x': get('x'),
        'ctxT': get('ctx_2048').reshape(NB * KEYS, D).T,
        'wq': get('L0_xattn_q_w').T, 'wk': get('L0_xattn_k_w').T, 'wki': get('L0_xattn_k_img_w').T,
        'wv': get('L0_xattn_v_w').T, 'wvi': get('L0_xattn_v_img_w').T, 'wo': get('L0_xattn_o_w').T,
        'wg': get('L0_ffn_gate_w'), 'agg': get('L0_ffn_agg_w'), 'bc': get('L0_ffn_bc_w'),
        'd1': get('L0_ffn_d1_w'), 'd2': get('L0_ffn_d2_w'),
        'cols': np.stack([get(n).reshape(KC, P).T for n in COLS], axis=1),
        'rows': np.stack([get(n) for n in ROWS]),
        'agg_b': get('L0_ffn_agg_b'), 'd2_b': get('L0_ffn_d2_b'), 'bc_b': get('L0_ffn_bc_b'),
        'd1_b': get('L0_ffn_d1_b'),
        'ident': eye, 'ind': ind, 'sel': np.tile(eye[:32, :32], (4, 1)),
    }
    nc = bacc.Bacc("TRN2", target_bir_lowering=False, num_devices=1)
    arrays = {n: np.ascontiguousarray(a) for n, a in host.items()}
    T = {n: nc.dram_tensor(n, a.shape, F32, kind="ExternalInput").ap() for n, a in arrays.items()}
    out = nc.dram_tensor("out", (NB, TOK, D), F32, kind="ExternalOutput").ap()
    build(nc, T, out)
    r = run_bass_kernel_spmd(nc, [arrays], core_ids=[0])
    return r.results[0]["out"]
```

```python
from contextlib import ExitStack

import numpy as np

import concourse.bass as bass
from concourse import mybir

F32 = mybir.dt.float32
F32R = mybir.dt.float32r
ALU = mybir.AluOpType
ACT = mybir.ActivationFunctionType
AX = mybir.AxisListType

P = 128
D = 512
KC = D // P
NB = 2
TOK = 512
KEYS = 1024
IMG = 257
IMG_CHUNK = IMG // P
NH = 16
HD = D // NH
HPG = P // HD
NG = NH // HPG
QH = TOK // 2
NU = 2 * NB * NG
CH = KEYS // P
PAIRS = 6
NP = 2
XS = 6
F_EVERY = 3
LEAD = 4
HID = 2048
K_STEPS = 4
CHUNKS = 2
EPS_LN = 1e-5
EPS = 1e-6
SCALE = 1.0 / float(np.sqrt(np.float32(HD)))

COLS = ['L0_xattn_q_b', 'L0_xattn_k_b', 'L0_xattn_k_img_b', 'L0_xattn_norm_q_w', 'L0_xattn_norm_k_w',
        'L0_xattn_norm_k_img_w', 'L0_xattn_v_b', 'L0_xattn_v_img_b', 'L0_ffn_in_gamma', 'L0_ffn_in_beta',
        'L0_ffn_pn_gamma', 'L0_ffn_pn_beta']
QB, KB, KIB, NQ, NK, NKI, VB, VIB, ING, INB, PNG, PNB = range(len(COLS))
ROWS = ['L0_xattn_o_b', 'L0_ffn_gate_b', 'L0_ffn_out_gamma', 'L0_ffn_out_beta']
R_O, R_GATE, R_OG, R_OB = range(4)


def make_plan():
    plan = []
    add = lambda *e: plan.append(e)

    def proj(tile):
        kind = TILES[tile]
        for oc in range(KC):
            for piece in range(2 if kind[0] == 'k' and kind[2] == 0 else 1):
                add('proj', tile, oc, piece)

    def v(b, chunks):
        for c in chunks:
            add('v', b, c)
            if c == IMG_CHUNK:
                add('vimg', b)
            add('vstore', b, c)

    add('split', 0)
    add('xstat', 1)
    add('xnorm', 1)
    for n in range(4):
        add('xT', 1, n)
    add('split', 1)
    add('xstat', 0)
    add('xnorm', 0)
    proj(0)
    for n in range(4):
        add('xT', 0, n)
    add('split', 2)
    add('sumsq', 0)
    add('split', 3)
    proj(1)
    add('norm', 0)
    add('split', 4)
    proj(2)
    add('sumsq', 1)
    add('norm', 1)
    add('split', 5)
    add('split', 6)
    proj(3)
    add('sumsq', 2)
    add('norm', 2)
    v(0, range(0, 1))
    add('sumsq', 3)
    v(0, range(1, 4))
    add('norm', 3)
    add('split', 7)
    v(0, range(4, 8))
    add('split', 8)
    proj(4)
    add('load', 0)
    proj(5)
    add('sumsq', 4)
    add('norm', 4)
    v(1, range(0, 1))
    add('sumsq', 5)
    v(1, range(1, 4))
    add('norm', 5)
    v(1, range(4, 8))
    add('phase2')
    add('load_v', 0)
    add('load', 1)
    add('load_v', 1)
    add('load', 2)
    ahead = 8 + LEAD
    extra = {}

    def at(step, *e):
        extra.setdefault(step, []).append(e)

    def closed(s):
        while any((s + n + ahead) % 8 == 1 for n in range(1, KC // CHUNKS)):
            s += 1
        return s

    s = 8 * 8 + 4
    at(s, 'ch_row')
    at(s + 2, 'ch_stat', 0)
    at(s + 3, 'ch_ln', 0)
    at(s + 3, 'ch_stat', 1)
    at(s + 4, 'ch_ln', 1)
    at(s + 4, 'ch_turn', 0)
    at(s + 5, 'ch_agg')
    at(s + 5, 'ch_stat', 2)
    s += 6
    for k in range(K_STEPS):
        at(s, 'ch_ln', 2 + k)
        at(s + 1, 'ch_turn', 1 + k)
        s = closed(s + 2)
        for kc in range(KC):
            at(s + kc // CHUNKS, 'ch_d1', k, kc)
        s += KC // CHUNKS
        at(s, 'ch_gelu', k)
        at(s + 1, 'ch_hT', k)
        s = closed(s + 2)
        for m in range(KC):
            at(s + m // CHUNKS, 'ch_d2', k, m)
        s += KC // CHUNKS
        at(s, 'ch_sum', k)
        if k < K_STEPS - 1:
            at(s, 'ch_stat', 3 + k)
        s += 1
    at(s, 'ch_turn', 1 + K_STEPS)
    at(s + 1, 'ch_bc')
    at(s + 2, 'ch_spread', 0)
    at(s + 2, 'ch_spread', 1)
    s += 3
    at(s, 'res2')
    for f in range(8):
        if f >= 6:
            s = max(s, 8 * NU)
        while (s + 4 + ahead) % 8 == 1 and s + 4 < 8 * NU:
            s += 1
        at(s, 'f_stat', f)
        at(s + 1, 'f_norm', f)
        at(s + 2, 'f_turn', f)
        at(s + 3, 'f_gate', f, 0)
        at(s + 4, 'f_gate', f, 1)
        at(s + 5, 'f_exp', f)
        at(s + 6, 'f_sig', f)
        at(s + 8, 'f_stat2', f)
        at(s + 9, 'f_out', f)
        s += F_EVERY
    cut = {s for s, es in extra.items() for e in es if e[0] in ('ch_d1', 'ch_d2', 'f_gate') and e[2] > 0
           and not any(x[:2] == e[:2] and x[2] == 0 for x in es)}
    for k in range(4):
        s = 8 * NG * (k + 1) + (1 if k < 3 else 0)
        for n in range(2):
            while s in cut:
                s += 1
            extra.setdefault(s, []).insert(n if k == 3 else 0, ('o', k, n))
            s += 1 if k < 3 else 0
    for t in range(ahead):
        add('S1', t)
    last = max(max(extra), 8 * NU)
    for r in range(last + 1):
        if r < 8 * NU:
            add('S2', r)
            if r % 8 == 0 and r > 0 and r // 8 + 2 < NU:
                add('load', r // 8 + 2)
            if r % 8 == 1 and r // 8 + 1 < NU and r > 8:
                add('load_v', r // 8 + 1)
        if 1 <= r <= 8 * NU:
            add('PV', r - 1)
            if r % 8 == 0:
                add('attn', r // 8 - 1)
        t = r + ahead
        if t % 8 == 1 and t // 8 <= NU:
            add('shift', t // 8 - 1)
        if r < 12:
            add('late', r)
        for e in extra.get(r, []):
            plan.append(e)
        if t < 8 * NU:
            add('S1', t)
        if t % 8 == 0 and t <= 8 * NU:
            add('logs', t // 8 - 1)
    first = [i for i, e in enumerate(plan) if e == ('S1', 8)][0]
    plan.insert(first + 1, ('logs', 0))
    first = [i for i, e in enumerate(plan) if e == ('S1', 9)][0]
    plan.insert(first + 1, ('shift', 0))
    return plan


TILES = [('q', 1), ('q', 0), ('k', 0, 0), ('k', 0, 1), ('k', 1, 0), ('k', 1, 1)]
SPLITS = ['wq', 'wki', 'wk', 'c00', 'c01', 'wvi', 'wv', 'c10', 'c11']
JOBS = {'xT': 'dve', 'proj': 'act', 'sumsq': 'act', 'v': 'act', 'vimg': 'act', 'shift': 'dve', 'o': 'dve',
        'ch_turn': 'dve', 'ch_agg': 'dve', 'ch_d1': 'dve', 'ch_hT': 'dve', 'ch_d2': 'dve', 'ch_sum': 'dve',
        'ch_bc': 'dve', 'ch_spread': 'dve', 'f_turn': 'act', 'f_gate': 'dve'}
PV_BANK = 6
SHARED_BANK = 7


def build(nc, T, out):
    plan = make_plan()
    jobs = [e for e in plan if e[0] in JOBS and not (e[0] in ('ch_d1', 'ch_d2') and e[2] < KC - 1)
            and not (e[0] == 'f_gate' and e[2] == 0)]
    for n, e in enumerate(plan):
        if e[0] in ('ch_d1', 'ch_d2', 'f_gate') and e[2] == 0:
            end = plan.index((e[0], e[1], 1 if e[0] == 'f_gate' else KC - 1))
            within = [x for x in plan[n:end] if x[0] in JOBS and x[:2] != e[:2]]
            assert not within, within
    job_at = {e: n for n, e in enumerate(jobs)}
    n_first = next(n for n, e in enumerate(jobs) if e[0] == 'shift')
    bank_of = [n % 8 if n < n_first else SHARED_BANK for n in range(len(jobs))]

    def emptied(n):
        eng = JOBS[jobs[n][0]]
        return eng, sum(JOBS[e[0]] == eng for e in jobs[:n + 1])

    def before_in_bank(bank, n):
        return max((m for m in range(n) if bank_of[m] == bank), default=None)

    def pieces(tile):
        kind = TILES[tile]
        if kind[0] == 'q':
            return [('wq', 0, 512, 0, 512, QB, None)]
        if kind[2] == 1:
            return [('wk', 0, 512, 0, 512, KB, NK)]
        return [('wki', 0, IMG + 1, 0, IMG, KIB, NKI), ('wk', IMG - 1, 512, IMG, 512, KB, NK)]

    def unit(u):
        k = u // NG
        return 1 - k // NB, k % NB, u % NG

    def pair_slot(u, j):
        n = 2 * u + j // 2
        return n % PAIRS, j % 2, n // PAIRS

    ctx = ExitStack()
    with ctx:
        base = (nc.sbuf_base + 63) // 64 * 64
        KB_ = 1024

        def sb(name, shape, dt, off):
            return nc.alloc_sbuf_tensor_at(name, shape, dt, offset=base + int(off))

        kst = sb("kst", [P, PAIRS, 2, KEYS], F32R, 0)
        qst = sb("qst", [P, PAIRS, 2, QH], F32R, 48 * KB_)
        o = 60 * KB_
        colp = sb("colp", [P, len(COLS), KC], F32, o); o += 256
        rows = sb("rows", [P, 4, D], F32, o); o += 8 * KB_
        chrow = sb("chrow", [P, D], F32, o); o += 2 * KB_
        d1b = sb("d1b", [P, D], F32, o)
        bcb0 = sb("bcb0", [P, D], F32, o); o += 2 * KB_
        ident = sb("ident", [P, P], F32, o); o += 512
        inv_d = sb("inv_d", [P, 1], F32, o); o += 32
        epsln = sb("epsln", [P, 1], F32, o); o += 32
        epsf = sb("epsf", [P, 1], F32, o); o += 32
        sel = sb("sel", [P, 32], F32, o); o += 128
        qw = sb("qw", [P, KC], F32, o); o += 64
        vbias = sb("vbias", [P, KC], F32, o); o += 64
        negm = sb("negm", [P, 2, 16], F32, o); o += 128
        esum = sb("esum", [P, 2, 16], F32, o); o += 128
        lnl = sb("lnl", [P, 2, 16], F32, o); o += 128
        negc = sb("negc", [P, 2, 16], F32, o); o += 128
        bst = sb("bst", [P, 8, 6], F32, o); o += 192
        mv = sb("mv", [P, 8, 2], F32, o); o += 64
        rs = sb("rs", [P, 8], F32, o); o += 64
        cst = sb("cst", [P, 6], F32, o); o += 32
        cmv = sb("cmv", [P, 2], F32, o); o += 32
        crs = sb("crs", [P, 1], F32, o); o += 32
        fst = sb("fst", [P, 2, 2, 6], F32, o); o += 96
        fmv = sb("fmv", [P, 2, 2, 2], F32, o); o += 32
        frs = sb("frs", [P, 2, 2], F32, o); o += 32
        crow = sb("crow", [8, 2, QH], F32R, o); o += 2 * KB_
        assert o % 32 == 0
        arena = o
        o += 96 * KB_
        rest = o
        xin = sb("xin", [P, 8, D], F32, 0)
        raw = sb("raw", [P, 2, KC, D], F32, 16 * KB_)
        token_parts = [sb(f"tok{i}", [P, 2, KC, 512], F32R, arena + 16 * KB_ * i) for i in range(2)]
        w_at = {'wki': 2, 'wk': 3, 'wvi': 4, 'wv': 5, 'wq': 4}
        w_parts = {n: sb("p_" + n, [P, 2, KC, D], F32R, arena + 16 * KB_ * i) for n, i in w_at.items()}
        raw4 = sb("raw4", [P, 2, KC, 512], F32, 32 * KB_)
        sq4 = sb("sq4", [P, KC, 512], F32, rest)
        ind_in = sb("ind_in", [4, KEYS], F32, rest)
        ssum = sb("ssum", [P, 512], F32, rest + 8 * KB_)
        rt = sb("rt", [P, 2, 512], F32, rest + 10 * KB_)
        hl = sb("hl", [P, 2, 2, 512], F32R, rest + 14 * KB_)
        vbuf = sb("vbuf", [P, 2, D], F32, rest + 22 * KB_)
        ind = sb("ind", [4, KEYS], F32R, rest + 26 * KB_)
        d1 = sb("d1", [P, KC, HID], F32, arena)
        vring = sb("vring", [P, 2, CH, P], F32, arena + 32 * KB_)
        wo = sb("wo", [P, KC, D], F32, arena + 40 * KB_)
        wg = sb("wg", [P, KC, D], F32, arena + 48 * KB_)
        aggbc = sb("aggbc", [P, KC, D], F32, arena + 56 * KB_)
        d2 = sb("d2", [P, HID // P, D], F32, arena + 64 * KB_)
        prob = sb("prob", [P, NP, HPG * QH], F32, rest)
        o = rest + 8 * KB_
        chx = sb("chx", [32, D], F32, o)
        th = sb("th", [32, D], F32, o + 2 * KB_)
        hb = sb("hb", [P, D], F32, o + 4 * KB_)
        hT = sb("hT", [P, KC, P], F32, o + 6 * KB_)
        tT = sb("tT", [P, KC, 32], F32, o + 8 * KB_)
        x2e = sb("x2e", [P, 8 - XS, D], F32, arena)
        x2n = sb("x2n", [P, 2, D], F32, arena + 4 * KB_)
        xTt = sb("xTt", [P, 2, KC, P], F32, arena + 8 * KB_)
        zt = sb("zt", [P, 3, D], F32, arena + 12 * KB_)
        attT = sb("attT", [P, NG, QH], F32, rest + 17 * KB_)
        bcb1 = sb("bcb1", [P, D], F32, rest + 21 * KB_)
        x2s = sb("x2s", [P, XS, D], F32, rest + 23 * KB_)

        def residual(f):
            return x2s[:, f, :] if f < XS else x2e[:, f - XS, :]

        psum = ctx.enter_context(nc.psum_tensor("psum", [P, 8, 512], F32))
        score1 = psum[:, 0:4, :].rearrange("p (a b) n -> p a (b n)", a=2)
        score2 = psum[:, 4:6, :].rearrange("p b n -> p (b n)")

        kscr = nc.dram_tensor("kscr", (2, NB, D, KEYS), F32).ap()
        qscr = nc.dram_tensor("qscr", (2, 2, D, NB * QH), F32).ap()
        vscr = nc.dram_tensor("vscr", (NB, CH, P, D), F32).ap()

        def sem(name):
            return ctx.enter_context(nc.semaphore(name))

        const_loaded = sem("const_loaded")
        ind_placed = sem("ind_placed")
        ind_ready = sem("ind_ready")
        x_loaded = [sem(f"x_loaded{i}") for i in range(2)]
        raw_loaded = [sem(f"raw_loaded{i}") for i in range(2)]
        hi_done = sem("hi_done")
        lo_done = sem("lo_done")
        x_mean = sem("x_mean")
        x_rstd = sem("x_rstd")
        xn_done = sem("xn_done")
        job_done = sem("job_done")
        emptied_by = {'act': sem("emptied_by_act"), 'dve': sem("emptied_by_dve")}
        sumsq_added = sem("sumsq_added")
        rms_done = sem("rms_done")
        norm_done = sem("norm_done")
        hl_stored = [sem(f"hl_stored{i}") for i in range(2)]
        v_stored = [sem(f"v_stored{i}") for i in range(2)]
        pair_loaded = [sem(f"pair_loaded{i}") for i in range(PAIRS)]
        v_loaded = [sem(f"v_loaded{i}") for i in range(2)]
        s1_done = sem("s1_done")
        max_done = sem("max_done")
        exp1_done = sem("exp1_done")
        ln_done = sem("ln_done")
        negc_done = sem("negc_done")
        shift_loaded = [sem(f"shift_loaded{i}") for i in range(2)]
        s2_done = sem("s2_done")
        exp2_done = sem("exp2_done")
        pv_done = sem("pv_done")
        attn_done = sem("attn_done")
        act_order = sem("act_order")
        dve_order = sem("dve_order")
        pool_order = sem("pool_order")
        qw_ready = sem("qw_ready")
        ones_ready = sem("ones_ready")
        res_loaded = sem("res_loaded")
        res_ready = sem("res_ready")
        late_loaded = {n: sem("loaded_" + n) for n in ('wo', 'wg', 'agg', 'd1', 'd2', 'bc')}
        chx_zero = sem("chx_zero")
        row_loaded = sem("row_loaded")
        ch_stats = sem("ch_stats")
        ch_rstd = sem("ch_rstd")
        ch_norm = sem("ch_norm")
        gelu_in = sem("gelu_in")
        gelu_done = sem("gelu_done")
        tb_ready = sem("tb_ready")
        f_stats = sem("f_stats")
        f_rstd = sem("f_rstd")
        x2n_done = sem("x2n_done")
        z_ready = sem("z_ready")
        z_exp = sem("z_exp")
        z_clamped = sem("z_clamped")
        gate_done = sem("gate_done")
        mix_done = sem("mix_done")
        x2b_ready = sem("x2b_ready")
        out_ready = sem("out_ready")
        out_stored = sem("out_stored")

        pieces_before = [sum(len(pieces(t)) for t in range(n)) * KC for n in range(7)]

        f_stat_count = {e: n + 1 for n, e in enumerate(e for e in plan if e[0] in ('f_stat', 'f_stat2'))}

        def stores_of(tiles):
            return 16 * (4 * tiles // 2)

        n_const = 4 + 3 + 4 + 2
        i_split = {n: i for i, n in enumerate(SPLITS)}
        tok_of = {('k', 0, 0): 'c00', ('k', 0, 1): 'c01', ('k', 1, 0): 'c10', ('k', 1, 1): 'c11'}

        def last_job(test):
            return max(n for n, e in enumerate(jobs) if test(e))

        split_after = {
            'c00': last_job(lambda e: e[0] == 'proj' and e[1] == 0),
            'c01': last_job(lambda e: e[0] == 'proj' and e[1] == 1),
            'wvi': last_job(lambda e: e[0] == 'proj' and e[1] == 1),
            'c10': last_job(lambda e: e[0] in ('v', 'vimg') and e[1] == 0 and (e[0] == 'vimg' or e[2] < 4)),
            'c11': last_job(lambda e: e[0] == 'v' and e[1] == 0),
        }
        last_k = last_job(lambda e: e[0] == 'proj')
        last_v = last_job(lambda e: e[0] == 'v')

        block = ctx.enter_context(nc.Block())

        @block.sync
        def _(sp):
            x_t = T['x'].rearrange("b (q p) d -> p b q d", p=P)

            def load_raw(i):
                name = SPLITS[i]
                if name[0] == 'w':
                    src = T[name].rearrange("(k p) n -> p k n", p=P)
                else:
                    c0 = int(name[1]) * KEYS + int(name[2]) * 512
                    src = T['ctxT'].rearrange("(k p) n -> p k n", p=P)[:, :, c0:c0 + 512]
                sp.dma_start(raw[:, i % 2], src).then_inc(raw_loaded[i % 2], 16)

            for h in (1,):
                for b in range(NB):
                    sp.dma_start(xin[:, 4 * h + 2 * b:4 * h + 2 * b + 2, :], x_t[:, b, 2 * h:2 * h + 2, :]).then_inc(x_loaded[h], 16)
            load_raw(0)
            load_raw(1)
            for b in range(NB):
                sp.dma_start(xin[:, 2 * b:2 * b + 2, :], x_t[:, b, 0:2, :]).then_inc(x_loaded[0], 16)

            def split(i):
                if i + 2 < len(SPLITS):
                    sp.wait_ge(lo_done, i + 1)
                    load_raw(i + 2)

            def norm(tile):
                kind = TILES[tile]
                for oc in range(KC):
                    n = KC * tile + oc
                    if kind[0] == 'q':
                        dst = qscr[:, kind[1], oc * P:(oc + 1) * P, :]
                    else:
                        dst = kscr[:, kind[1], oc * P:(oc + 1) * P, 512 * kind[2]:512 * kind[2] + 512]
                    sp.wait_ge(norm_done, n + 1)
                    sp.dma_start(dst.rearrange("s p n -> p s n"), hl[:, n % 2].bitcast(F32)).then_inc(hl_stored[n % 2], 16)

            def vstore(b, c):
                i = CH * b + c
                n = job_at[('vimg', b)] if c == IMG_CHUNK else job_at[('v', b, c)]
                sp.wait_ge(emptied_by['act'], emptied(n)[1])
                sp.dma_start(vscr[b, c], vbuf[:, i % 2, :]).then_inc(v_stored[i % 2], 16)

            def load(u):
                h, b, g = unit(u)
                if u == 0:
                    for s in range(2):
                        sp.wait_ge(hl_stored[s], stores_of(4))
                    sp.wait_ge(ind_ready, 1)
                    sp.wait_ge(xn_done, 8)
                    sp.wait_ge(job_done, job_at[('xT', 0, 3)] + 1)
                    sp.wait_ge(lo_done, len(SPLITS))
                if u == 2:
                    for s in range(2):
                        sp.wait_ge(hl_stored[s], stores_of(6))
                for pp in range(2):
                    n = 2 * u + pp
                    slot = n % PAIRS
                    if n >= PAIRS:
                        sp.wait_ge(s2_done, 8 * ((n - PAIRS) // 2 + 1))
                    else:
                        for jj in range(2):
                            sp.dma_start(kst[96:100, slot, jj, :].bitcast(F32), ind[:, :].bitcast(F32)).then_inc(ind_placed, 16)
                    r0 = P * g + 64 * pp
                    for part, row in ((0, 0), (0, 32), (1, 64)):
                        src = kscr[part, b, r0:r0 + 64, :].rearrange("(j d) n -> d j n", d=HD)
                        sp.dma_start(kst[row:row + 32, slot].bitcast(F32), src).then_inc(pair_loaded[slot], 16)
                    for part, row in ((0, 0), (1, 32), (0, 64)):
                        src = qscr[part, h, r0:r0 + 64, b * QH:(b + 1) * QH].rearrange("(j d) n -> d j n", d=HD)
                        sp.dma_start(qst[row:row + 32, slot].bitcast(F32), src).then_inc(pair_loaded[slot], 16)

            def load_v(u):
                h, b, g = unit(u)
                if u == 0:
                    for s in range(2):
                        sp.wait_ge(v_stored[s], 16 * CH)
                    sp.wait_ge(job_done, last_k + 1)
                if u >= 2:
                    sp.wait_ge(pv_done, 8 * (u - 1))
                sp.dma_start(vring[:, u % 2], vscr[b, :, :, P * g:P * (g + 1)].rearrange("c p n -> p c n")).then_inc(v_loaded[u % 2], 16)

            def shift(u):
                sp.wait_ge(emptied_by['dve'], emptied(job_at[('shift', u)])[1])
                slot = pair_slot(u, 0)[0]
                for part in range(2):
                    row = 96 + 2 * part
                    sp.dma_start(qst[row:row + 2, slot:slot + 2].rearrange("s a b n -> s (a b) n").bitcast(F32),
                                 crow[:, part, :].bitcast(F32)).then_inc(shift_loaded[u % 2], 16)

            def ch_row():
                sp.wait_ge(emptied_by['dve'], emptied(job_at[('o', 1, 1)])[1])
                sp.wait_ge(chx_zero, 1)
                for b in range(NB):
                    sp.dma_start(chx[b:b + 1, :], x2s[P - 1:P, 2 * b + 1, :]).then_inc(row_loaded, 16)

            def f_out(f):
                h, b, _ = unit(NG * (f // 2))
                sp.wait_ge(out_ready, f + 1)
                sp.dma_start(out.rearrange("b (q p) d -> b q p d", p=P)[b, 2 * h + f % 2], residual(f))\
                  .then_inc(out_stored, 16)

            steps = {'split': split, 'norm': norm, 'vstore': vstore, 'load': load, 'load_v': load_v, 'shift': shift,
                     'ch_row': ch_row, 'f_out': f_out}
            for e in plan:
                if e[0] in steps:
                    steps[e[0]](*e[1:])
            sp.wait_ge(out_stored, 16 * 8)

        @block.tensor
        def _(pe):
            def open_bank(n):
                m = before_in_bank(bank_of[n], n)
                if m is not None:
                    eng, count = emptied(m)
                    pe.wait_ge(emptied_by[eng], count)
                return psum[:, bank_of[n], :]

            def xT(h, n):
                job = job_at[('xT', h, n)]
                ps = open_bank(job)
                if job == 0:
                    pe.wait_ge(const_loaded, 16 * n_const)
                pe.wait_ge(xn_done, 4 * (1 - h) + n + 1)
                for kc in range(KC):
                    mm = pe.transpose(ps[:, kc * P:(kc + 1) * P], xin[:, 4 * h + n, kc * P:(kc + 1) * P], ident[:, :])
                mm.then_inc(job_done, 1)

            def three_passes(ps, left, right):
                for kc in range(KC):
                    for a, b in ((0, 0), (0, 1), (1, 0)):
                        mm = pe.matmul(ps, left(a, kc), right(b, kc), start=(kc == 0 and a + b == 0), stop=(kc == KC - 1 and a == 1))
                return mm

            def proj(tile, oc, piece):
                kind = TILES[tile]
                w, c0, c1 = pieces(tile)[piece][:3]
                job = job_at[('proj', tile, oc, piece)]
                ps = open_bank(job)
                if oc == 0 and piece == 0:
                    if kind[0] == 'q':
                        pe.wait_ge(emptied_by['dve'], emptied(job_at[('xT', kind[1], 3)])[1])
                        pe.wait_ge(lo_done, i_split['wq'] + 1)
                    else:
                        pe.wait_ge(lo_done, max(i_split[tok_of[kind]], i_split['wk']) + 1)
                x = token_parts[1 - kind[1] if kind[0] == 'q' else kind[2]]
                wt = w_parts[w]
                three_passes(ps[:, 0:c1 - c0], lambda a, kc: wt[:, a, kc, oc * P:(oc + 1) * P],
                             lambda a, kc: x[:, a, kc, c0:c1]).then_inc(job_done, 1)

            def sumsq(tile):
                ps = open_bank(job_at[('sumsq', tile)])
                if tile == 0:
                    pe.wait_ge(ones_ready, 1)
                pe.wait_ge(sumsq_added, tile + 1)
                pe.matmul(ps, inv_d[:, :].to_broadcast([P, P]), ssum[:, :], start=True, stop=True).then_inc(job_done, 1)

            def v_job(job, b, c, w):
                ps = open_bank(job)
                pe.wait_ge(lo_done, i_split[w] + 1)
                pe.wait_ge(lo_done, i_split[f"c{b}{c // 4}"] + 1)
                x = token_parts[c // 4]
                wt = w_parts[w]
                t0 = (c % 4) * P
                three_passes(ps, lambda a, kc: x[:, a, kc, t0:t0 + P], lambda a, kc: wt[:, a, kc, :]).then_inc(job_done, 1)

            def v(b, c):
                v_job(job_at[('v', b, c)], b, c, 'wvi' if c < IMG_CHUNK else 'wv')

            def vimg(b):
                v_job(job_at[('vimg', b)], b, IMG_CHUNK, 'wvi')

            def bank_before_attention(bank):
                eng, count = emptied(before_in_bank(bank, n_first))
                pe.wait_ge(emptied_by[eng], count)

            def S1(t):
                u, s = t // 8, t % 8
                j, qt = s // 2, s % 2
                slot, jj, rnd = pair_slot(u, j)
                if s % 4 == 0:
                    pe.wait_ge(pair_loaded[slot], 96 * (rnd + 1))
                if t < 2:
                    bank_before_attention(2 * t)
                    bank_before_attention(2 * t + 1)
                else:
                    pe.wait_ge(exp1_done, t - 1)
                for half in range(2):
                    mm = pe.matmul(score1[:, t % 2, half * 512:(half + 1) * 512], qst[0:96, slot, jj, qt * P:(qt + 1) * P],
                                   kst[0:96, slot, jj, half * 512:(half + 1) * 512], start=True, stop=True)
                mm.then_inc(s1_done, 1)

            def S2(r):
                u, c = r // 8, r % 8
                if r == 0:
                    pe.wait_ge(ind_placed, 16 * 2 * PAIRS)
                    bank_before_attention(4)
                    bank_before_attention(5)
                else:
                    pe.wait_ge(exp2_done, r)
                if c == 0:
                    pe.wait_ge(shift_loaded[u % 2], 16 * 2 * (u // 2 + 1))
                for j in range(HPG):
                    slot, jj, _ = pair_slot(u, j)
                    mm = pe.matmul(score2[:, j * QH:(j + 1) * QH], kst[0:100, slot, jj, c * P:(c + 1) * P],
                                   qst[0:100, slot, jj, :], start=True, stop=True)
                mm.then_inc(s2_done, 1)

            def PV(r):
                u, c = r // 8, r % 8
                if c == 0:
                    pe.wait_ge(v_loaded[u % 2], 16 * (u // 2 + 1))
                    if u == 0:
                        bank_before_attention(PV_BANK)
                    else:
                        pe.wait_ge(attn_done, u)
                pe.wait_ge(exp2_done, r + 1)
                for j in range(HPG):
                    mm = pe.matmul(psum[32 * j:32 * j + 32, PV_BANK, 0:QH], vring[:, u % 2, c, 32 * j:32 * j + 32],
                                   prob[:, r % NP, j * QH:(j + 1) * QH], start=(c == 0), stop=(c == 7))
                mm.then_inc(pv_done, 1)

            def shift(u):
                ps = open_bank(job_at[('shift', u)])
                pe.wait_ge(negc_done, u + 1)
                for qt in range(2):
                    mm = pe.transpose(ps[0:8, qt * P:(qt + 1) * P], negc[:, u % 2, qt * 8:qt * 8 + 8], ident[:, :])
                mm.then_inc(job_done, 1)

            def o(k, n):
                ps = open_bank(job_at[('o', k, n)])
                pe.wait_ge(attn_done, NG * (k + 1))
                if k == 0:
                    pe.wait_ge(late_loaded['wo'], 16)
                for g in range(NG):
                    mm = pe.matmul(ps, attT[:, g, n * P:(n + 1) * P], wo[:, g, :], start=(g == 0), stop=(g == NG - 1))
                mm.then_inc(job_done, 1)

            def ch_turn(i):
                ps = open_bank(job_at[('ch_turn', i)])
                src = chx
                if i == 1 + K_STEPS:
                    pe.wait_ge(emptied_by['dve'], emptied(job_at[('ch_sum', K_STEPS - 1)])[1])
                    src = th
                else:
                    pe.wait_ge(ch_norm, i + 2)
                for kc in range(KC):
                    mm = pe.transpose(ps[:, kc * 32:(kc + 1) * 32], src[:, kc * P:(kc + 1) * P], ident[0:32, 0:32])
                mm.then_inc(job_done, 1)

            def thin(ps, w):
                for kc in range(KC):
                    mm = pe.matmul(ps[0:32, :], tT[:, kc, :], w[:, kc, :], start=(kc == 0), stop=(kc == KC - 1))
                mm.then_inc(job_done, 1)

            def ch_agg():
                ps = open_bank(job_at[('ch_agg',)])
                pe.wait_ge(late_loaded['agg'], 16)
                thin(ps, aggbc)

            def ch_d1(k, kc):
                ps = psum[:, SHARED_BANK, :]
                if kc == 0:
                    open_bank(job_at[('ch_d1', k, KC - 1)])
                    if k == 0:
                        pe.wait_ge(late_loaded['d1'], 64)
                for j in range(4):
                    mm = pe.matmul(ps[32 * j:32 * j + 32, :], tT[:, kc, :], d1[:, kc, 512 * j:512 * (j + 1)],
                                   start=(kc == 0), stop=(kc == KC - 1))
                if kc == KC - 1:
                    mm.then_inc(job_done, 1)

            def ch_hT(k):
                ps = open_bank(job_at[('ch_hT', k)])
                pe.wait_ge(gelu_done, k + 1)
                for m in range(4):
                    mm = pe.transpose(ps[:, m * P:(m + 1) * P], hb[:, m * P:(m + 1) * P], ident[:, :])
                mm.then_inc(job_done, 1)

            def ch_d2(k, j):
                ps = psum[:, SHARED_BANK, :]
                if j == 0:
                    open_bank(job_at[('ch_d2', k, KC - 1)])
                    if k == 0:
                        pe.wait_ge(late_loaded['d2'], 64)
                for m in range(4):
                    mm = pe.matmul(ps[32 * m:32 * m + 32, :], hT[:, m, 32 * j:32 * j + 32], d2[:, 4 * j + m, :],
                                   start=(j == 0), stop=(j == 3))
                if j == KC - 1:
                    mm.then_inc(job_done, 1)

            def ch_sum(k):
                ps = open_bank(job_at[('ch_sum', k)])
                pe.matmul(ps[0:32, :], sel[:, :], hb[:, :], start=True, stop=True).then_inc(job_done, 1)

            def ch_bc():
                ps = open_bank(job_at[('ch_bc',)])
                pe.wait_ge(late_loaded['bc'], 16)
                thin(ps, aggbc)

            def ch_spread(b):
                ps = open_bank(job_at[('ch_spread', b)])
                pe.wait_ge(emptied_by['dve'], emptied(job_at[('ch_bc',)])[1])
                pe.matmul(ps, ident[0:32, b:b + 1].to_broadcast([32, P]), chx[:, :], start=True, stop=True).then_inc(job_done, 1)

            def f_turn(f):
                ps = open_bank(job_at[('f_turn', f)])
                pe.wait_ge(x2n_done, f + 1)
                for kc in range(KC):
                    mm = pe.transpose(ps[:, kc * P:(kc + 1) * P], x2n[:, f % 2, kc * P:(kc + 1) * P], ident[:, :])
                mm.then_inc(job_done, 1)

            def f_gate(f, half):
                ps = psum[:, SHARED_BANK, :]
                if half == 0:
                    open_bank(job_at[('f_gate', f, 1)])
                    if f == 0:
                        pe.wait_ge(late_loaded['wg'], 16)
                for kc in (2 * half, 2 * half + 1):
                    mm = pe.matmul(ps, xTt[:, f % 2, kc, :], wg[:, kc, :], start=(kc == 0), stop=(kc == KC - 1))
                if half == 1:
                    mm.then_inc(job_done, 1)

            steps = {'xT': xT, 'proj': proj, 'sumsq': sumsq, 'v': v, 'vimg': vimg, 'S1': S1, 'S2': S2, 'PV': PV,
                     'shift': shift, 'o': o, 'ch_turn': ch_turn, 'ch_agg': ch_agg, 'ch_d1': ch_d1, 'ch_hT': ch_hT,
                     'ch_d2': ch_d2, 'ch_sum': ch_sum, 'ch_bc': ch_bc, 'ch_spread': ch_spread, 'f_turn': f_turn,
                     'f_gate': f_gate}
            for e in plan:
                if e[0] in steps:
                    steps[e[0]](*e[1:])

        @block.scalar
        def _(act):
            for dst, src in ((colp[:], T['cols']), (ident[:, :], T['ident']), (sel[:, :], T['sel'])):
                act.dma_start(dst, src).then_inc(const_loaded, 16)
            act.dma_start(ind_in[:, :], T['ind']).then_inc(const_loaded, 16)
            for i, n in enumerate(('d2_b', 'agg_b', 'bc_b')):
                act.dma_start(chrow[32 * i:32 * i + 32, :], T[n].partition_broadcast(32)).then_inc(const_loaded, 16)
            for j in range(4):
                act.dma_start(d1b[32 * j:32 * j + 32, :], T['d1_b'][512 * j:512 * (j + 1)].partition_broadcast(32)).then_inc(const_loaded, 16)
            act.dma_start(rows[:, 0:2, :], T['rows'][0:2].partition_broadcast(P)).then_inc(const_loaded, 16)
            act.dma_start(rows[:, 2:4, :], T['rows'][2:4].partition_broadcast(P)).then_inc(const_loaded, 16)
            links = [0]

            def link(ins):
                links[0] += 1
                ins.then_inc(act_order, 1)
                act.wait_ge(act_order, links[0])

            def rstd(dst, var, eps):
                link(act.activation(dst, var, ACT.Ln, bias=eps))
                return act.activation(dst, dst, ACT.Exp, scale=-0.5)

            def split(i):
                name = SPLITS[i]
                act.wait_ge(raw_loaded[i % 2], 16 * (i // 2 + 1))
                if name in split_after:
                    act.wait_ge(job_done, split_after[name] + 1)
                dst = w_parts[name] if name[0] == 'w' else token_parts[int(name[2])]
                act.activation(dst[:, 0], raw[:, i % 2], ACT.Copy).then_inc(hi_done, 1)

            def xstat(h):
                act.wait_ge(x_mean, 2 - h)
                rstd(rs[:, 4 * h:4 * h + 4], mv[:, 4 * h:4 * h + 4, 1], epsln[:, 0:1]).then_inc(x_rstd, 1)

            def proj(tile, oc, piece):
                _, c0, _, k0, k1, bias, _ = pieces(tile)[piece]
                job = job_at[('proj', tile, oc, piece)]
                if oc == 0 and piece == 0:
                    if tile >= 1:
                        act.wait_ge(sumsq_added, tile)
                    if tile == 0:
                        act.wait_ge(ind_ready, 1)
                if tile >= 2 and piece == 0:
                    act.wait_ge(norm_done, KC * (tile - 2) + oc + 1)
                act.wait_ge(job_done, job + 1)
                src = psum[:, bank_of[job], k0 - c0:k1 - c0]
                b = colp[:, bias, oc:oc + 1]
                act.activation(raw4[:, tile % 2, oc, k0:k1], src, ACT.Identity, bias=b)
                act.activation(sq4[:, oc, k0:k1], src, ACT.Square, bias=b).then_inc(emptied_by['act'], 1)

            def sumsq(tile):
                job = job_at[('sumsq', tile)]
                if tile >= 2:
                    act.wait_ge(norm_done, KC * (tile - 1))
                act.wait_ge(job_done, job + 1)
                r = rt[:, tile % 2, :]
                n = emptied(job)[1]
                act.activation(r, psum[:, bank_of[job], :], ACT.Ln, bias=epsf[:, 0:1]).then_inc(emptied_by['act'], 1)
                act.wait_ge(emptied_by['act'], n)
                act.activation(r, r, ACT.Exp, scale=-0.5).then_inc(rms_done, 1)

            def v(b, c):
                i = CH * b + c
                job = job_at[('v', b, c)]
                if i >= 2:
                    act.wait_ge(v_stored[i % 2], 16 * (i // 2))
                act.wait_ge(job_done, job + 1)
                act.copy(vbuf[:, i % 2, :], psum[:, bank_of[job], :]).then_inc(emptied_by['act'], 1)

            def vimg(b):
                job = job_at[('vimg', b)]
                act.wait_ge(emptied_by['act'], emptied(job_at[('v', b, IMG_CHUNK)])[1])
                act.wait_ge(job_done, job + 1)
                act.copy(vbuf[0:1, (CH * b + IMG_CHUNK) % 2, :], psum[0:1, bank_of[job], :]).then_inc(emptied_by['act'], 1)

            def exp1(t):
                u, s = t // 8, t % 8
                j, qt = s // 2, s % 2
                act.wait_ge(max_done, t + 1)
                for st, (k0, k1) in enumerate(((0, IMG), (IMG, KEYS))):
                    col = qt * 8 + st * 4 + j
                    s1 = score1[:, t % 2, k0:k1]
                    ins = act.activation(s1, s1, ACT.Exp, bias=negm[:, u % 2, col:col + 1], accum_out=esum[:, u % 2, col:col + 1])
                ins.then_inc(exp1_done, 1)

            def S1(t):
                if t >= 1:
                    exp1(t - 1)
                if t == 8 * NU - 1:
                    exp1(t)

            def S2(r):
                act.wait_ge(s2_done, r + 1)
                if r >= NP:
                    act.wait_ge(pv_done, r - NP + 1)
                act.activation(prob[:, r % NP, :], score2, ACT.Exp).then_inc(exp2_done, 1)

            def logs(u):
                act.wait_ge(exp1_done, 8 * (u + 1))
                act.activation(lnl[:, u % 2, :], esum[:, u % 2, :], ACT.Ln).then_inc(ln_done, 1)

            def ch_stat(i):
                act.wait_ge(ch_stats, i + 1)
                rstd(crs[0:32, :], cmv[0:32, 1:2], (epsln if i == 0 else epsf)[0:32, 0:1]).then_inc(ch_rstd, 1)

            def ch_gelu(k):
                act.wait_ge(gelu_in, k + 1)
                act.activation(hb[:, :], hb[:, :], ACT.Gelu).then_inc(gelu_done, 1)
                act.preload_act_table_set("natural_log_exp_and_others")

            def f_stat(f):
                act.wait_ge(f_stats, f_stat_count[('f_stat', f)])
                rstd(frs[:, f % 2, 0:1], fmv[:, f % 2, 0, 1:2], epsln[:, 0:1]).then_inc(f_rstd, 1)

            def f_turn(f):
                job = job_at[('f_turn', f)]
                act.wait_ge(job_done, job + 1)
                act.copy(xTt[:, f % 2].rearrange("p k n -> p (k n)"), psum[:, bank_of[job], :]).then_inc(emptied_by['act'], 1)

            def f_exp(f):
                z = zt[:, f % 3, :]
                act.wait_ge(z_ready, f + 1)
                act.activation(z, z, ACT.Exp, scale=-1.0).then_inc(z_exp, 1)

            def f_sig(f):
                z = zt[:, f % 3, :]
                act.wait_ge(z_clamped, f + 1)
                link(act.activation(z, z, ACT.Ln, bias=1.0))
                act.activation(z, z, ACT.Exp, scale=-1.0).then_inc(gate_done, 1)

            def f_stat2(f):
                act.wait_ge(f_stats, f_stat_count[('f_stat2', f)])
                rstd(frs[:, f % 2, 1:2], fmv[:, f % 2, 1, 1:2], epsf[:, 0:1]).then_inc(f_rstd, 1)

            act.preload_act_table_set("natural_log_exp_and_others")
            act.wait_ge(ones_ready, 1)
            act.wait_ge(const_loaded, 16 * n_const)
            steps = {'split': split, 'xstat': xstat, 'proj': proj, 'sumsq': sumsq, 'v': v, 'vimg': vimg, 'S1': S1,
                     'S2': S2, 'logs': logs, 'ch_stat': ch_stat, 'ch_gelu': ch_gelu, 'f_stat': f_stat, 'f_turn': f_turn,
                     'f_exp': f_exp, 'f_sig': f_sig, 'f_stat2': f_stat2}
            for e in plan:
                if e[0] in steps:
                    steps[e[0]](*e[1:])

        @block.vector
        def _(dve):
            links = [0]

            def link(ins):
                links[0] += 1
                ins.then_inc(dve_order, 1)
                dve.wait_ge(dve_order, links[0])

            dve.memset(epsln[:, :], EPS_LN)
            dve.memset(epsf[:, :], EPS)
            dve.memset(inv_d[:, :], 1.0 / D).then_inc(ones_ready, 1)
            dve.wait_ge(const_loaded, 16 * n_const)
            dve.tensor_copy(ind[:, :], ind_in[:, :]).then_inc(ind_ready, 1)
            dve.tensor_scalar(qw[:, :], colp[:, NQ, :], SCALE, None, ALU.mult)
            dve.tensor_tensor(vbias[:, :], colp[:, VB, :], colp[:, VIB, :], ALU.add).then_inc(qw_ready, 1)

            def stats(src, st, mean_var):
                link(dve.bn_stats(st, src))
                return dve.bn_aggr(mean_var, st)

            def split(i):
                name = SPLITS[i]
                dst = w_parts[name] if name[0] == 'w' else token_parts[int(name[2])]
                dve.wait_ge(hi_done, i + 1)
                dve.tensor_tensor(dst[:, 1], raw[:, i % 2], dst[:, 0], ALU.subtract).then_inc(lo_done, 1)

            def xstat(h):
                dve.wait_ge(x_loaded[h], 32)
                for n in range(4):
                    dve.bn_stats(bst[:, 4 * h + n, :], xin[:, 4 * h + n, :]).then_inc(dve_order, 1)
                links[0] += 4
                dve.wait_ge(dve_order, links[0])
                for n in range(4):
                    ins = dve.bn_aggr(mv[:, 4 * h + n, :], bst[:, 4 * h + n, :])
                ins.then_inc(x_mean, 1)

            def xnorm(h):
                dve.wait_ge(x_mean, 2 - h)
                dve.wait_ge(x_rstd, 2 - h)
                for n in range(4):
                    i = 4 * h + n
                    dve.tensor_scalar(xin[:, i, :], xin[:, i, :], mv[:, i, 0:1], rs[:, i:i + 1], ALU.subtract, ALU.mult)\
                       .then_inc(xn_done, 1)

            def xT(h, n):
                job = job_at[('xT', h, n)]
                dve.wait_ge(job_done, job + 1)
                src = psum[:, bank_of[job], :].rearrange("p (k n) -> p k n", k=KC)
                dst = token_parts[1 - h]
                cols = slice(n * P, (n + 1) * P)
                link(dve.tensor_copy(dst[:, 0, :, cols], src))
                dve.tensor_tensor(dst[:, 1, :, cols], src, dst[:, 0, :, cols], ALU.subtract).then_inc(emptied_by['dve'], 1)

            def norm(tile):
                kind = TILES[tile]
                dve.wait_ge(rms_done, tile + 1)
                for oc in range(KC):
                    n = KC * tile + oc
                    x = raw4[:, tile % 2, oc, :]
                    for _, _, _, k0, k1, _, w in pieces(tile):
                        wcol = qw[:, oc:oc + 1] if w is None else colp[:, w, oc:oc + 1]
                        ins = dve.scalar_tensor_tensor(x[:, k0:k1], x[:, k0:k1], wcol, rt[:, tile % 2, k0:k1], ALU.mult, ALU.mult)
                    link(ins)
                    if n >= 2:
                        dve.wait_ge(hl_stored[n % 2], 16 * (n // 2))
                    link(dve.tensor_copy(hl[:, n % 2, 0, :], x))
                    dve.tensor_tensor(hl[:, n % 2, 1, :], x, hl[:, n % 2, 0, :], ALU.subtract).then_inc(norm_done, 1)

            def S1(t):
                u, s = t // 8, t % 8
                j, qt = s // 2, s % 2
                dve.wait_ge(s1_done, t + 1)
                for st, (k0, k1) in enumerate(((0, IMG), (IMG, KEYS))):
                    col = qt * 8 + st * 4 + j
                    ins = dve.tensor_reduce(negm[:, u % 2, col:col + 1], score1[:, t % 2, k0:k1], AX.X, ALU.max, negate=True)
                ins.then_inc(max_done, 1)

            def attn(u):
                g = u % NG
                dve.wait_ge(pv_done, 8 * (u + 1))
                if u >= NG and g == 0:
                    dve.wait_ge(job_done, job_at[('o', u // NG - 1, 1)] + 1)
                dve.tensor_scalar(attT[:, g, :], psum[:, PV_BANK, 0:QH], vbias[:, g:g + 1], None, ALU.add).then_inc(attn_done, 1)

            def shift(u):
                job = job_at[('shift', u)]
                dve.wait_ge(ln_done, u + 1)
                dve.wait_ge(max_done, 8 * (u + 1))
                dve.tensor_tensor(negc[:, u % 2, :], negm[:, u % 2, :], lnl[:, u % 2, :], ALU.subtract).then_inc(negc_done, 1)
                if u >= 1:
                    dve.wait_ge(shift_loaded[(u - 1) % 2], 16 * 2 * ((u + 1) // 2))
                dve.wait_ge(job_done, job + 1)
                src = psum[0:8, bank_of[job], 0:QH]
                link(dve.tensor_copy(crow[:, 0, :], src))
                dve.tensor_tensor(crow[:, 1, :], src, crow[:, 0, :], ALU.subtract).then_inc(emptied_by['dve'], 1)

            def o(k, n):
                job = job_at[('o', k, n)]
                f = 2 * k + n
                dve.wait_ge(res_ready, f + 1)
                dve.wait_ge(job_done, job + 1)
                dve.tensor_tensor(residual(f), psum[:, bank_of[job], :], residual(f), ALU.add).then_inc(emptied_by['dve'], 1)

            def ch_stat(i):
                src = chx if i < 2 else th
                if i == 0:
                    dve.wait_ge(row_loaded, 32)
                elif i == 1:
                    dve.wait_ge(ch_norm, 1)
                else:
                    job = job_at[('ch_agg',)] if i == 2 else job_at[('ch_sum', i - 3)]
                    dve.wait_ge(emptied_by['dve'], emptied(job)[1])
                stats(src[:, :], cst[0:32, :], cmv[0:32, :]).then_inc(ch_stats, 1)

            def ch_ln(i):
                src = chx if i < 2 else th
                dve.wait_ge(ch_stats, i + 1)
                dve.wait_ge(ch_rstd, i + 1)
                dve.tensor_scalar(chx[:, :], src[:, :], cmv[0:32, 0:1], crs[0:32, 0:1], ALU.subtract, ALU.mult).then_inc(ch_norm, 1)

            def ch_turn(i):
                job = job_at[('ch_turn', i)]
                dve.wait_ge(job_done, job + 1)
                for kc in range(KC):
                    src = psum[:, bank_of[job], kc * 32:(kc + 1) * 32]
                    if i == 1 + K_STEPS:
                        ins = dve.tensor_copy(tT[:, kc, :], src)
                    else:
                        ga, be = (ING, INB) if i == 0 else (PNG, PNB)
                        ins = dve.tensor_scalar(tT[:, kc, :], src, colp[:, ga, kc:kc + 1], colp[:, be, kc:kc + 1], ALU.mult, ALU.add)
                ins.then_inc(emptied_by['dve'], 1)

            def ch_agg():
                job = job_at[('ch_agg',)]
                dve.wait_ge(job_done, job + 1)
                dve.tensor_tensor(th[:, :], psum[0:32, bank_of[job], :], chrow[32:64, :], ALU.add).then_inc(emptied_by['dve'], 1)

            def ch_d1(k, kc):
                if kc < KC - 1:
                    return
                job = job_at[('ch_d1', k, KC - 1)]
                dve.wait_ge(job_done, job + 1)
                dve.tensor_tensor(hb[:, :], psum[:, bank_of[job], :], d1b[:, :], ALU.add).then_inc(gelu_in, 1)
                dve.wait_ge(gelu_in, k + 1)
                dve.engine_nop().then_inc(emptied_by['dve'], 1)

            def ch_hT(k):
                job = job_at[('ch_hT', k)]
                dve.wait_ge(job_done, job + 1)
                dve.tensor_copy(hT[:].rearrange("p k n -> p (k n)"), psum[:, bank_of[job], :]).then_inc(emptied_by['dve'], 1)

            def ch_d2(k, j):
                if j < KC - 1:
                    return
                job = job_at[('ch_d2', k, KC - 1)]
                dve.wait_ge(job_done, job + 1)
                dve.tensor_copy(hb[:, :], psum[:, bank_of[job], :]).then_inc(emptied_by['dve'], 1)

            def ch_sum(k):
                job = job_at[('ch_sum', k)]
                dve.wait_ge(tb_ready, k + 1)
                dve.wait_ge(job_done, job + 1)
                dve.tensor_tensor(th[:, :], psum[0:32, bank_of[job], :], th[:, :], ALU.add).then_inc(emptied_by['dve'], 1)

            def ch_bc():
                job = job_at[('ch_bc',)]
                dve.wait_ge(job_done, job + 1)
                dve.tensor_tensor(chx[:, :], psum[0:32, bank_of[job], :], chrow[64:96, :], ALU.add).then_inc(emptied_by['dve'], 1)

            def ch_spread(b):
                job = job_at[('ch_spread', b)]
                dve.wait_ge(job_done, job + 1)
                dve.tensor_copy((bcb0, bcb1)[b][:, :], psum[:, bank_of[job], :]).then_inc(emptied_by['dve'], 1)

            def f_stat(f):
                dve.wait_ge(emptied_by['dve'], emptied(job_at[('o', f // 2, f % 2)])[1])
                stats(residual(f), fst[:, f % 2, 0, :], fmv[:, f % 2, 0, :]).then_inc(f_stats, 1)

            def f_norm(f):
                if f >= 2:
                    dve.wait_ge(mix_done, f - 1)
                dve.wait_ge(f_stats, f_stat_count[('f_stat', f)])
                dve.wait_ge(f_rstd, f_stat_count[('f_stat', f)])
                dve.tensor_scalar(x2n[:, f % 2, :], residual(f), fmv[:, f % 2, 0, 0:1], frs[:, f % 2, 0:1], ALU.subtract, ALU.mult)\
                   .then_inc(x2n_done, 1)

            def f_gate(f, half):
                if half == 0:
                    return
                job = job_at[('f_gate', f, 1)]
                if f >= 3:
                    dve.wait_ge(out_ready, f - 2)
                dve.wait_ge(job_done, job + 1)
                dve.tensor_tensor(zt[:, f % 3, :], psum[:, bank_of[job], :], rows[:, R_GATE, :], ALU.add).then_inc(z_ready, 1)
                dve.wait_ge(z_ready, f + 1)
                dve.engine_nop().then_inc(emptied_by['dve'], 1)

            def f_stat2(f):
                dve.wait_ge(mix_done, f + 1)
                stats(zt[:, f % 3, :], fst[:, f % 2, 1, :], fmv[:, f % 2, 1, :]).then_inc(f_stats, 1)

            def f_out(f):
                z = zt[:, f % 3, :]
                dve.wait_ge(f_stats, f_stat_count[('f_stat2', f)])
                dve.wait_ge(f_rstd, f_stat_count[('f_stat2', f)])
                dve.wait_ge(x2b_ready, f + 1)
                link(dve.tensor_scalar(z, z, fmv[:, f % 2, 1, 0:1], frs[:, f % 2, 1:2], ALU.subtract, ALU.mult))
                link(dve.tensor_tensor(z, z, rows[:, R_OG, :], ALU.mult))
                dve.tensor_tensor(residual(f), z, residual(f), ALU.add).then_inc(out_ready, 1)

            steps = {'split': split, 'xstat': xstat, 'xnorm': xnorm, 'xT': xT, 'norm': norm, 'S1': S1, 'attn': attn,
                     'shift': shift, 'o': o, 'ch_stat': ch_stat, 'ch_ln': ch_ln, 'ch_turn': ch_turn, 'ch_agg': ch_agg,
                     'ch_d1': ch_d1, 'ch_hT': ch_hT, 'ch_d2': ch_d2, 'ch_sum': ch_sum, 'ch_bc': ch_bc,
                     'ch_spread': ch_spread, 'f_stat': f_stat, 'f_norm': f_norm, 'f_gate': f_gate,
                     'f_stat2': f_stat2, 'f_out': f_out}
            for e in plan:
                if e[0] in steps:
                    steps[e[0]](*e[1:])

        @block.gpsimd
        def _(pool):
            links = [0]

            def link(ins):
                links[0] += 1
                ins.then_inc(pool_order, 1)
                pool.wait_ge(pool_order, links[0])

            def sumsq(tile):
                pool.wait_ge(emptied_by['act'], emptied(job_at[('proj', tile, KC - 1, len(pieces(tile)) - 1)])[1])
                if tile >= 1:
                    pool.wait_ge(job_done, job_at[('sumsq', tile - 1)] + 1)
                link(pool.tensor_tensor(ssum[:, :], sq4[:, 0, :], sq4[:, 1, :], ALU.add))
                link(pool.tensor_tensor(ssum[:, :], ssum[:, :], sq4[:, 2, :], ALU.add))
                pool.tensor_tensor(ssum[:, :], ssum[:, :], sq4[:, 3, :], ALU.add).then_inc(sumsq_added, 1)

            def load_res(f):
                h, b, _ = unit(NG * (f // 2))
                pool.dma_start(residual(f), T['x'][b, (2 * h + f % 2) * P:(2 * h + f % 2 + 1) * P, :]).then_inc(res_loaded, 16)

            def add_o_bias(f):
                pool.tensor_tensor(residual(f), residual(f), rows[:, R_O, :], ALU.add).then_inc(res_ready, 1)

            def res2():
                pool.wait_ge(job_done, job_at[('ch_d1', K_STEPS - 1, KC - 1)] + 1)
                for f in range(XS, 8):
                    load_res(f)
                pool.wait_ge(res_loaded, 16 * 8)
                for f in range(XS, 8):
                    add_o_bias(f)

            def phase2():
                pool.wait_ge(job_done, last_v + 1)
                for s in range(2):
                    pool.wait_ge(hl_stored[s], stores_of(6))
                    pool.wait_ge(v_stored[s], 16 * CH)
                pool.wait_ge(ind_placed, 16 * 2 * PAIRS)
                for f in range(XS):
                    load_res(f)
                pool.dma_start(wo[:], T['wo'].rearrange("(k p) n -> p k n", p=P)).then_inc(late_loaded['wo'], 16)

            def late(i):
                if i == 0:
                    pool.wait_ge(res_loaded, 16 * XS)
                    for f in range(XS):
                        add_o_bias(f)
                elif i == 1:
                    pool.dma_start(aggbc[:], T['agg'].rearrange("(k p) n -> p k n", p=P)).then_inc(late_loaded['agg'], 16)
                elif i == 2:
                    pool.dma_start(wg[:], T['wg'].rearrange("(k p) n -> p k n", p=P)).then_inc(late_loaded['wg'], 16)
                elif i < 7:
                    kc = i - 3
                    pool.dma_start(d1[:, kc, :], T['d1'][kc * P:(kc + 1) * P, :]).then_inc(late_loaded['d1'], 16)
                elif i < 11:
                    c = 4 * (i - 7)
                    pool.dma_start(d2[:, c:c + 4, :], T['d2'][c * P:(c + 4) * P, :].rearrange("(k p) n -> p k n", p=P))\
                        .then_inc(late_loaded['d2'], 16)
                else:
                    pool.wait_ge(max_done, 24)
                    pool.memset(chx[:, :], 0.0).then_inc(chx_zero, 1)

            def ch_d1(k, kc):
                if kc > 0:
                    return
                pool.wait_ge(ch_norm, 3 + k)
                pool.tensor_tensor(th[:, :], th[:, :], chrow[0:32, :], ALU.add).then_inc(tb_ready, 1)

            def ch_d2(k, j):
                if k == 0 and j == 0:
                    pool.dma_start(aggbc[:], T['bc'].rearrange("(k p) n -> p k n", p=P)).then_inc(late_loaded['bc'], 16)

            def f_norm(f):
                pool.wait_ge(x2n_done, f + 1)
                pool.tensor_tensor(residual(f), residual(f), rows[:, R_OB, :], ALU.add).then_inc(x2b_ready, 1)

            def f_exp(f):
                z = zt[:, f % 3, :]
                pool.wait_ge(z_exp, f + 1)
                pool.tensor_scalar(z, z, 1e18, 0.0, ALU.min, ALU.max).then_inc(z_clamped, 1)

            def f_sig(f):
                h, b, _ = unit(NG * (f // 2))
                z = zt[:, f % 3, :]
                pool.wait_ge(gate_done, f + 1)
                if f < 2:
                    pool.wait_ge(emptied_by['dve'], emptied(job_at[('ch_spread', 1)])[1])
                link(pool.tensor_tensor(z, z, (bcb0, bcb1)[b][:, :], ALU.mult))
                pool.tensor_tensor(z, z, x2n[:, f % 2, :], ALU.add).then_inc(mix_done, 1)

            steps = {'sumsq': sumsq, 'phase2': phase2, 'late': late, 'res2': res2, 'ch_d1': ch_d1, 'ch_d2': ch_d2, 'f_norm': f_norm,
                     'f_exp': f_exp, 'f_sig': f_sig}
            for e in plan:
                if e[0] in steps:
                    steps[e[0]](*e[1:])


def kernel(**inputs):
    import concourse.bacc as bacc
    from concourse.bass_utils import run_bass_kernel_spmd

    get = lambda n: np.asarray(inputs[n])
    eye = np.eye(P, dtype=np.float32)
    ind = np.zeros((4, KEYS), np.float32)
    ind[0::2, :IMG] = 1
    ind[1::2, IMG:] = 1
    host = {
        'x': get('x'),
        'ctxT': get('ctx_2048').reshape(NB * KEYS, D).T,
        'wq': get('L0_xattn_q_w').T, 'wk': get('L0_xattn_k_w').T, 'wki': get('L0_xattn_k_img_w').T,
        'wv': get('L0_xattn_v_w').T, 'wvi': get('L0_xattn_v_img_w').T, 'wo': get('L0_xattn_o_w').T,
        'wg': get('L0_ffn_gate_w'), 'agg': get('L0_ffn_agg_w'), 'bc': get('L0_ffn_bc_w'),
        'd1': get('L0_ffn_d1_w'), 'd2': get('L0_ffn_d2_w'),
        'cols': np.stack([get(n).reshape(KC, P).T for n in COLS], axis=1),
        'rows': np.stack([get(n) for n in ROWS]),
        'agg_b': get('L0_ffn_agg_b'), 'd2_b': get('L0_ffn_d2_b'), 'bc_b': get('L0_ffn_bc_b'),
        'd1_b': get('L0_ffn_d1_b'),
        'ident': eye, 'ind': ind, 'sel': np.tile(eye[:32, :32], (4, 1)),
    }
    nc = bacc.Bacc("TRN2", target_bir_lowering=False, num_devices=1)
    arrays = {n: np.ascontiguousarray(a) for n, a in host.items()}
    T = {n: nc.dram_tensor(n, a.shape, F32, kind="ExternalInput").ap() for n, a in arrays.items()}
    out = nc.dram_tensor("out", (NB, TOK, D), F32, kind="ExternalOutput").ap()
    build(nc, T, out)
    r = run_bass_kernel_spmd(nc, [arrays], core_ids=[0])
    return r.results[0]["out"]
```

```python
from contextlib import ExitStack

import numpy as np

import concourse.bass as bass
from concourse import mybir

F32 = mybir.dt.float32
F32R = mybir.dt.float32r
ALU = mybir.AluOpType
ACT = mybir.ActivationFunctionType
AX = mybir.AxisListType

P = 128
D = 512
KC = D // P
NB = 2
TOK = 512
KEYS = 1024
IMG = 257
IMG_CHUNK = IMG // P
NH = 16
HD = D // NH
HPG = P // HD
NG = NH // HPG
QH = TOK // 2
NU = 2 * NB * NG
CH = KEYS // P
PAIRS = 6
NP = 4
ORDER = (3, 4, 5, 6, 7, 2, 0, 1)
N_ADDED = 5
NX = 4
XS = 6
F_EVERY = 3
LEAD = 4
HID = 2048
K_STEPS = 4
CHUNKS = 2
EPS_LN = 1e-5
EPS = 1e-6
SCALE = 1.0 / float(np.sqrt(np.float32(HD)))

COLS = ['L0_xattn_q_b', 'L0_xattn_k_b', 'L0_xattn_k_img_b', 'L0_xattn_norm_q_w', 'L0_xattn_norm_k_w',
        'L0_xattn_norm_k_img_w', 'L0_xattn_v_b', 'L0_xattn_v_img_b', 'L0_ffn_in_gamma', 'L0_ffn_in_beta',
        'L0_ffn_pn_gamma', 'L0_ffn_pn_beta']
QB, KB, KIB, NQ, NK, NKI, VB, VIB, ING, INB, PNG, PNB = range(len(COLS))
ROWS = ['L0_xattn_o_b', 'L0_ffn_gate_b', 'L0_ffn_out_gamma', 'L0_ffn_out_beta']
R_O, R_GATE, R_OG, R_OB = range(4)


def make_plan():
    plan = []
    add = lambda *e: plan.append(e)

    def proj(tile, ocs=range(KC)):
        kind = TILES[tile]
        for oc in ocs:
            for piece in range(2 if kind[0] == 'k' and kind[2] == 0 else 1):
                add('proj', tile, oc, piece)

    def v(b, chunks):
        for c in chunks:
            if c == IMG_CHUNK:
                add('vimg', b)
                add('vstore', b, c)
            add('v', b, c)
            add('vstore', b, c if c < IMG_CHUNK else c + 1)

    add('xstat', 1)
    add('xnorm', 1)
    for n in range(4):
        add('xT', 1, n)
    add('split', 0)
    add('consts')
    proj(0, (0, 1))
    add('xstat', 0)
    add('xnorm', 0)
    for n in range(4):
        add('xT', 0, n)
    proj(0, (2, 3))
    add('split', 1)
    add('split', 2)
    proj(1, (0, 1))
    add('sumsq', 0)
    add('split', 3)
    for tile, before in ((0, None), (1, 4), (2, None)):
        if before:
            add('split', before)
        proj(tile + 1, (2,))
        add('norm', tile, 0)
        if tile == 1:
            add('split', 5)
        proj(tile + 1, (3,))
        add('norm', tile, 1)
        if tile == 1:
            add('split', 6)
        if tile < 2:
            proj(tile + 2, (0,))
            add('norm', tile, 2)
            proj(tile + 2, (1,))
            add('norm', tile, 3)
            add('sumsq', tile + 1)
        else:
            v(0, (0,))
            add('norm', 2, 2)
            v(0, (1,))
            add('norm', 2, 3)
            add('sumsq', 3)
    for c in range(2, 6):
        v(0, (c,))
        if c == 4:
            add('split', 7)
        add('norm', 3, c - 2)
    v(0, (6, 7))
    add('split', 8)
    add('load', 0)
    add('load', 1)
    proj(4)
    proj(5, (0, 1))
    add('sumsq', 4)
    proj(5, (2,))
    add('norm', 4, 0)
    proj(5, (3,))
    add('norm', 4, 1)
    add('load_v', 0)
    add('load_v', 1)
    v(1, (0,))
    add('norm', 4, 2)
    for c in range(1, CH):
        v(1, (c,))
        if c == 1:
            add('norm', 4, 3)
            add('sumsq', 5)
        if c >= 3:
            add('S1', 2 * c - 6)
            if 3 <= c < 7:
                add('norm', 5, c - 3)
            add('S1', 2 * c - 5)
            if c == 6:
                add('maxes', 0)
    add('shift', 0)
    add('load', 2)
    add('phase2')
    ahead = 8 + LEAD
    extra, post = {}, {}

    def at(step, *e):
        extra.setdefault(step, []).append(e)
        if e[0] == 'ch_stat':
            post.setdefault(step, []).append(('ch_rstd', e[1]))

    def closed(s):
        while any((s + n + ahead) % 8 == 1 for n in range(1, KC // CHUNKS)):
            s += 1
        return s

    s = 8 * 8 + 5
    at(s, 'ch_row')
    at(s + 2, 'ch_stat', 0)
    at(s + 3, 'ch_ln', 0)
    at(s + 3, 'ch_stat', 1)
    at(s + 4, 'ch_ln', 1)
    at(s + 5, 'ch_turn', 0)
    at(s + 6, 'ch_agg')
    at(s + 6, 'ch_stat', 2)
    s += 7
    for k in range(K_STEPS):
        at(s, 'ch_ln', 2 + k)
        at(s + 1, 'ch_turn', 1 + k)
        s = closed(s + 2)
        for kc in range(KC):
            at(s + kc // CHUNKS, 'ch_d1', k, kc)
        s += KC // CHUNKS
        at(s, 'ch_gelu', k)
        at(s + 1, 'ch_hT', k)
        s = closed(s + 2)
        for m in range(KC):
            at(s + m // CHUNKS, 'ch_d2', k, m)
        s += KC // CHUNKS
        at(s, 'ch_sum', k)
        if k < K_STEPS - 1:
            at(s, 'ch_stat', 3 + k)
        s += 1
    at(s, 'ch_turn', 1 + K_STEPS)
    at(s + 1, 'ch_bc')
    at(s + 2, 'ch_spread', 0)
    at(s + 2, 'ch_spread', 1)
    s += 3
    at(s, 'res2')
    for f in range(8):
        if f >= 6:
            s = max(s, 8 * NU + 2)
        while (s + 4 + ahead) % 8 == 1 and s + 4 < 8 * NU:
            s += 1
        if f in (0, XS):
            at(s, 'f_terms', f // XS)
        for n, e in ((1, ('f_norm', f)), (2, ('f_turn', f)), (3, ('f_gate', f, 0)),
                     (4, ('f_gate', f, 1)),
                     (5, ('f_exp', f)), (6, ('f_sig', f)), (8, ('f_stat2', f)), (9, ('f_out', f))):
            older = extra.setdefault(s + n, [])
            older.insert(1 if e == ('f_gate', f, 1) and older[:1] == [('f_gate', f, 0)] else 0, e)
        s += F_EVERY
    cut = {s for s, es in extra.items() for e in es if e[0] in ('ch_d1', 'ch_d2', 'f_gate') and e[2] > 0
           and not any(x[:2] == e[:2] and x[2] == 0 for x in es)}
    for k in range(4):
        s = 8 * NG * (k + 1) + 2
        for n in range(2):
            while s in cut:
                s += 1
            extra.setdefault(s, []).insert(n if k == 3 else 0, ('o', k, n))
            s += 1 if k < 3 else 0
    for t in range(10, ahead):
        add('S1', t)
    last = max(max(extra), 8 * NU + 1)
    for r in range(last + 1):
        if r < 8 * NU:
            add('S2', r)
            if r % 8 == 0 and r > 0 and r // 8 + 2 < NU:
                add('load', r // 8 + 2)
            if r % 8 == 1 and r // 8 + 1 < NU and r > 8:
                add('load_v', r // 8 + 1)
        if 1 <= r <= 8 * NU:
            add('PV', r - 1)
            if r % 8 == 0:
                add('attn', r // 8 - 1)
        if r % 8 == 1 and 8 < r <= 8 * NU + 1:
            add('weigh', r // 8 - 1)
        t = r + ahead
        if t % 8 == 0 and t // 8 <= NU:
            add('maxes', t // 8 - 1)
        if r == 2:
            add('late', r)
        elif r % 8 == 7 and r // 8 < XS:
            add('bias', r // 8)
        elif r % 8 == 5 and r < 64:
            add('late', 3 + r // 8)
        for e in extra.get(r, []):
            plan.append(e)
        if t < 8 * NU:
            add('S1', t)
        if t % 8 == 0 and t <= 8 * NU:
            add('shift', t // 8 - 1)
        plan += post.get(r, [])
    return plan


TILES = [('q', 1), ('q', 0), ('k', 0, 0), ('k', 0, 1), ('k', 1, 0), ('k', 1, 1)]
SPLITS = ['wq', 'wki', 'wk', 'c00', 'c01', 'wvi', 'wv', 'c10', 'c11']
JOBS = {'xT': 'dve', 'proj': 'act', 'sumsq': 'act', 'v': 'act', 'vimg': 'act', 'shift': 'dve', 'o': 'dve',
        'ch_turn': 'dve', 'ch_agg': 'dve', 'ch_d1': 'dve', 'ch_hT': 'dve', 'ch_d2': 'dve', 'ch_sum': 'dve',
        'ch_bc': 'dve', 'ch_spread': 'dve', 'f_turn': 'act', 'f_gate': 'dve'}
PV_BANK = 3
SUM_BANK = 6
SHARED_BANK = 7


def build(nc, T, out):
    plan = make_plan()
    jobs = [e for e in plan if e[0] in JOBS and not (e[0] in ('ch_d1', 'ch_d2') and e[2] < KC - 1)
            and not (e[0] == 'f_gate' and e[2] == 0)]
    for n, e in enumerate(plan):
        if e[0] in ('ch_d1', 'ch_d2', 'f_gate') and e[2] == 0:
            end = plan.index((e[0], e[1], 1 if e[0] == 'f_gate' else KC - 1))
            within = [x for x in plan[n:end] if x[0] in JOBS and x[:2] != e[:2]]
            assert not within, within
    job_at = {e: n for n, e in enumerate(jobs)}
    n_v1, last_v = (job_at[e] for e in (('v', 1, 0), ('v', 1, CH - 1)))
    bank_of = [n % 8 if n < n_v1 else SHARED_BANK if n > last_v or e[0] == 'shift' else 3 + (n - n_v1) % 4
               for n, e in enumerate(jobs)]
    in_plan = {e: n for n, e in enumerate(plan)}
    n_late = next(n for n, e in enumerate(jobs) if in_plan[e] > in_plan[('S1', 8 * NU - 1)] and e[0].startswith('f_'))
    for n in range(n_late, len(jobs)):
        bank_of[n] = (SHARED_BANK, 0, 1, 2)[(n - n_late) % 4]

    def emptied(n):
        eng = JOBS[jobs[n][0]]
        return eng, sum(JOBS[e[0]] == eng for e in jobs[:n + 1])

    def before_in_bank(bank, n):
        return max((m for m in range(n) if bank_of[m] == bank), default=None)

    def pieces(tile):
        kind = TILES[tile]
        if kind[0] == 'q':
            return [('wq', 0, 512, 0, 512, QB, None)]
        if kind[2] == 1:
            return [('wk', 0, 512, 0, 512, KB, NK)]
        return [('wki', 0, IMG + 1, 0, IMG, KIB, NKI), ('wk', IMG - 1, 512, IMG, 512, KB, NK)]

    def unit(u):
        k = u // NG
        return 1 - k // NB, k % NB, u % NG

    def pair_slot(u, j):
        n = 2 * u + j // 2
        return n % PAIRS, j % 2, n // PAIRS

    ctx = ExitStack()
    with ctx:
        base = (nc.sbuf_base + 63) // 64 * 64
        KB_ = 1024

        def sb(name, shape, dt, off):
            return nc.alloc_sbuf_tensor_at(name, shape, dt, offset=base + int(off))

        kst = sb("kst", [P, PAIRS, 2, KEYS], F32R, 0)
        qst = sb("qst", [P, PAIRS, 2, QH], F32R, 48 * KB_)
        o = 60 * KB_
        colp = sb("colp", [P, len(COLS), KC], F32, o); o += 256
        rows = sb("rows", [P, 4, D], F32, o); o += 8 * KB_
        chrow = sb("chrow", [P, D], F32, o); o += 2 * KB_
        d1b = sb("d1b", [P, D], F32, o)
        bcb0 = sb("bcb0", [P, D], F32, o); o += 2 * KB_
        ident = sb("ident", [P, P], F32, o); o += 512
        inv_d = sb("inv_d", [P, 1], F32, o); o += 32
        epsln = sb("epsln", [P, 1], F32, o); o += 32
        epsf = sb("epsf", [P, 1], F32, o); o += 32
        sel = sb("sel", [P, 32], F32, o); o += 128
        qw = sb("qw", [P, KC], F32, o); o += 64
        vbias = sb("vbias", [P, KC], F32, o); o += 64
        negm = sb("negm", [P, 2, 16], F32, o); o += 128
        negt = sb("negt", [P, 2, 2, 2, HPG], F32, o); o += 128
        ones = sb("ones", [P, 3, HD], F32, o); o += 384
        mask = sb("mask", [P, 2], F32, o); o += 32
        bst = sb("bst", [P, 8, 6], F32, o); o += 192
        mv = sb("mv", [P, 8, 2], F32, o); o += 64
        rs = sb("rs", [P, 8], F32, o); o += 64
        cst = sb("cst", [P, 6], F32, o); o += 32
        cmv = sb("cmv", [P, 2], F32, o); o += 32
        crs = sb("crs", [P, 1], F32, o); o += 32
        fst = sb("fst", [P, 2, 6], F32, o); o += 64
        fmv = sb("fmv", [P, 2, 2], F32, o); o += 32
        frs = sb("frs", [P, 2], F32, o); o += 32
        xterms = sb("xterms", [P, 2, 8], F32, o); o += 64
        crow = sb("crow", [8, 2, QH], F32R, o); o += 2 * KB_
        assert o % 32 == 0
        arena = o
        o += 97 * KB_
        rest = o
        xin = sb("xin", [P, 8, D], F32, 0)
        raw = sb("raw", [P, 2, KC, D], F32, 16 * KB_)
        token_parts = [sb(f"tok{i}", [P, 2, KC, 512], F32R, arena + 16 * KB_ * i) for i in range(2)]
        w_at = {'wki': 2, 'wk': 3, 'wvi': 4, 'wv': 5, 'wq': 4}
        w_parts = {n: sb("p_" + n, [P, 2, KC, D], F32R, arena + 16 * KB_ * i) for n, i in w_at.items()}
        raw4 = sb("raw4", [P, 2, KC, 512], F32, 32 * KB_)
        sq4 = sb("sq4", [P, KC, 512], F32, rest)
        ind_in = sb("ind_in", [4, KEYS], F32, rest)
        ssum = sb("ssum", [P, 512], F32, rest + 8 * KB_)
        rt = sb("rt", [P, 2, 512], F32, rest + 10 * KB_)
        hl = sb("hl", [P, 2, 2, 512], F32R, rest + 14 * KB_)
        vbuf = sb("vbuf", [P, 4, D], F32, rest + 22 * KB_)
        ind = sb("ind", [4, KEYS], F32R, rest + 30 * KB_)
        d1 = sb("d1", [P, KC, HID], F32, arena)
        vring = sb("vring", [P, 2, CH + 1, P], F32, arena + 32 * KB_)
        pvc = sb("pvc", [P, 2, QH], F32, arena + 41 * KB_)
        rsum = sb("rsum", [P, 2, QH], F32, arena + 43 * KB_)
        prob = sb("prob", [P, NP, HPG * QH], F32, arena + 45 * KB_)
        added = sb("added", [P, HPG * QH], F32, arena + 61 * KB_)
        d2 = sb("d2", [P, HID // P, D], F32, arena + 65 * KB_)
        wbuf = sb("wbuf", [P, KC, D], F32, rest)
        o = rest + 8 * KB_
        chx = sb("chx", [32, D], F32, o)
        th = sb("th", [32, D], F32, o + 2 * KB_)
        hb = sb("hb", [P, D], F32, o + 4 * KB_)
        hT = sb("hT", [P, KC, P], F32, o + 6 * KB_)
        tT = sb("tT", [P, KC, 32], F32, o + 8 * KB_)
        x2e = sb("x2e", [P, 8 - XS, D], F32, arena)
        x2n = sb("x2n", [P, NX, D], F32, arena + 4 * KB_)
        wg = sb("wg", [P, KC, D], F32, arena + 65 * KB_)
        xTt = sb("xTt", [P, 2, KC, P], F32, arena + 12 * KB_)
        zt = sb("zt", [P, NX, D], F32, arena + 16 * KB_)
        attT = sb("attT", [P, NG, QH], F32, rest + 16 * KB_ + 512)
        bcb1 = sb("bcb1", [P, D], F32, rest + 20 * KB_ + 512)
        x2s = sb("x2s", [P, XS, D], F32, rest + 22 * KB_ + 512)

        def residual(f):
            return x2s[:, f, :] if f < XS else x2e[:, f - XS, :]

        psum = ctx.enter_context(nc.psum_tensor("psum", [P, 8, 512], F32))
        score2 = psum[:, 4:6, :].rearrange("p b n -> p (b n)")

        kscr = nc.dram_tensor("kscr", (2, NB, D, KEYS), F32).ap()
        qscr = nc.dram_tensor("qscr", (2, 2, D, NB * QH), F32).ap()
        vscr = nc.dram_tensor("vscr", (NB, CH + 1, P, D), F32).ap()

        def sem(name):
            return ctx.enter_context(nc.semaphore(name))

        const_loaded = sem("const_loaded")
        rows_loaded = sem("rows_loaded")
        ind_placed = [sem(f"ind_placed{i}") for i in range(2)]
        ind_ready = sem("ind_ready")
        x_loaded = [sem(f"x_loaded{i}") for i in range(2)]
        raw_loaded = [sem(f"raw_loaded{i}") for i in range(2)]
        hi_done = sem("hi_done")
        lo_done = sem("lo_done")
        x_mean = sem("x_mean")
        x_rstd = sem("x_rstd")
        xn_done = sem("xn_done")
        xhi_done = sem("xhi_done")
        job_done = sem("job_done")
        emptied_by = {'act': sem("emptied_by_act"), 'dve': sem("emptied_by_dve")}
        sumsq_added = sem("sumsq_added")
        rms_done = sem("rms_done")
        norm_done = sem("norm_done")
        hl_stored = [sem(f"hl_stored{i}") for i in range(2)]
        v_stored = [sem(f"v_stored{i}") for i in range(4)]
        pair_loaded = [sem(f"pair_loaded{i}") for i in range(PAIRS)]
        v_loaded = [sem(f"v_loaded{i}") for i in range(2)]
        s1_done = sem("s1_done")
        max_done = sem("max_done")
        negm_done = sem("negm_done")
        shift_loaded = [sem(f"shift_loaded{i}") for i in range(2)]
        s2_done = sem("s2_done")
        exp2_done = sem("exp2_done")
        pv_done = sem("pv_done")
        pv_emptied = sem("pv_emptied")
        rsum_done = sem("rsum_done")
        added_done = sem("added_done")
        attn_mult = sem("attn_mult")
        attn_done = sem("attn_done")
        act_order = sem("act_order")
        dve_order = sem("dve_order")
        pool_order = sem("pool_order")
        qw_ready = sem("qw_ready")
        ones_ready = sem("ones_ready")
        res_loaded, res2_loaded = sem("res_loaded"), sem("res2_loaded")
        res_ready = sem("res_ready")
        late_loaded = {n: sem("loaded_" + n) for n in ('wg', 'd1', 'd2')}
        wo_loaded, w_loaded = sem("wo_loaded"), sem("w_loaded")
        chx_zero = sem("chx_zero")
        row_loaded = sem("row_loaded")
        ch_stats = sem("ch_stats")
        ch_rstd = sem("ch_rstd")
        ch_norm = sem("ch_norm")
        gelu_in = sem("gelu_in")
        gelu_done = sem("gelu_done")
        tb_ready = sem("tb_ready")
        f_stats = sem("f_stats")
        f_rstd = sem("f_rstd")
        x2_stats = sem("x2_stats")
        x2_rstd = sem("x2_rstd")
        x2_terms = sem("x2_terms")
        x2n_done = sem("x2n_done")
        z_ready = sem("z_ready")
        z_exp = sem("z_exp")
        gate_done = sem("gate_done")
        mix_done = sem("mix_done")
        x2b_ready = sem("x2b_ready")
        out_ready = sem("out_ready")
        out_stored = sem("out_stored")

        pieces_before = [sum(len(pieces(t)) for t in range(n)) * KC for n in range(7)]

        def stores_of(tiles):
            return 16 * (4 * tiles // 2)

        def v_stores(slot, chunks):
            return 16 * ((chunks - slot + 3) // 4)

        n_const, n_rows = 3, 1 + 3 + 4 + 2
        i_split = {n: i for i, n in enumerate(SPLITS)}
        tok_of = {('k', 0, 0): 'c00', ('k', 0, 1): 'c01', ('k', 1, 0): 'c10', ('k', 1, 1): 'c11'}

        def last_job(test):
            return max(n for n, e in enumerate(jobs) if test(e))

        split_after = {
            'c00': last_job(lambda e: e[0] == 'proj' and e[1] == 0),
            'c01': last_job(lambda e: e[0] == 'proj' and e[1] == 1),
            'wvi': last_job(lambda e: e[0] == 'proj' and e[1] == 1),
            'c10': last_job(lambda e: e[0] in ('v', 'vimg') and e[1] == 0 and (e[0] == 'vimg' or e[2] < 4)),
            'c11': last_job(lambda e: e[0] == 'v' and e[1] == 0),
        }
        last_k = last_job(lambda e: e[0] == 'proj')

        block = ctx.enter_context(nc.Block())

        @block.sync
        def _(sp):
            x_t = T['x'].rearrange("b (q p) d -> p b q d", p=P)

            def load_raw(i):
                name = SPLITS[i]
                if name[0] == 'w':
                    src = T[name].rearrange("(k p) n -> p k n", p=P)
                else:
                    c0 = int(name[1]) * KEYS + int(name[2]) * 512
                    src = T['ctxT'].rearrange("(k p) n -> p k n", p=P)[:, :, c0:c0 + 512]
                sp.dma_start(raw[:, i % 2], src).then_inc(raw_loaded[i % 2], 16)

            def load_x(h):
                for b in range(NB):
                    sp.dma_start(xin[:, 4 * h + 2 * b:4 * h + 2 * b + 2, :], x_t[:, b, 2 * h:2 * h + 2, :]).then_inc(x_loaded[h], 16)

            load_x(1)
            load_raw(0)
            load_x(0)
            load_raw(1)

            def split(i):
                if i + 2 < len(SPLITS):
                    sp.wait_ge(lo_done, i + 1)
                    load_raw(i + 2)

            def norm(tile, oc):
                kind = TILES[tile]
                n = KC * tile + oc
                if kind[0] == 'q':
                    dst = qscr[:, kind[1], oc * P:(oc + 1) * P, :]
                else:
                    dst = kscr[:, kind[1], oc * P:(oc + 1) * P, 512 * kind[2]:512 * kind[2] + 512]
                sp.wait_ge(norm_done, n + 1)
                sp.dma_start(dst.rearrange("s p n -> p s n"), hl[:, n % 2].bitcast(F32)).then_inc(hl_stored[n % 2], 16)

            def vstore(b, c):
                i = (CH + 1) * b + c
                n = job_at[('vimg', b)] if c == IMG_CHUNK else job_at[('v', b, c - (c > IMG_CHUNK))]
                sp.wait_ge(emptied_by['act'], emptied(n)[1])
                sp.dma_start(vscr[b, c], vbuf[:, i % 4, :]).then_inc(v_stored[i % 4], 16)

            def load(u):
                h, b, g = unit(u)
                if u == 0:
                    for s in range(2):
                        sp.wait_ge(hl_stored[s], stores_of(4))
                    sp.wait_ge(ind_ready, 1)
                    sp.wait_ge(xn_done, 8)
                    sp.wait_ge(job_done, job_at[('xT', 0, 3)] + 1)
                    sp.wait_ge(lo_done, len(SPLITS))
                if u == 2:
                    for s in range(2):
                        sp.wait_ge(hl_stored[s], stores_of(6))
                for pp in range(2):
                    n = 2 * u + pp
                    slot = n % PAIRS
                    if n >= PAIRS:
                        sp.wait_ge(s2_done, 16 * ((n - PAIRS) // 2 + 1))
                    else:
                        for jj in range(2):
                            sp.dma_start(kst[96:100, slot, jj, :].bitcast(F32), ind[:, :].bitcast(F32)).then_inc(ind_placed[u // 2], 16)
                    r0 = P * g + 64 * pp
                    for part, row in ((0, 0), (0, 32), (1, 64)):
                        src = kscr[part, b, r0:r0 + 64, :].rearrange("(j d) n -> d j n", d=HD)
                        sp.dma_start(kst[row:row + 32, slot].bitcast(F32), src).then_inc(pair_loaded[slot], 16)
                    for part, row in ((0, 0), (1, 32), (0, 64)):
                        src = qscr[part, h, r0:r0 + 64, b * QH:(b + 1) * QH].rearrange("(j d) n -> d j n", d=HD)
                        sp.dma_start(qst[row:row + 32, slot].bitcast(F32), src).then_inc(pair_loaded[slot], 16)

            def phase2():
                sp.wait_ge(job_done, last_v + 1)
                for s in range(2):
                    sp.wait_ge(hl_stored[s], stores_of(6))
                for s in range(4):
                    sp.wait_ge(v_stored[s], v_stores(s, 2 * (CH + 1)))
                sp.wait_ge(ind_placed[0], 16 * 8)
                sp.wait_ge(ind_placed[1], 16 * 4)
                for f in range(XS):
                    h, b, _ = unit(NG * (f // 2))
                    sp.dma_start(residual(f), T['x'][b, (2 * h + f % 2) * P:(2 * h + f % 2 + 1) * P, :]).then_inc(res_loaded, 16)
                sp.dma_start(wbuf[:], T['wo'].rearrange("(k p) n -> p k n", p=P)).then_inc(wo_loaded, 16)

            def load_v(u):
                h, b, g = unit(u)
                if u == 0:
                    for s in range(4):
                        sp.wait_ge(v_stored[s], v_stores(s, CH + 1))
                    sp.wait_ge(job_done, last_k + 1)
                if u == NG:
                    for s in range(4):
                        sp.wait_ge(v_stored[s], v_stores(s, 2 * (CH + 1)))
                if u >= 2:
                    sp.wait_ge(pv_done, 8 * (u - 1))
                sp.dma_start(vring[:, u % 2], vscr[b, :, :, P * g:P * (g + 1)].rearrange("c p n -> p c n")).then_inc(v_loaded[u % 2], 16)

            def shift(u):
                sp.wait_ge(emptied_by['dve'], emptied(job_at[('shift', u)])[1])
                slot = pair_slot(u, 0)[0]
                for part in range(2):
                    row = 96 + 2 * part
                    sp.dma_start(qst[row:row + 2, slot:slot + 2].rearrange("s a b n -> s (a b) n").bitcast(F32),
                                 crow[:, part, :].bitcast(F32)).then_inc(shift_loaded[u % 2], 16)

            def ch_row():
                sp.wait_ge(emptied_by['dve'], emptied(job_at[('o', 1, 1)])[1])
                sp.wait_ge(chx_zero, 1)
                for b in range(NB):
                    sp.dma_start(chx[b:b + 1, :], x2s[P - 1:P, 2 * b + 1, :]).then_inc(row_loaded, 16)

            def f_out(f):
                h, b, _ = unit(NG * (f // 2))
                sp.wait_ge(out_ready, f + 1)
                sp.dma_start(out.rearrange("b (q p) d -> b q p d", p=P)[b, 2 * h + f % 2], residual(f))\
                  .then_inc(out_stored, 16)

            steps = {'split': split, 'norm': norm, 'vstore': vstore, 'load': load, 'load_v': load_v, 'phase2': phase2, 'shift': shift,
                     'ch_row': ch_row, 'f_out': f_out}
            for e in plan:
                if e[0] in steps:
                    steps[e[0]](*e[1:])
            sp.wait_ge(out_stored, 16 * 8)

        @block.tensor
        def _(pe):
            def open_bank(n):
                m = before_in_bank(bank_of[n], n)
                if n >= n_late and bank_of[n] != SHARED_BANK and m <= last_v:
                    pe.wait_ge(max_done, 16 * NU)
                elif m is not None:
                    eng, count = emptied(m)
                    pe.wait_ge(emptied_by[eng], count)
                return psum[:, bank_of[n], :]

            def xT(h, n):
                job = job_at[('xT', h, n)]
                ps = open_bank(job)
                if job == 0:
                    pe.wait_ge(const_loaded, 16 * n_const)
                pe.wait_ge(xn_done, 4 * (1 - h) + n + 1)
                for kc in range(KC):
                    mm = pe.transpose(ps[:, kc * P:(kc + 1) * P], xin[:, 4 * h + n, kc * P:(kc + 1) * P], ident[:, :])
                mm.then_inc(job_done, 1)

            def three_passes(ps, left, right):
                for kc in range(KC):
                    for a, b in ((0, 0), (0, 1), (1, 0)):
                        mm = pe.matmul(ps, left(a, kc), right(b, kc), start=(kc == 0 and a + b == 0), stop=(kc == KC - 1 and a == 1))
                return mm

            def proj(tile, oc, piece):
                kind = TILES[tile]
                w, c0, c1 = pieces(tile)[piece][:3]
                job = job_at[('proj', tile, oc, piece)]
                ps = open_bank(job)
                if oc == 0 and piece == 0:
                    if kind[0] == 'q':
                        pe.wait_ge(emptied_by['dve'], emptied(job_at[('xT', kind[1], 3)])[1])
                        pe.wait_ge(lo_done, i_split['wq'] + 1)
                    else:
                        pe.wait_ge(lo_done, max(i_split[tok_of[kind]], i_split['wk']) + 1)
                x = token_parts[1 - kind[1] if kind[0] == 'q' else kind[2]]
                wt = w_parts[w]
                three_passes(ps[:, 0:c1 - c0], lambda a, kc: wt[:, a, kc, oc * P:(oc + 1) * P],
                             lambda a, kc: x[:, a, kc, c0:c1]).then_inc(job_done, 1)

            def sumsq(tile):
                ps = open_bank(job_at[('sumsq', tile)])
                if tile == 0:
                    pe.wait_ge(ones_ready, 1)
                pe.wait_ge(sumsq_added, tile + 1)
                pe.matmul(ps, inv_d[:, :].to_broadcast([P, P]), ssum[:, :], start=True, stop=True).then_inc(job_done, 1)

            def v_job(job, b, c, w):
                ps = open_bank(job)
                pe.wait_ge(lo_done, i_split[w] + 1)
                pe.wait_ge(lo_done, i_split[f"c{b}{c // 4}"] + 1)
                x = token_parts[c // 4]
                wt = w_parts[w]
                t0 = (c % 4) * P
                three_passes(ps, lambda a, kc: x[:, a, kc, t0:t0 + P], lambda a, kc: wt[:, a, kc, :]).then_inc(job_done, 1)

            def v(b, c):
                v_job(job_at[('v', b, c)], b, c, 'wvi' if c < IMG_CHUNK else 'wv')

            def vimg(b):
                v_job(job_at[('vimg', b)], b, IMG_CHUNK, 'wvi')

            def bank_before_attention(bank):
                eng, count = emptied(before_in_bank(bank, last_v + 1))
                pe.wait_ge(emptied_by[eng], count)

            def S1(t):
                u, s = t // 8, t % 8
                j, qt = s // 2, s % 2
                slot, jj, rnd = pair_slot(u, j)
                if s % 4 == 0:
                    pe.wait_ge(pair_loaded[slot], 96 * (rnd + 1))
                for half in range(2):
                    n = 2 * t + half
                    if n < 3:
                        bank_before_attention(n)
                    else:
                        pe.wait_ge(max_done, n - 2)
                    pe.matmul(psum[:, n % 3, :], qst[0:96, slot, jj, qt * P:(qt + 1) * P],
                              kst[0:96, slot, jj, half * 512:(half + 1) * 512], start=True, stop=True).then_inc(s1_done, 1)

            def S2(r):
                u, c = r // 8, r % 8
                if r == 0:
                    pe.wait_ge(ind_placed[0], 16 * 8)
                    bank_before_attention(4)
                    bank_before_attention(5)
                if r == 16:
                    pe.wait_ge(ind_placed[1], 16 * 4)
                if c == 0:
                    pe.wait_ge(shift_loaded[u % 2], 16 * 2 * (u // 2 + 1))
                k0 = ORDER[c] * P
                for j in range(HPG):
                    slot, jj, _ = pair_slot(u, j)
                    if r > 0 and j % 2 == 0:
                        pe.wait_ge(exp2_done, 2 * r - 1 + j // 2)
                    mm = pe.matmul(score2[:, j * QH:(j + 1) * QH], kst[0:100, slot, jj, k0:k0 + P],
                                   qst[0:100, slot, jj, :], start=True, stop=True)
                    if j % 2 == 1:
                        mm.then_inc(s2_done, 1)

            def PV(r):
                u, c = r // 8, r % 8
                if c == 0:
                    pe.wait_ge(v_loaded[u % 2], 16 * (u // 2 + 1))
                    if u == 0:
                        bank_before_attention(PV_BANK)
                        bank_before_attention(SUM_BANK)
                    else:
                        pe.wait_ge(pv_emptied, 2 * u)
                pe.wait_ge(exp2_done, 2 * (r + 1))
                k = ORDER[c]
                for vc, st in ((k + 1, 1),) if k > IMG_CHUNK else ((3, 1), (2, 0)) if k == IMG_CHUNK else ((k, 0),):
                    for j in range(HPG):
                        mm = pe.matmul(psum[32 * j:32 * j + 32, PV_BANK, st * QH:(st + 1) * QH], vring[:, u % 2, vc, 32 * j:32 * j + 32],
                                       prob[:, r % NP, j * QH:(j + 1) * QH], start=(vc in (ORDER[0] + 1, 2)), stop=(vc in (3, ORDER[-1])))

                def add_sum(kind, source, st, first, last):
                    for j in range(HPG):
                        mm = pe.matmul(psum[32 * j:32 * j + 32, SUM_BANK, st * QH:(st + 1) * QH], ones[:, kind, :],
                                       source[:, j * QH:(j + 1) * QH], start=first, stop=last)
                    return mm

                if c == N_ADDED:
                    mm = add_sum(2, prob[:, r % NP, :], 1, True, False)
                elif c == N_ADDED + 1:
                    pe.wait_ge(added_done, (N_ADDED - 1) * (u + 1))
                    add_sum(0, added, 1, False, True)
                    add_sum(1, prob[:, (r - 1) % NP, :], 0, True, False)
                    mm = add_sum(0, prob[:, r % NP, :], 0, False, False)
                elif c == N_ADDED + 2:
                    mm = add_sum(0, prob[:, r % NP, :], 0, False, True)
                mm.then_inc(pv_done, 1)

            def shift(u):
                ps = open_bank(job_at[('shift', u)])
                pe.wait_ge(negm_done, u + 1)
                for qt in range(2):
                    mm = pe.transpose(ps[0:8, qt * P:(qt + 1) * P], negm[:, u % 2, qt * 8:qt * 8 + 8], ident[:, :])
                mm.then_inc(job_done, 1)

            def o(k, n):
                ps = open_bank(job_at[('o', k, n)])
                pe.wait_ge(attn_done, NG * (k + 1))
                if k == 0:
                    pe.wait_ge(wo_loaded, 16)
                elif n == 0 and k >= 2:
                    pe.wait_ge(w_loaded, 16 * (2 * k - 2))
                for g in range(NG):
                    mm = pe.matmul(ps, attT[:, g, n * P:(n + 1) * P], wbuf[:, g, :], start=(g == 0), stop=(g == NG - 1))
                mm.then_inc(job_done, 1)

            def ch_turn(i):
                ps = open_bank(job_at[('ch_turn', i)])
                src = chx
                if i == 1 + K_STEPS:
                    pe.wait_ge(emptied_by['dve'], emptied(job_at[('ch_sum', K_STEPS - 1)])[1])
                    src = th
                else:
                    pe.wait_ge(ch_norm, i + 2)
                for kc in range(KC):
                    mm = pe.transpose(ps[:, kc * 32:(kc + 1) * 32], src[:, kc * P:(kc + 1) * P], ident[0:32, 0:32])
                mm.then_inc(job_done, 1)

            def thin(ps, w):
                for kc in range(KC):
                    for j in range(4):
                        mm = pe.matmul(ps[32 * j:32 * j + 32, 0:P], tT[:, kc, :], w[:, kc, j * P:(j + 1) * P],
                                       start=(kc == 0), stop=(kc == KC - 1))
                mm.then_inc(job_done, 1)

            def ch_agg():
                ps = open_bank(job_at[('ch_agg',)])
                pe.wait_ge(w_loaded, 16)
                thin(ps, wbuf)

            def ch_d1(k, kc):
                ps = psum[:, SHARED_BANK, :]
                if kc == 0:
                    open_bank(job_at[('ch_d1', k, KC - 1)])
                    if k == 0:
                        pe.wait_ge(late_loaded['d1'], 64)
                for j in range(4):
                    mm = pe.matmul(ps[32 * j:32 * j + 32, :], tT[:, kc, :], d1[:, kc, 512 * j:512 * (j + 1)],
                                   start=(kc == 0), stop=(kc == KC - 1))
                if kc == KC - 1:
                    mm.then_inc(job_done, 1)

            def ch_hT(k):
                ps = open_bank(job_at[('ch_hT', k)])
                pe.wait_ge(gelu_done, k + 1)
                for m in range(4):
                    mm = pe.transpose(ps[:, m * P:(m + 1) * P], hb[:, m * P:(m + 1) * P], ident[:, :])
                mm.then_inc(job_done, 1)

            def ch_d2(k, j):
                ps = psum[:, SHARED_BANK, :]
                if j == 0:
                    open_bank(job_at[('ch_d2', k, KC - 1)])
                    if k == 0:
                        pe.wait_ge(late_loaded['d2'], 64)
                for m in range(4):
                    mm = pe.matmul(ps[32 * m:32 * m + 32, :], hT[:, m, 32 * j:32 * j + 32], d2[:, 4 * j + m, :],
                                   start=(j == 0), stop=(j == 3))
                if j == KC - 1:
                    mm.then_inc(job_done, 1)

            def ch_sum(k):
                ps = open_bank(job_at[('ch_sum', k)])
                pe.wait_ge(rows_loaded, 16 * n_rows)
                pe.matmul(ps[0:32, :], sel[:, :], hb[:, :], start=True, stop=True).then_inc(job_done, 1)

            def ch_bc():
                ps = open_bank(job_at[('ch_bc',)])
                pe.wait_ge(w_loaded, 16 * 3)
                thin(ps, wbuf)

            def ch_spread(b):
                ps = open_bank(job_at[('ch_spread', b)])
                pe.wait_ge(emptied_by['dve'], emptied(job_at[('ch_bc',)])[1])
                pe.matmul(ps, ident[0:32, b:b + 1].to_broadcast([32, P]), chx[:, :], start=True, stop=True).then_inc(job_done, 1)

            def f_turn(f):
                ps = open_bank(job_at[('f_turn', f)])
                pe.wait_ge(x2n_done, f + 1)
                for kc in range(KC):
                    mm = pe.transpose(ps[:, kc * P:(kc + 1) * P], x2n[:, f % NX, kc * P:(kc + 1) * P], ident[:, :])
                mm.then_inc(job_done, 1)

            def f_gate(f, half):
                ps = psum[:, bank_of[job_at[('f_gate', f, 1)]], :]
                if half == 0:
                    open_bank(job_at[('f_gate', f, 1)])
                    pe.wait_ge(emptied_by['act'], emptied(job_at[('f_turn', f)])[1])
                    if f == 0:
                        pe.wait_ge(late_loaded['wg'], 16)
                for kc in (2 * half, 2 * half + 1):
                    mm = pe.matmul(ps, xTt[:, f % 2, kc, :], wg[:, kc, :], start=(kc == 0), stop=(kc == KC - 1))
                if half == 1:
                    mm.then_inc(job_done, 1)

            steps = {'xT': xT, 'proj': proj, 'sumsq': sumsq, 'v': v, 'vimg': vimg, 'S1': S1, 'S2': S2, 'PV': PV,
                     'shift': shift, 'o': o, 'ch_turn': ch_turn, 'ch_agg': ch_agg, 'ch_d1': ch_d1, 'ch_hT': ch_hT,
                     'ch_d2': ch_d2, 'ch_sum': ch_sum, 'ch_bc': ch_bc, 'ch_spread': ch_spread, 'f_turn': f_turn,
                     'f_gate': f_gate}
            for e in plan:
                if e[0] in steps:
                    steps[e[0]](*e[1:])

        @block.scalar
        def _(act):
            for dst, src in ((ident[:, :], T['ident']), (colp[:], T['cols']), (ind_in[:, :], T['ind'])):
                act.dma_start(dst, src).then_inc(const_loaded, 16)

            def consts():
                act.wait_ge(const_loaded, 16 * n_const)
                act.dma_start(sel[:, :], T['sel']).then_inc(rows_loaded, 16)
                for i, n in enumerate(('d2_b', 'agg_b', 'bc_b')):
                    act.dma_start(chrow[32 * i:32 * i + 32, :], T[n].partition_broadcast(32)).then_inc(rows_loaded, 16)
                for j in range(4):
                    act.dma_start(d1b[32 * j:32 * j + 32, :], T['d1_b'][512 * j:512 * (j + 1)].partition_broadcast(32)).then_inc(rows_loaded, 16)
                act.dma_start(rows[:, 0:2, :], T['rows'][0:2].partition_broadcast(P)).then_inc(rows_loaded, 16)
                act.dma_start(rows[:, 2:4, :], T['rows'][2:4].partition_broadcast(P)).then_inc(rows_loaded, 16)

            links = [0]

            def link(ins):
                links[0] += 1
                ins.then_inc(act_order, 1)
                act.wait_ge(act_order, links[0])

            def rstd(dst, var, eps):
                link(act.activation(dst, var, ACT.Ln, bias=eps))
                return act.activation(dst, dst, ACT.Exp, scale=-0.5)

            def split(i):
                name = SPLITS[i]
                act.wait_ge(raw_loaded[i % 2], 16 * (i // 2 + 1))
                if name in split_after:
                    act.wait_ge(job_done, split_after[name] + 1)
                dst = w_parts[name] if name[0] == 'w' else token_parts[int(name[2])]
                act.activation(dst[:, 0], raw[:, i % 2], ACT.Copy).then_inc(hi_done, 1)

            def xstat(h):
                act.wait_ge(x_mean, 2 - h)
                rstd(rs[:, 4 * h:4 * h + 4], mv[:, 4 * h:4 * h + 4, 1], epsln[:, 0:1]).then_inc(x_rstd, 1)

            def xT(h, n):
                job = job_at[('xT', h, n)]
                act.wait_ge(job_done, job + 1)
                src = psum[:, bank_of[job], :].rearrange("p (k n) -> p k n", k=KC)
                act.copy(token_parts[1 - h][:, 0, :, n * P:(n + 1) * P], src).then_inc(xhi_done, 1)

            def proj(tile, oc, piece):
                _, c0, _, k0, k1, bias, _ = pieces(tile)[piece]
                job = job_at[('proj', tile, oc, piece)]
                if oc == 0 and piece == 0:
                    if tile >= 1:
                        act.wait_ge(sumsq_added, tile)
                    if tile == 0:
                        act.wait_ge(ind_ready, 1)
                if tile >= 2 and piece == 0:
                    act.wait_ge(norm_done, KC * (tile - 2) + oc + 1)
                act.wait_ge(job_done, job + 1)
                src = psum[:, bank_of[job], k0 - c0:k1 - c0]
                b = colp[:, bias, oc:oc + 1]
                act.activation(raw4[:, tile % 2, oc, k0:k1], src, ACT.Identity, bias=b)
                act.activation(sq4[:, oc, k0:k1], src, ACT.Square, bias=b).then_inc(emptied_by['act'], 1)

            def sumsq(tile):
                job = job_at[('sumsq', tile)]
                if tile >= 2:
                    act.wait_ge(norm_done, KC * (tile - 1))
                act.wait_ge(job_done, job + 1)
                r = rt[:, tile % 2, :]
                n = emptied(job)[1]
                act.activation(r, psum[:, bank_of[job], :], ACT.Ln, bias=epsf[:, 0:1]).then_inc(emptied_by['act'], 1)
                act.wait_ge(emptied_by['act'], n)
                act.activation(r, r, ACT.Exp, scale=-0.5).then_inc(rms_done, 1)

            def fill_vbuf(i, job, scale):
                if i >= 4:
                    act.wait_ge(v_stored[i % 4], 16 * (i // 4))
                act.wait_ge(job_done, job + 1)
                act.activation(vbuf[:, i % 4, :], psum[:, bank_of[job], :], ACT.Copy, scale=scale).then_inc(emptied_by['act'], 1)

            def v(b, c):
                fill_vbuf((CH + 1) * b + c + (c >= IMG_CHUNK), job_at[('v', b, c)], mask[:, 1:2] if c == IMG_CHUNK else 1.0)

            def vimg(b):
                fill_vbuf((CH + 1) * b + IMG_CHUNK, job_at[('vimg', b)], mask[:, 0:1])

            def S2(r):
                if r >= NP:
                    u, c = (r - NP) // 8, (r - NP) % 8
                    act.wait_ge(pv_done, r - NP + 1 + (c == N_ADDED))
                    if c < N_ADDED:
                        act.wait_ge(added_done, (N_ADDED - 1) * u + max(c, 1))
                for n in range(2):
                    part = slice(512 * n, 512 * (n + 1))
                    act.wait_ge(s2_done, 2 * r + n + 1)
                    act.activation(prob[:, r % NP, part], score2[:, part], ACT.Exp).then_inc(exp2_done, 1)

            def attn(u):
                act.wait_ge(pv_done, 8 * (u + 1))
                if u >= 1:
                    act.wait_ge(attn_done, u)
                act.copy(pvc[:].rearrange("p s n -> p (s n)"), psum[:, PV_BANK, :]).then_inc(pv_emptied, 1)
                r = rsum[:].rearrange("p s n -> p (s n)")
                act.activation(r, psum[:, SUM_BANK, :], ACT.Ln).then_inc(pv_emptied, 1)
                act.wait_ge(pv_emptied, 2 * (u + 1))
                act.activation(r, r, ACT.Exp, scale=-1.0).then_inc(rsum_done, 1)

            def ch_rstd_of(i):
                act.wait_ge(ch_stats, i + 1)
                rstd(crs[0:32, :], cmv[0:32, 1:2], (epsln if i == 0 else epsf)[0:32, 0:1]).then_inc(ch_rstd, 1)

            def ch_gelu(k):
                act.wait_ge(gelu_in, k + 1)
                act.activation(hb[:, :], hb[:, :], ACT.Gelu).then_inc(gelu_done, 1)
                act.preload_act_table_set("natural_log_exp_and_others")

            def f_terms(i):
                tiles = slice(0, XS) if i == 0 else slice(XS, 8)
                act.wait_ge(x2_stats, tiles.stop)
                rstd(xterms[:, 0, tiles], mv[:, tiles, 1], epsln[:, 0:1]).then_inc(x2_rstd, 1)

            def f_norm(f):
                act.wait_ge(x2_terms, 1 + f // XS)
                if f >= NX:
                    act.wait_ge(mix_done, f - NX + 1)
                act.activation(x2n[:, f % NX, :], residual(f), ACT.Identity, bias=xterms[:, 1, f:f + 1], scale=xterms[:, 0, f:f + 1])\
                   .then_inc(x2n_done, 1)

            def f_turn(f):
                job = job_at[('f_turn', f)]
                act.wait_ge(job_done, job + 1)
                act.copy(xTt[:, f % 2].rearrange("p k n -> p (k n)"), psum[:, bank_of[job], :]).then_inc(emptied_by['act'], 1)

            def f_exp(f):
                z = zt[:, f % NX, :]
                act.wait_ge(z_ready, f + 1)
                act.activation(z, z, ACT.Exp, scale=-1.0).then_inc(z_exp, 1)

            def f_sig(f):
                z = zt[:, f % NX, :]
                act.wait_ge(z_exp, f + 1)
                link(act.activation(z, z, ACT.Ln, bias=1.0))
                act.activation(z, z, ACT.Exp, scale=-1.0).then_inc(gate_done, 1)

            def f_stat2(f):
                act.wait_ge(f_stats, f + 1)
                rstd(frs[:, f % 2:f % 2 + 1], fmv[:, f % 2, 1:2], epsf[:, 0:1]).then_inc(f_rstd, 1)

            act.preload_act_table_set("natural_log_exp_and_others")
            act.wait_ge(ones_ready, 1)
            steps = {'consts': consts, 'split': split, 'xstat': xstat, 'xT': xT, 'proj': proj, 'sumsq': sumsq, 'v': v, 'vimg': vimg, 'attn': attn,
                     'S2': S2, 'ch_rstd': ch_rstd_of, 'ch_gelu': ch_gelu, 'f_terms': f_terms, 'f_norm': f_norm, 'f_turn': f_turn,
                     'f_exp': f_exp, 'f_sig': f_sig, 'f_stat2': f_stat2}
            for e in plan:
                if e[0] in steps:
                    steps[e[0]](*e[1:])

        @block.vector
        def _(dve):
            links = [0]

            def link(ins):
                links[0] += 1
                ins.then_inc(dve_order, 1)
                dve.wait_ge(dve_order, links[0])

            dve.memset(epsln[:, :], EPS_LN)
            dve.memset(mask[:, 0:1], 0.0)
            dve.memset(mask[:, 1:2], 1.0)
            dve.memset(ones[:, 0, :], 1.0)
            dve.memset(ones[:, 1, :], 0.0)
            link(dve.memset(ones[:, 2, :], 1.0))
            dve.memset(mask[0:1, 0:1], 1.0)
            dve.memset(mask[0:1, 1:2], 0.0)
            dve.memset(ones[0:1, 1, :], 1.0)
            link(dve.memset(ones[0:1, 2, :], 0.0))
            dve.memset(epsf[:, :], EPS)
            dve.memset(inv_d[:, :], 1.0 / D).then_inc(ones_ready, 1)

            def consts():
                dve.wait_ge(const_loaded, 16 * n_const)
                dve.tensor_copy(ind[:, :], ind_in[:, :]).then_inc(ind_ready, 1)
                dve.tensor_scalar(qw[:, :], colp[:, NQ, :], SCALE, None, ALU.mult)
                dve.tensor_tensor(vbias[:, :], colp[:, VB, :], colp[:, VIB, :], ALU.add).then_inc(qw_ready, 1)

            def stats(src, st, mean_var):
                link(dve.bn_stats(st, src))
                return dve.bn_aggr(mean_var, st)

            def split(i):
                name = SPLITS[i]
                dst = w_parts[name] if name[0] == 'w' else token_parts[int(name[2])]
                dve.wait_ge(hi_done, i + 1)
                dve.tensor_tensor(dst[:, 1], raw[:, i % 2], dst[:, 0], ALU.subtract).then_inc(lo_done, 1)

            def xstat(h):
                dve.wait_ge(x_loaded[h], 32)
                for n in range(4):
                    dve.bn_stats(bst[:, 4 * h + n, :], xin[:, 4 * h + n, :]).then_inc(dve_order, 1)
                links[0] += 4
                dve.wait_ge(dve_order, links[0])
                for n in range(4):
                    ins = dve.bn_aggr(mv[:, 4 * h + n, :], bst[:, 4 * h + n, :])
                ins.then_inc(x_mean, 1)

            def xnorm(h):
                dve.wait_ge(x_mean, 2 - h)
                dve.wait_ge(x_rstd, 2 - h)
                for n in range(4):
                    i = 4 * h + n
                    dve.tensor_scalar(xin[:, i, :], xin[:, i, :], mv[:, i, 0:1], rs[:, i:i + 1], ALU.subtract, ALU.mult)\
                       .then_inc(xn_done, 1)

            def xT(h, n):
                job = job_at[('xT', h, n)]
                dve.wait_ge(xhi_done, 4 * (1 - h) + n + 1)
                src = psum[:, bank_of[job], :].rearrange("p (k n) -> p k n", k=KC)
                dst = token_parts[1 - h]
                cols = slice(n * P, (n + 1) * P)
                dve.tensor_tensor(dst[:, 1, :, cols], src, dst[:, 0, :, cols], ALU.subtract).then_inc(emptied_by['dve'], 1)

            def norm(tile, oc):
                dve.wait_ge(rms_done, tile + 1)
                n = KC * tile + oc
                x = raw4[:, tile % 2, oc, :]
                for _, _, _, k0, k1, _, w in pieces(tile):
                    wcol = qw[:, oc:oc + 1] if w is None else colp[:, w, oc:oc + 1]
                    ins = dve.scalar_tensor_tensor(x[:, k0:k1], x[:, k0:k1], wcol, rt[:, tile % 2, k0:k1], ALU.mult, ALU.mult)
                link(ins)
                if n >= 2:
                    dve.wait_ge(hl_stored[n % 2], 16 * (n // 2))
                link(dve.tensor_copy(hl[:, n % 2, 0, :], x))
                dve.tensor_tensor(hl[:, n % 2, 1, :], x, hl[:, n % 2, 0, :], ALU.subtract).then_inc(norm_done, 1)

            def S1(t):
                u, s = t // 8, t % 8
                j, qt = s // 2, s % 2
                if t == 0:
                    dve.wait_ge(rows_loaded, 16 * n_rows)
                neg = negm[:, u % 2, qt * 8 + j:qt * 8 + j + 1]
                for half in range(2):
                    n = 2 * t + half
                    dve.wait_ge(s1_done, n + 1)
                    if half == 0:
                        dve.tensor_reduce(neg, psum[:, n % 3, 0:IMG], AX.X, ALU.max, negate=True)
                    k0 = IMG if half == 0 else 0
                    dve.tensor_reduce(negt[:, u % 2, qt, half, j:j + 1], psum[:, n % 3, k0:512], AX.X, ALU.max, negate=True)\
                       .then_inc(max_done, 1)

            def maxes(u):
                dve.wait_ge(max_done, 16 * (u + 1))
                both = negt[:, u % 2]
                dve.tensor_tensor(negm[:, u % 2, :].rearrange("p (q s j) -> p q s j", q=2, s=2)[:, :, 1, :], both[:, :, 0, :], both[:, :, 1, :],
                                  ALU.min).then_inc(negm_done, 1)

            def weigh(u):
                g = u % NG
                dve.wait_ge(rsum_done, u + 1)
                if u >= NG and g == 0:
                    dve.wait_ge(job_done, job_at[('o', u // NG - 1, 1)] + 1)
                dve.tensor_tensor(pvc[:], pvc[:], rsum[:], ALU.mult).then_inc(attn_mult, 1)
                dve.wait_ge(attn_mult, u + 1)
                dve.scalar_tensor_tensor(attT[:, g, :], pvc[:, 0, :], vbias[:, g:g + 1], pvc[:, 1, :], ALU.add, ALU.add)\
                   .then_inc(attn_done, 1)

            def shift(u):
                job = job_at[('shift', u)]
                if u >= 1:
                    dve.wait_ge(shift_loaded[(u - 1) % 2], 16 * 2 * ((u + 1) // 2))
                dve.wait_ge(job_done, job + 1)
                src = psum[0:8, bank_of[job], 0:QH]
                link(dve.tensor_copy(crow[:, 0, :], src))
                dve.tensor_tensor(crow[:, 1, :], src, crow[:, 0, :], ALU.subtract).then_inc(emptied_by['dve'], 1)

            def o(k, n):
                job = job_at[('o', k, n)]
                f = 2 * k + n
                dve.wait_ge(res_ready, f + 1)
                dve.wait_ge(job_done, job + 1)
                dve.tensor_tensor(residual(f), psum[:, bank_of[job], :], residual(f), ALU.add).then_inc(emptied_by['dve'], 1)
                dve.wait_ge(emptied_by['dve'], emptied(job)[1])
                stats(residual(f), fst[:, f % 2, :], mv[:, f, :]).then_inc(x2_stats, 1)

            def ch_stat(i):
                src = chx if i < 2 else th
                if i == 0:
                    dve.wait_ge(row_loaded, 32)
                elif i == 1:
                    dve.wait_ge(ch_norm, 1)
                else:
                    job = job_at[('ch_agg',)] if i == 2 else job_at[('ch_sum', i - 3)]
                    dve.wait_ge(emptied_by['dve'], emptied(job)[1])
                stats(src[:, :], cst[0:32, :], cmv[0:32, :]).then_inc(ch_stats, 1)

            def ch_ln(i):
                src = chx if i < 2 else th
                dve.wait_ge(ch_stats, i + 1)
                dve.wait_ge(ch_rstd, i + 1)
                dve.tensor_scalar(chx[:, :], src[:, :], cmv[0:32, 0:1], crs[0:32, 0:1], ALU.subtract, ALU.mult).then_inc(ch_norm, 1)

            def ch_turn(i):
                job = job_at[('ch_turn', i)]
                dve.wait_ge(job_done, job + 1)
                for kc in range(KC):
                    src = psum[:, bank_of[job], kc * 32:(kc + 1) * 32]
                    if i == 1 + K_STEPS:
                        ins = dve.tensor_copy(tT[:, kc, :], src)
                    else:
                        ga, be = (ING, INB) if i == 0 else (PNG, PNB)
                        ins = dve.tensor_scalar(tT[:, kc, :], src, colp[:, ga, kc:kc + 1], colp[:, be, kc:kc + 1], ALU.mult, ALU.add)
                ins.then_inc(emptied_by['dve'], 1)

            def gather(dst, bank, row):
                for j in range(4):
                    cols = slice(j * P, (j + 1) * P)
                    ins = dve.tensor_tensor(dst[:, cols], psum[32 * j:32 * j + 32, bank, 0:P], chrow[row:row + 32, cols], ALU.add)
                ins.then_inc(emptied_by['dve'], 1)

            def ch_agg():
                job = job_at[('ch_agg',)]
                dve.wait_ge(job_done, job + 1)
                gather(th, bank_of[job], 32)

            def ch_d1(k, kc):
                if kc < KC - 1:
                    return
                job = job_at[('ch_d1', k, KC - 1)]
                dve.wait_ge(job_done, job + 1)
                dve.tensor_tensor(hb[:, :], psum[:, bank_of[job], :], d1b[:, :], ALU.add).then_inc(gelu_in, 1)
                dve.wait_ge(gelu_in, k + 1)
                dve.engine_nop().then_inc(emptied_by['dve'], 1)

            def ch_hT(k):
                job = job_at[('ch_hT', k)]
                dve.wait_ge(job_done, job + 1)
                dve.tensor_copy(hT[:].rearrange("p k n -> p (k n)"), psum[:, bank_of[job], :]).then_inc(emptied_by['dve'], 1)

            def ch_d2(k, j):
                if j < KC - 1:
                    return
                job = job_at[('ch_d2', k, KC - 1)]
                dve.wait_ge(job_done, job + 1)
                dve.tensor_copy(hb[:, :], psum[:, bank_of[job], :]).then_inc(emptied_by['dve'], 1)

            def ch_sum(k):
                job = job_at[('ch_sum', k)]
                dve.wait_ge(tb_ready, k + 1)
                dve.wait_ge(job_done, job + 1)
                dve.tensor_tensor(th[:, :], psum[0:32, bank_of[job], :], th[:, :], ALU.add).then_inc(emptied_by['dve'], 1)

            def ch_bc():
                job = job_at[('ch_bc',)]
                dve.wait_ge(job_done, job + 1)
                gather(chx, bank_of[job], 64)

            def ch_spread(b):
                job = job_at[('ch_spread', b)]
                dve.wait_ge(job_done, job + 1)
                dve.tensor_copy((bcb0, bcb1)[b][:, :], psum[:, bank_of[job], :]).then_inc(emptied_by['dve'], 1)

            def f_terms(i):
                tiles = slice(0, XS) if i == 0 else slice(XS, 8)
                dve.wait_ge(x2_rstd, i + 1)
                dve.scalar_tensor_tensor(xterms[:, 1, tiles], mv[:, tiles, 0], -1.0, xterms[:, 0, tiles], ALU.mult, ALU.mult).then_inc(x2_terms, 1)

            def f_gate(f, half):
                if half == 0:
                    return
                job = job_at[('f_gate', f, 1)]
                if f >= NX:
                    dve.wait_ge(out_ready, f - NX + 1)
                dve.wait_ge(job_done, job + 1)
                z = zt[:, f % NX, :]
                dve.tensor_tensor(z, psum[:, bank_of[job], :], rows[:, R_GATE, :], ALU.add).then_inc(emptied_by['dve'], 1)
                dve.wait_ge(emptied_by['dve'], emptied(job)[1])
                dve.tensor_scalar(z, z, -41.0, None, ALU.max).then_inc(z_ready, 1)

            def f_stat2(f):
                dve.wait_ge(mix_done, f + 1)
                stats(zt[:, f % NX, :], fst[:, f % 2, :], fmv[:, f % 2, :]).then_inc(f_stats, 1)

            def f_out(f):
                z = zt[:, f % NX, :]
                dve.wait_ge(f_rstd, f + 1)
                dve.wait_ge(x2b_ready, f + 1)
                link(dve.tensor_scalar(z, z, fmv[:, f % 2, 0:1], frs[:, f % 2:f % 2 + 1], ALU.subtract, ALU.mult))
                link(dve.tensor_tensor(z, z, rows[:, R_OG, :], ALU.mult))
                dve.tensor_tensor(residual(f), z, residual(f), ALU.add).then_inc(out_ready, 1)

            steps = {'consts': consts, 'split': split, 'xstat': xstat, 'xnorm': xnorm, 'xT': xT, 'norm': norm,
                     'S1': S1, 'maxes': maxes, 'weigh': weigh,
                     'shift': shift, 'o': o, 'ch_stat': ch_stat, 'ch_ln': ch_ln, 'ch_turn': ch_turn, 'ch_agg': ch_agg,
                     'ch_d1': ch_d1, 'ch_hT': ch_hT, 'ch_d2': ch_d2, 'ch_sum': ch_sum, 'ch_bc': ch_bc,
                     'ch_spread': ch_spread, 'f_terms': f_terms, 'f_gate': f_gate,
                     'f_stat2': f_stat2, 'f_out': f_out}
            for e in plan:
                if e[0] in steps:
                    steps[e[0]](*e[1:])

        @block.gpsimd
        def _(pool):
            links = [0]

            def link(ins):
                links[0] += 1
                ins.then_inc(pool_order, 1)
                pool.wait_ge(pool_order, links[0])

            def sumsq(tile):
                pool.wait_ge(emptied_by['act'], emptied(job_at[('proj', tile, KC - 1, len(pieces(tile)) - 1)])[1])
                if tile >= 1:
                    pool.wait_ge(job_done, job_at[('sumsq', tile - 1)] + 1)
                link(pool.tensor_tensor(ssum[:, :], sq4[:, 0, :], sq4[:, 1, :], ALU.add))
                link(pool.tensor_tensor(ssum[:, :], ssum[:, :], sq4[:, 2, :], ALU.add))
                pool.tensor_tensor(ssum[:, :], ssum[:, :], sq4[:, 3, :], ALU.add).then_inc(sumsq_added, 1)

            def load_res(f):
                h, b, _ = unit(NG * (f // 2))
                pool.dma_start(residual(f), T['x'][b, (2 * h + f % 2) * P:(2 * h + f % 2 + 1) * P, :]).then_inc(res2_loaded, 16)

            def add_o_bias(f):
                pool.tensor_tensor(residual(f), residual(f), rows[:, R_O, :], ALU.add).then_inc(res_ready, 1)

            def ch_hT(k):
                if k == K_STEPS - 1:
                    pool.wait_ge(job_done, job_at[('ch_d1', k, KC - 1)] + 1)
                    for f in range(XS, 8):
                        load_res(f)

            def ch_sum(k):
                if k == K_STEPS - 1:
                    pool.wait_ge(job_done, job_at[('ch_d2', k, KC - 1)] + 1)
                    pool.dma_start(wg[:], T['wg'].rearrange("(k p) n -> p k n", p=P)).then_inc(late_loaded['wg'], 16)

            def res2():
                load_w(4)
                pool.wait_ge(res2_loaded, 16 * (8 - XS))
                for f in range(XS, 8):
                    add_o_bias(f)

            def load_w(i):
                name, reader = (None, ('agg', ('o', 1, 1)), ('wo', ('ch_agg',)), ('bc', ('o', 2, 1)), ('wo', ('ch_bc',)))[i]
                pool.wait_ge(job_done, job_at[reader] + 1)
                pool.dma_start(wbuf[:], T[name].rearrange("(k p) n -> p k n", p=P)).then_inc(w_loaded, 16)

            def o(k, n):
                if (k, n) == (1, 1):
                    load_w(1)
                elif (k, n) == (2, 1):
                    load_w(3)

            def PV(r):
                u, c = r // 8, r % 8
                if not 1 <= c < N_ADDED:
                    return
                pool.wait_ge(exp2_done, 2 * (r + 1))
                if c == 1:
                    if u >= 1:
                        pool.wait_ge(pv_done, 8 * u)
                    pool.tensor_tensor(added[:, :], prob[:, (r - 1) % NP, :], prob[:, r % NP, :], ALU.add).then_inc(added_done, 1)
                else:
                    pool.wait_ge(added_done, (N_ADDED - 1) * u + c - 1)
                    pool.tensor_tensor(added[:, :], added[:, :], prob[:, r % NP, :], ALU.add).then_inc(added_done, 1)

            def bias(f):
                if f == 0:
                    pool.wait_ge(res_loaded, 16 * XS)
                    pool.wait_ge(rows_loaded, 16 * n_rows)
                add_o_bias(f)

            def late(i):
                if i == 2:
                    pool.wait_ge(max_done, 24)
                    pool.memset(chx[:, :], 0.0).then_inc(chx_zero, 1)
                elif i < 7:
                    kc = i - 3
                    pool.dma_start(d1[:, kc, :], T['d1'][kc * P:(kc + 1) * P, :]).then_inc(late_loaded['d1'], 16)
                else:
                    c = 4 * (i - 7)
                    pool.dma_start(d2[:, c:c + 4, :], T['d2'][c * P:(c + 4) * P, :].rearrange("(k p) n -> p k n", p=P))\
                        .then_inc(late_loaded['d2'], 16)

            def ch_d1(k, kc):
                if kc > 0:
                    return
                pool.wait_ge(ch_norm, 3 + k)
                pool.tensor_tensor(th[:, :], th[:, :], chrow[0:32, :], ALU.add).then_inc(tb_ready, 1)

            def ch_ln(i):
                if i == 2:
                    load_w(2)

            def f_norm(f):
                pool.wait_ge(x2n_done, f + 1)
                pool.tensor_tensor(residual(f), residual(f), rows[:, R_OB, :], ALU.add).then_inc(x2b_ready, 1)

            def f_sig(f):
                h, b, _ = unit(NG * (f // 2))
                z = zt[:, f % NX, :]
                pool.wait_ge(gate_done, f + 1)
                if f < 2:
                    pool.wait_ge(emptied_by['dve'], emptied(job_at[('ch_spread', 1)])[1])
                link(pool.tensor_tensor(z, z, (bcb0, bcb1)[b][:, :], ALU.mult))
                pool.tensor_tensor(z, z, x2n[:, f % NX, :], ALU.add).then_inc(mix_done, 1)

            steps = {'sumsq': sumsq, 'PV': PV, 'late': late, 'bias': bias, 'o': o, 'ch_ln': ch_ln, 'ch_d1': ch_d1,
                     'ch_hT': ch_hT, 'ch_sum': ch_sum, 'res2': res2, 'f_norm': f_norm, 'f_sig': f_sig}
            for e in plan:
                if e[0] in steps:
                    steps[e[0]](*e[1:])


def kernel(**inputs):
    import concourse.bacc as bacc
    from concourse.bass_utils import run_bass_kernel_spmd

    get = lambda n: np.asarray(inputs[n])
    eye = np.eye(P, dtype=np.float32)
    ind = np.zeros((4, KEYS), np.float32)
    ind[0::2, :IMG] = 1
    ind[1::2, IMG:] = 1
    host = {
        'x': get('x'),
        'ctxT': get('ctx_2048').reshape(NB * KEYS, D).T,
        'wq': get('L0_xattn_q_w').T, 'wk': get('L0_xattn_k_w').T, 'wki': get('L0_xattn_k_img_w').T,
        'wv': get('L0_xattn_v_w').T, 'wvi': get('L0_xattn_v_img_w').T, 'wo': get('L0_xattn_o_w').T,
        'wg': get('L0_ffn_gate_w'), 'agg': get('L0_ffn_agg_w'), 'bc': get('L0_ffn_bc_w'),
        'd1': get('L0_ffn_d1_w'), 'd2': get('L0_ffn_d2_w'),
        'cols': np.stack([get(n).reshape(KC, P).T for n in COLS], axis=1),
        'rows': np.stack([get(n) for n in ROWS]),
        'agg_b': get('L0_ffn_agg_b'), 'd2_b': get('L0_ffn_d2_b'), 'bc_b': get('L0_ffn_bc_b'),
        'd1_b': get('L0_ffn_d1_b'),
        'ident': eye, 'ind': ind, 'sel': np.tile(eye[:32, :32], (4, 1)),
    }
    nc = bacc.Bacc("TRN2", target_bir_lowering=False, num_devices=1)
    arrays = {n: np.ascontiguousarray(a) for n, a in host.items()}
    T = {n: nc.dram_tensor(n, a.shape, F32, kind="ExternalInput").ap() for n, a in arrays.items()}
    out = nc.dram_tensor("out", (NB, TOK, D), F32, kind="ExternalOutput").ap()
    build(nc, T, out)
    r = run_bass_kernel_spmd(nc, [arrays], core_ids=[0])
    return r.results[0]["out"]
```
